# Optimizing a Trainium2 kernel written in Bass

```python
import numpy as np
import jax
import jax.numpy as jnp

def _softmax(x, axis=-1):
    return jax.nn.softmax(x, axis=axis)

def _gelu(x):
    return jax.nn.gelu(x, approximate=True)

def _silu(x):
    return jax.nn.silu(x)

def _sigmoid(x):
    return jax.nn.sigmoid(x)

def _layernorm(x, axis=-1, eps=1e-05):
    m = jnp.mean(x, axis=axis, keepdims=True)
    v = jnp.var(x, axis=axis, keepdims=True)
    return (x - m) / jnp.sqrt(v + eps)

def _scatter_add(tgt, idx, src, axis=0):
    return tgt.at[idx].add(src)

def _segment_sum(src, seg, n):
    return jax.ops.segment_sum(src, seg, n)
kernel_name = 'mk_vit_tower_postln_d2_tok_img256_r4_4f9c47'

def setup_inputs(seed: int=0):
    np.random.seed(seed)
    _w = jnp.asarray

    def _rec_inputs():
        import jax
        import jax.numpy as jnp
        _rk = jax.random.key(seed)
        x = -0.000798584 + 1.00089 * jax.random.normal(jax.random.fold_in(_rk, 1), (64, 64, 75, 3), jnp.float32)
        return x
    x = _rec_inputs()

    def _L0_tok_setup():
        import jax, jax.numpy as jnp
        import numpy as np
        EPS = 1e-05
        B, T, V = (32, 64, 75)
        DIMS = [3, 128, 128, 64]

        def _layer(x, A, W, b, g, be, m, v, relu):
            x = jnp.einsum('btvc,co->btvo', x, W)
            x = jnp.einsum('uv,btvo->btuo', A, x)
            x = x + b
            x = (x - m) * (g * jax.lax.rsqrt(v + EPS)) + be
            if relu:
                x = jax.nn.relu(x)
            return x
        key = jax.random.key(seed)
        ks = jax.random.split(key, 32)
        inp = {'x': jax.random.normal(ks[0], (B, T, V, DIMS[0]), dtype=jnp.float32), 'A': jax.random.uniform(ks[1], (V, V), dtype=jnp.float32) / V}
        ki = 2
        for i in range(3):
            cin, cout = (DIMS[i], DIMS[i + 1])
            bound = float(np.sqrt(6.0 / (cin + cout)))
            inp[f'W{i}'] = jax.random.uniform(ks[ki], (cin, cout), minval=-bound, maxval=bound, dtype=jnp.float32)
            ki += 1
            inp[f'b{i}'] = jnp.zeros((cout,), dtype=jnp.float32)
            inp[f'g{i}'] = jnp.ones((cout,), dtype=jnp.float32)
            inp[f'be{i}'] = jnp.zeros((cout,), dtype=jnp.float32)
            inp[f'm{i}'] = 0.1 * jax.random.normal(ks[ki], (cout,), dtype=jnp.float32)
            ki += 1
            inp[f'v{i}'] = jax.random.uniform(ks[ki], (cout,), minval=0.5, maxval=1.5, dtype=jnp.float32)
            ki += 1
        return inp
    _L0_tok_all = _L0_tok_setup()
    _L0_tok_in = {k: v for k, v in _L0_tok_all.items() if k in ('A', 'W0', 'b0', 'g0', 'be0', 'm0', 'v0', 'W1', 'b1', 'g1', 'be1', 'm1', 'v1', 'W2', 'b2', 'g2', 'be2', 'm2', 'v2')}
    del _L0_tok_all

    def _L0_attn_setup():
        import jax, jax.numpy as jnp
        import numpy as np
        key = jax.random.key(seed)
        ks = jax.random.split(key, 4)
        B, S, D = (4, 1024, 64)
        x = jax.random.normal(ks[0], (B, S, D), dtype=jnp.float32)
        Wq = jax.random.normal(ks[1], (D, D), dtype=jnp.float32) * 0.02
        Wk = jax.random.normal(ks[2], (D, D), dtype=jnp.float32) * 0.02
        Wv = jax.random.normal(ks[3], (D, D), dtype=jnp.float32) * 0.02
        bq = jnp.zeros((D,), dtype=jnp.float32)
        bk = jnp.zeros((D,), dtype=jnp.float32)
        bv = jnp.zeros((D,), dtype=jnp.float32)
        return {'x': x, 'Wq': Wq, 'bq': bq, 'Wk': Wk, 'bk': bk, 'Wv': Wv, 'bv': bv}
    _L0_attn_all = _L0_attn_setup()
    _L0_attn_in = {k: v for k, v in _L0_attn_all.items() if k in ('Wq', 'bq', 'Wk', 'bk', 'Wv', 'bv')}
    del _L0_attn_all

    def _L0_ffn_setup():
        import jax, jax.numpy as jnp
        import numpy as np
        TOP_K = 6
        LN_EPS = 1e-05
        key = jax.random.key(seed)
        ks = jax.random.split(key, 4)
        B, S, D, E = (2, 64, 64, 64)
        x = jax.random.normal(ks[0], (B, S, D), dtype=jnp.float32)
        gate_w = jax.random.normal(ks[1], (E, D), dtype=jnp.float32) * 0.02
        lattice_weights = jax.random.normal(ks[2], (E, D, D), dtype=jnp.float32) * 0.02
        out_w = jax.random.normal(ks[3], (D, D), dtype=jnp.float32) * 0.02
        out_b = jnp.zeros((D,), dtype=jnp.float32)
        ln_g = jnp.ones((D,), dtype=jnp.float32)
        ln_b = jnp.zeros((D,), dtype=jnp.float32)
        return {'x': x, 'gate_w': gate_w, 'lattice_weights': lattice_weights, 'out_w': out_w, 'out_b': out_b, 'ln_g': ln_g, 'ln_b': ln_b}
    _L0_ffn_all = _L0_ffn_setup()
    _L0_ffn_in = {k: v for k, v in _L0_ffn_all.items() if k in ('gate_w', 'lattice_weights', 'out_w', 'out_b', 'ln_g', 'ln_b')}
    del _L0_ffn_all

    def _L1_attn_setup():
        import jax, jax.numpy as jnp
        import numpy as np
        import math
        B, T, D_MODEL = (1, 512, 64)
        N_Q, N_KV = (16, 1)
        D_HEAD = D_MODEL // N_KV
        QPG = N_Q // N_KV
        ROPE_BASE = 10000.0
        WINDOW = 128
        EPS = 1.1920929e-07
        NEG = -1e+30

        def _rope(x, base=ROPE_BASE):
            t, d = (x.shape[-2], x.shape[-1])
            freqs = base ** (-2.0 * jnp.arange(d // 2, dtype=jnp.float32) / d)
            theta = jnp.arange(t, dtype=jnp.float32)[:, None] * freqs[None, :]
            cos, sin = (jnp.cos(theta), jnp.sin(theta))
            x1, x2 = (x[..., 0::2], x[..., 1::2])
            r1 = x1 * cos - x2 * sin
            r2 = x1 * sin + x2 * cos
            return jnp.stack([r1, r2], axis=-1).reshape(x.shape)

        def _rmsnorm(x, w):
            return x * jax.lax.rsqrt(jnp.mean(x * x, axis=-1, keepdims=True) + EPS) * w
        key = jax.random.key(seed)
        k0, k1, k2, k3 = jax.random.split(key, 4)
        x = jax.random.normal(k0, (B, T, D_MODEL), dtype=jnp.float32)
        wq = jax.random.normal(k1, (QPG * N_KV * D_HEAD, D_MODEL), dtype=jnp.float32) * 0.02
        wkv = jax.random.normal(k2, (2 * D_HEAD * N_KV, D_MODEL), dtype=jnp.float32) * 0.02
        wo = jax.random.normal(k3, (D_MODEL, D_HEAD * N_Q * N_KV), dtype=jnp.float32) * 0.02
        q_norm_w = jnp.ones((D_HEAD,), dtype=jnp.float32)
        k_norm_w = jnp.ones((D_HEAD,), dtype=jnp.float32)
        return {'x': x, 'wq': wq, 'wkv': wkv, 'wo': wo, 'q_norm_w': q_norm_w, 'k_norm_w': k_norm_w}
    _L1_attn_all = _L1_attn_setup()
    _L1_attn_in = {k: v for k, v in _L1_attn_all.items() if k in ('wq', 'wkv', 'wo', 'q_norm_w', 'k_norm_w')}
    del _L1_attn_all

    def _L1_ffn_setup():
        import jax, jax.numpy as jnp
        import numpy as np
        E = 8
        K = 2
        D = 64
        H = 128
        DOUT = 64
        EPS = 1e-05
        key = jax.random.key(seed)
        ks = jax.random.split(key, 9)
        s = 0.02
        return {'x': jax.random.normal(ks[0], (4, 2048, D), jnp.float32), 'gamma': 1.0 + 0.05 * jax.random.normal(ks[1], (D,), jnp.float32), 'beta': 0.05 * jax.random.normal(ks[2], (D,), jnp.float32), 'Wr': 0.01 * jax.random.normal(ks[3], (D, E), jnp.float32), 'br': jnp.zeros((E,), jnp.float32), 'W1': s * jax.random.normal(ks[4], (E, D, H), jnp.float32), 'b1': s * jax.random.normal(ks[5], (E, H), jnp.float32), 'W2': s * jax.random.normal(ks[6], (E, H, DOUT), jnp.float32), 'b2': s * jax.random.normal(ks[7], (E, DOUT), jnp.float32)}
    _L1_ffn_all = _L1_ffn_setup()
    _L1_ffn_in = {k: v for k, v in _L1_ffn_all.items() if k in ('gamma', 'beta', 'Wr', 'br', 'W1', 'b1', 'W2', 'b2')}
    del _L1_ffn_all
    return {'x': x, 'L0_tok_A': _L0_tok_in['A'], 'L0_tok_W0': _L0_tok_in['W0'], 'L0_tok_b0': _L0_tok_in['b0'], 'L0_tok_g0': _L0_tok_in['g0'], 'L0_tok_be0': _L0_tok_in['be0'], 'L0_tok_m0': _L0_tok_in['m0'], 'L0_tok_v0': _L0_tok_in['v0'], 'L0_tok_W1': _L0_tok_in['W1'], 'L0_tok_b1': _L0_tok_in['b1'], 'L0_tok_g1': _L0_tok_in['g1'], 'L0_tok_be1': _L0_tok_in['be1'], 'L0_tok_m1': _L0_tok_in['m1'], 'L0_tok_v1': _L0_tok_in['v1'], 'L0_tok_W2': _L0_tok_in['W2'], 'L0_tok_b2': _L0_tok_in['b2'], 'L0_tok_g2': _L0_tok_in['g2'], 'L0_tok_be2': _L0_tok_in['be2'], 'L0_tok_m2': _L0_tok_in['m2'], 'L0_tok_v2': _L0_tok_in['v2'], 'L0_attn_Wq': _L0_attn_in['Wq'], 'L0_attn_bq': _L0_attn_in['bq'], 'L0_attn_Wk': _L0_attn_in['Wk'], 'L0_attn_bk': _L0_attn_in['bk'], 'L0_attn_Wv': _L0_attn_in['Wv'], 'L0_attn_bv': _L0_attn_in['bv'], 'L0_ffn_gate_w': _L0_ffn_in['gate_w'], 'L0_ffn_lattice_weights': _L0_ffn_in['lattice_weights'], 'L0_ffn_out_w': _L0_ffn_in['out_w'], 'L0_ffn_out_b': _L0_ffn_in['out_b'], 'L0_ffn_ln_g': _L0_ffn_in['ln_g'], 'L0_ffn_ln_b': _L0_ffn_in['ln_b'], 'L1_attn_wq': _L1_attn_in['wq'], 'L1_attn_wkv': _L1_attn_in['wkv'], 'L1_attn_wo': _L1_attn_in['wo'], 'L1_attn_q_norm_w': _L1_attn_in['q_norm_w'], 'L1_attn_k_norm_w': _L1_attn_in['k_norm_w'], 'L1_ffn_gamma': _L1_ffn_in['gamma'], 'L1_ffn_beta': _L1_ffn_in['beta'], 'L1_ffn_Wr': _L1_ffn_in['Wr'], 'L1_ffn_br': _L1_ffn_in['br'], 'L1_ffn_W1': _L1_ffn_in['W1'], 'L1_ffn_b1': _L1_ffn_in['b1'], 'L1_ffn_W2': _L1_ffn_in['W2'], 'L1_ffn_b2': _L1_ffn_in['b2']}

def reference(x, L0_tok_A, L0_tok_W0, L0_tok_b0, L0_tok_g0, L0_tok_be0, L0_tok_m0, L0_tok_v0, L0_tok_W1, L0_tok_b1, L0_tok_g1, L0_tok_be1, L0_tok_m1, L0_tok_v1, L0_tok_W2, L0_tok_b2, L0_tok_g2, L0_tok_be2, L0_tok_m2, L0_tok_v2, L0_attn_Wq, L0_attn_bq, L0_attn_Wk, L0_attn_bk, L0_attn_Wv, L0_attn_bv, L0_ffn_gate_w, L0_ffn_lattice_weights, L0_ffn_out_w, L0_ffn_out_b, L0_ffn_ln_g, L0_ffn_ln_b, L1_attn_wq, L1_attn_wkv, L1_attn_wo, L1_attn_q_norm_w, L1_attn_k_norm_w, L1_ffn_gamma, L1_ffn_beta, L1_ffn_Wr, L1_ffn_br, L1_ffn_W1, L1_ffn_b1, L1_ffn_W2, L1_ffn_b2):
    import jax
    import jax.numpy as jnp

    def _L0_tok_ref(x, A, W0, b0, g0, be0, m0, v0, W1, b1, g1, be1, m1, v1, W2, b2, g2, be2, m2, v2):
        import jax, jax.numpy as jnp
        import numpy as np
        EPS = 1e-05
        B, T, V = (32, 64, 75)
        DIMS = [3, 128, 128, 64]

        def _layer(x, A, W, b, g, be, m, v, relu):
            x = jnp.einsum('btvc,co->btvo', x, W)
            x = jnp.einsum('uv,btvo->btuo', A, x)
            x = x + b
            x = (x - m) * (g * jax.lax.rsqrt(v + EPS)) + be
            if relu:
                x = jax.nn.relu(x)
            return x
        x = _layer(x, A, W0, b0, g0, be0, m0, v0, relu=True)
        x = _layer(x, A, W1, b1, g1, be1, m1, v1, relu=True)
        x = _layer(x, A, W2, b2, g2, be2, m2, v2, relu=False)
        return x.mean(axis=2)

    def _L0_attn_ref(x, Wq, bq, Wk, bk, Wv, bv):
        import jax, jax.numpy as jnp
        import numpy as np
        Q = jnp.einsum('bsd,de->bse', x, Wq) + bq
        K = jnp.einsum('bsd,de,->bse'.replace(',->', '->'), x, Wk) + bk
        V = jnp.einsum('bsd,de->bse', x, Wv) + bv
        scale = 1.0 / jnp.sqrt(jnp.asarray(Q.shape[-1], dtype=jnp.float32))
        scores = jnp.einsum('bqd,bkd->bqk', Q, K) * scale
        weights = jax.nn.softmax(scores, axis=-1)
        return jnp.einsum('bqk,bkd->bqd', weights, V)

    def _L0_ffn_ref(x, gate_w, lattice_weights, out_w, out_b, ln_g, ln_b):
        import jax, jax.numpy as jnp
        import numpy as np
        TOP_K = 6
        LN_EPS = 1e-05
        logits = jnp.einsum('bsd,ed->bse', x, gate_w)
        top_logits, indices = jax.lax.top_k(logits, TOP_K)
        scores = jax.nn.softmax(top_logits, axis=-1)
        W_sel = lattice_weights[indices]
        xW = jnp.einsum('bsd,bskde->bske', x, W_sel)
        lattice_out = jnp.einsum('bske,bsk->bse', xW, scores)
        proj = jnp.einsum('bsd,ed->bse', lattice_out, out_w) + out_b
        h = x + proj
        mu = jnp.mean(h, axis=-1, keepdims=True)
        var = jnp.mean(jnp.square(h - mu), axis=-1, keepdims=True)
        return (h - mu) * jax.lax.rsqrt(var + LN_EPS) * ln_g + ln_b

    def _L1_attn_ref(x, wq, wkv, wo, q_norm_w, k_norm_w):
        import jax, jax.numpy as jnp
        import numpy as np
        import math
        B, T, D_MODEL = (1, 512, 64)
        N_Q, N_KV = (16, 1)
        D_HEAD = D_MODEL // N_KV
        QPG = N_Q // N_KV
        ROPE_BASE = 10000.0
        WINDOW = 128
        EPS = 1.1920929e-07
        NEG = -1e+30

        def _rope(x, base=ROPE_BASE):
            t, d = (x.shape[-2], x.shape[-1])
            freqs = base ** (-2.0 * jnp.arange(d // 2, dtype=jnp.float32) / d)
            theta = jnp.arange(t, dtype=jnp.float32)[:, None] * freqs[None, :]
            cos, sin = (jnp.cos(theta), jnp.sin(theta))
            x1, x2 = (x[..., 0::2], x[..., 1::2])
            r1 = x1 * cos - x2 * sin
            r2 = x1 * sin + x2 * cos
            return jnp.stack([r1, r2], axis=-1).reshape(x.shape)

        def _rmsnorm(x, w):
            return x * jax.lax.rsqrt(jnp.mean(x * x, axis=-1, keepdims=True) + EPS) * w
        Bx, Tx, C = x.shape
        q = x @ wq.T
        kv = x @ wkv.T
        k, v = (kv[..., :N_KV * D_HEAD], kv[..., N_KV * D_HEAD:])
        q = q.reshape(Bx, Tx, QPG, N_KV, D_HEAD).transpose(0, 2, 3, 1, 4)
        k = k.reshape(Bx, Tx, 1, N_KV, D_HEAD).transpose(0, 2, 3, 1, 4)
        v = v.reshape(Bx, Tx, 1, N_KV, D_HEAD).transpose(0, 2, 3, 1, 4)
        q = _rmsnorm(_rope(q), q_norm_w)
        k = _rmsnorm(_rope(k), k_norm_w)
        rows = jnp.arange(Tx)[:, None]
        cols = jnp.arange(Tx)[None, :]
        mask = (cols <= rows) & (rows - cols <= WINDOW)
        scale = 1.0 / math.sqrt(D_HEAD)
        scores = jnp.einsum('bqgtd,bqgsd->bqgts', q, k) * scale
        scores = jnp.where(mask[None, None, None], scores, NEG)
        attn = jax.nn.softmax(scores, axis=-1)
        out = jnp.einsum('bqgts,bqgsd->bqgtd', attn, v)
        out = out.transpose(0, 3, 1, 2, 4).reshape(Bx, Tx, QPG * N_KV * D_HEAD)
        return out @ wo.T

    def _L1_ffn_ref(x, gamma, beta, Wr, br, W1, b1, W2, b2):
        import jax, jax.numpy as jnp
        import numpy as np
        E = 8
        K = 2
        D = 64
        H = 128
        DOUT = 64
        EPS = 1e-05
        mu = jnp.mean(x, axis=-1, keepdims=True)
        var = jnp.mean(jnp.square(x - mu), axis=-1, keepdims=True)
        xn = (x - mu) * jax.lax.rsqrt(var + EPS) * gamma + beta
        logits = jnp.einsum('bsd,de->bse', xn, Wr) + br
        top_vals, top_idx = jax.lax.top_k(logits, K)
        w = jax.nn.softmax(top_vals, axis=-1)
        w_full = jnp.einsum('bsk,bske->bse', w, jax.nn.one_hot(top_idx, E, dtype=w.dtype))
        y = jnp.zeros(x.shape[:-1] + (DOUT,), x.dtype)
        for e in range(E):
            h = jax.nn.gelu(jnp.einsum('bsd,dh->bsh', xn, W1[e]) + b1[e], approximate=False)
            y_e = jnp.einsum('bsh,hd->bsd', h, W2[e]) + b2[e]
            y = y + y_e * w_full[..., e, None]
        return y
    h = _L0_tok_ref(x, L0_tok_A, L0_tok_W0, L0_tok_b0, L0_tok_g0, L0_tok_be0, L0_tok_m0, L0_tok_v0, L0_tok_W1, L0_tok_b1, L0_tok_g1, L0_tok_be1, L0_tok_m1, L0_tok_v1, L0_tok_W2, L0_tok_b2, L0_tok_g2, L0_tok_be2, L0_tok_m2, L0_tok_v2)
    h = _layernorm(h + _L0_attn_ref(h, L0_attn_Wq, L0_attn_bq, L0_attn_Wk, L0_attn_bk, L0_attn_Wv, L0_attn_bv), axis=-1)
    h = _layernorm(h + _L0_ffn_ref(h, L0_ffn_gate_w, L0_ffn_lattice_weights, L0_ffn_out_w, L0_ffn_out_b, L0_ffn_ln_g, L0_ffn_ln_b), axis=-1)
    h = _layernorm(h + _L1_attn_ref(h, L1_attn_wq, L1_attn_wkv, L1_attn_wo, L1_attn_q_norm_w, L1_attn_k_norm_w), axis=-1)
    h = _layernorm(h + _L1_ffn_ref(h, L1_ffn_gamma, L1_ffn_beta, L1_ffn_Wr, L1_ffn_br, L1_ffn_W1, L1_ffn_b1, L1_ffn_W2, L1_ffn_b2), axis=-1)
    return h

_drawn_inputs = setup_inputs


def setup_inputs(seed=0):
    import zlib

    import numpy as np

    out = dict(_drawn_inputs(seed))
    spreads = {'L0_tok_b0': (0.0, 0.1),
     'L0_tok_g0': (1.0, 0.6),
     'L0_tok_be0': (0.0, 0.1),
     'L0_tok_b1': (0.0, 0.1),
     'L0_tok_g1': (1.0, 0.2),
     'L0_tok_be1': (0.0, 0.1),
     'L0_tok_b2': (0.0, 0.1),
     'L0_tok_g2': (1.0, 0.2),
     'L0_tok_be2': (0.0, 0.1),
     'L0_attn_bq': (0.0, 0.8),
     'L0_attn_bk': (0.0, 2.0),
     'L0_attn_bv': (0.0, 0.1),
     'L0_ffn_out_b': (0.0, 0.1),
     'L0_ffn_ln_g': (1.0, 0.2),
     'L0_ffn_ln_b': (0.0, 0.1),
     'L1_attn_q_norm_w': (1.0, 0.6),
     'L1_attn_k_norm_w': (1.0, 0.6),
     'L1_ffn_br': (0.0, 0.8)}
    factors = {'x': 5.268,
     'L0_tok_A': 8.0,
     'L0_tok_W0': 4.351,
     'L0_tok_v0': 3.003,
     'L0_attn_Wq': 8.0,
     'L0_attn_Wk': 8.0,
     'L0_ffn_gate_w': 8.0,
     'L0_ffn_lattice_weights': 8.0,
     'L0_ffn_out_w': 8.0,
     'L1_attn_wq': 8.0,
     'L1_ffn_gamma': 8.0,
     'L1_ffn_beta': 8.0,
     'L1_ffn_Wr': 4.352,
     'L1_ffn_W1': 4.152,
     'L1_ffn_b1': 8.0,
     'L1_ffn_W2': 4.027,
     'L1_ffn_b2': 11.697}
    for name, (base, spread) in spreads.items():
        noise = np.random.default_rng([zlib.crc32(name.encode()), seed]).standard_normal(out[name].shape)
        drawn = base * np.exp(spread * noise) if base else spread * noise
        out[name] = jnp.asarray(drawn.astype(out[name].dtype))
    for name, factor in factors.items():
        out[name] = (out[name] * factor).astype(out[name].dtype)
    return out
```

```python
from contextlib import ExitStack

import concourse.bass as bass
from concourse import mybir

F32 = mybir.dt.float32
F32R = mybir.dt.float32r
BF16 = mybir.dt.bfloat16
ALU = mybir.AluOpType
ACT = mybir.ActivationFunctionType
AX_X = mybir.AxisListType.X

P = 128
BATCHES = 64
SEQ = 64
TOKENS = BATCHES * SEQ
V = 75
C0 = 3
CH = 128
D = 64
EPS_BN = 1e-5

NODES_INV = 1.0 / V
EPS_LN = 1e-5
EPS_RMS = 1.1920929e-07
CHUNK_BLOCKS = 4
BLOCKS = TOKENS // P
CHUNKS = BLOCKS // CHUNK_BLOCKS
CT = CHUNK_BLOCKS * P
CB = CT // SEQ
EXPERTS0 = 64
TOP0 = 6
HEADS = 16
PAIRS = HEADS // 2
EXPERTS1 = 8
HID1 = 128
BIG = 3.0e38
MASKED = -1.0e30

UNIT = 4
GROUP = 8
ITER = 32
UNITS = SEQ // UNIT
ROWS = 32
BIAS_ROW = GROUP * C0


N_ATT, N_LAT, N_ROT, N_GELU = 12, 33, 36, 43

class Tally:

    def __init__(self):
        self.base, self.trip, self.k = 0, 0, 0

    def enter(self, i, per_trip):
        self.trip, self.k, self.per = i * per_trip, 0, per_trip

    def leave(self, trips):
        assert self.k == self.per, (self.k, self.per)
        self.base, self.trip, self.k = self.base + trips * self.per, 0, 0

    def next(self):
        self.k += 1
        return self.trip + (self.base + self.k)


class Chain:

    def __init__(self, eng, sem):
        self.eng, self.sem, self.base, self.trip, self.k = eng, sem, 0, 0, 0

    def enter(self, i, per_trip):
        self.base, self.trip, self.k, self.per = self.base + self.k, i * per_trip, 0, per_trip

    def leave(self, trips):
        assert self.k == self.per, (self.k, self.per)
        self.base, self.trip, self.k = self.base + trips * self.per, 0, 0

    def __call__(self, ins):
        ins.then_inc(self.sem, 1)
        self.k += 1
        return self.trip + (self.base + self.k)

    def wait(self, mark=None):
        self.eng.wait_ge(self.sem, self.trip + (self.base + self.k) if mark is None else mark)


ROW_NAMES = ("bv", "out_b", "ln_g", "ln_b", "q_norm", "k_norm", "gamma", "beta")
ROW_AT = {name: n * D for n, name in enumerate(ROW_NAMES)}
ROW_AT["b2"] = len(ROW_NAMES) * D
ROW_AT["br"] = ROW_AT["b2"] + EXPERTS1 * D
ROW_WIDTH = ROW_AT["br"] + EXPERTS1


def build(nc, t):
    with ExitStack() as ctx:
        def sb(name, shape, dt=F32):
            return ctx.enter_context(nc.sbuf_tensor(name, shape, dt))

        def sem(name):
            return ctx.enter_context(nc.semaphore(name))

        bank = [ctx.enter_context(nc.psum_tensor(f"bank{i}", [P, 512], F32)) for i in range(8)]

        ident = sb("ident", [P, P])
        cols = sb("cols", [P, 16])
        cols64 = sb("cols64", [P, 8])
        AT = sb("AT", [P, V])
        A_nat = sb("A_nat", [V, V])
        ones = sb("ones", [P, P])
        w0_hl = sb("w0_hl", [P, GROUP * CH], F32R)
        w1_raw = sb("w1_raw", [CH, CH])
        w1_s = sb("w1_s", [CH, CH])
        w2_raw = sb("w2_raw", [CH, D])
        w2_s = sb("w2_s", [CH, D])
        half_neg = sb("half_neg", [P, 64])
        bn_scale = sb("bn_scale", [P, 4])
        bn_bias = sb("bn_bias", [P, 4])
        bn_tmp = sb("bn_tmp", [P, 4])
        neg_b1 = sb("neg_b1", [P, 1])
        diag = sb("diag", [P, 5, P])
        rows_b = sb("rows_b", [P, 5, P])
        abar = sb("abar", [P, V])
        a_sum = sb("a_sum", [P, 1])
        s_corr = sb("s_corr", [P, 1])

        x_t = sb("x_t", [V, 2, ITER * C0])
        x_rep = sb("x_rep", [V, 2, ITER // GROUP, P // ROWS, ROWS])
        y_hl = sb("y_hl", [P, 2, ITER // GROUP, V], F32R)
        h0_sb = sb("h0_sb", [P, 2, UNIT * CH])
        ah_sb = sb("ah_sb", [CH, 2, UNIT * V])
        prod_bd = sb("prod_bd", [P, 2 * 4 * UNIT * V])
        prod = prod_bd[:].rearrange("p (s q n) -> p s q n", s=2, q=4)
        sT = sb("sT", [CH, TOKENS])


        rows = sb("rows", [P, ROW_WIDTH])
        att_w = sb("att_w", [D, 3 * D])
        gate_wT = sb("gate_wT", [D, EXPERTS0])
        lat_w = sb("lat_w", [P, EXPERTS0 // 2, D])
        out_wT = sb("out_wT", [D, D])
        pick = sb("pick", [P, EXPERTS0, D], F32R)
        ident2 = sb("ident2", [P, D])
        q_wh = sb("q_wh", [P, 2, HEADS * D], F32R)
        q_wl = sb("q_wl", [P, 2, HEADS * D], F32R)
        kv_w = sb("kv_w", [P, 4 * D])
        kv_wh = sb("kv_wh", [P, 4 * D], F32R)
        kv_wl = sb("kv_wl", [P, 4 * D], F32R)
        wo_w = sb("wo_w", [P, PAIRS, D])
        trig_f = sb("trig_f", [P, 2, SEQ])
        trig_t = sb("trig_t", [P, 2, D])
        qk_gain = sb("qk_gain", [P, D])
        head_of = sb("head_of", [P, 2])
        ident_bf = sb("ident_bf", [P, P], BF16)
        mask_bf = sb("mask_bf", [P, CT], BF16)
        mask_in = sb("mask_in", [P, CT])
        r_w = sb("r_w", [P, EXPERTS1])
        r_wh = sb("r_wh", [P, EXPERTS1], F32R)
        r_wl = sb("r_wl", [P, EXPERTS1], F32R)
        e1_wh = sb("e1_wh", [P, EXPERTS1 * HID1], F32R)
        e1_wl = sb("e1_wl", [P, EXPERTS1 * HID1], F32R)
        e1_b = sb("e1_b", [P, EXPERTS1])
        e2_w = sb("e2_w", [P, EXPERTS1, D])

        hN = sb("hN", [P, BLOCKS, D])
        s_chunk = sb("s_chunk", [CH, CT])
        hT = sb("hT", [D, CT])
        x_tok = sb("x_tok", [P, CHUNK_BLOCKS, D])
        qT = sb("qT", [D, CT])
        kT = sb("kT", [D, CT])
        v_sb = sb("v_sb", [SEQ, CB, D])
        xc = sb("xc", [P, CHUNK_BLOCKS, D])
        xsq = sb("xsq", [P, CHUNK_BLOCKS, D])
        res = sb("res", [P, CHUNK_BLOCKS, D])
        ln_mean = sb("ln_mean", [P, CHUNK_BLOCKS])
        ln_var = sb("ln_var", [P, CHUNK_BLOCKS])
        ln_rstd = sb("ln_rstd", [P, CHUNK_BLOCKS])
        row_max = sb("row_max", [P, CHUNK_BLOCKS])
        row_sum = sb("row_sum", [P, CHUNK_BLOCKS])
        row_inv = sb("row_inv", [P, CHUNK_BLOCKS])
        sc = sb("sc", [P, CHUNK_BLOCKS, D])
        sc_e = sb("sc_e", [P, CHUNK_BLOCKS, D])
        eT = sb("eT", [SEQ, CHUNK_BLOCKS, P])
        x2 = sb("x2", [P, CHUNK_BLOCKS, 2, D])
        xT2 = sb("xT2", [P, CT])
        lg = sb("lg", [P, CHUNK_BLOCKS, EXPERTS0])
        top = sb("top", [P, CHUNK_BLOCKS, 8])
        top_max = sb("top_max", [P, CHUNK_BLOCKS])
        left = sb("left", [P, CHUNK_BLOCKS, EXPERTS0])
        w2x = sb("w2x", [P, CHUNK_BLOCKS, 2, EXPERTS0])
        wT_hl = sb("wT_hl", [P, CT], F32R)
        zT = sb("zT", [P, 2, CT])
        latT = sb("latT", [D, CT])
        xT_hl = sb("xT_hl", [P, CT], F32R)
        rope_c = zT
        rope_s = sb("rope_s", [P, 2, CT])
        q_sq = sb("q_sq", [P, 2, CT])
        qr = sT
        k_t = sb("k_t", [P, CHUNK_BLOCKS, D])
        k_s = sb("k_s", [P, CHUNK_BLOCKS, D])
        k_var = sb("k_var", [P, CHUNK_BLOCKS])
        k_rms = sb("k_rms", [P, CHUNK_BLOCKS])
        q_var = sb("q_var", [P, CHUNK_BLOCKS * HEADS])
        q_rms = sb("q_rms", [P, CHUNK_BLOCKS * HEADS])
        k_bd = prod_bd[:, 0:2 * CT].rearrange("p (b h s) -> p b h s", b=CB, h=2)
        v_bd = prod_bd[:, 2 * CT:4 * CT].rearrange("p (b h s) -> p b h s", b=CB, h=2)
        vw = sb("vw", [P, CB, PAIRS * D])
        q_w = vw[:, 0:4, :].rearrange("p b n -> p (b n)").rearrange("p (s n) -> p s n", s=2)
        e1_w = vw[:, 4:6, :].rearrange("p b n -> p (b n)")
        p_max = sb("p_max", [P, 2, HEADS])
        p_sum = sb("p_sum", [P, 2, HEADS])
        p_inv = sb("p_inv", [P, 2, HEADS])
        p_sc = sb("p_sc", [P, 2, HEADS * SEQ])
        w0_tmp = p_sc[:, 0, :]
        pT = sb("pT", [P, 2, PAIRS * P])
        w0_raw = pT[:, 0, :]
        hid = rope_s
        wf = sb("wf", [P, CHUNK_BLOCKS, EXPERTS1])
        moe = q_sq

        y_ps = bank[0]
        h0_ps = [bank[1], bank[2]]
        ah_ps = [bank[3], bank[4]]
        z_ps = [bank[5], bank[6]]
        mix_ps = bank[7]

        consts_in = sem("consts_in")
        x_in = [sem("x_in0"), sem("x_in1")]
        pool_order, dve_order, act_order = sem("pool_order"), sem("dve_order"), sem("act_order")
        pe_gate, pool_gate = sem("pe_gate"), sem("pool_gate")
        ones_set = sem("ones_set")
        bn_var = sem("bn_var")
        bn_rsqrt = sem("bn_rsqrt")
        diag_ready = sem("diag_ready")
        rows_done = sem("rows_done")
        abar_done = sem("abar_done")
        weights_ready = sem("weights_ready")
        h0_zeroed = sem("h0_zeroed")
        x_copied = sem("x_copied")
        y_done = sem("y_done")
        y_high = sem("y_high")
        y_ready = sem("y_ready")
        l0_done = sem("l0_done")
        h0_ready = sem("h0_ready")
        amix_done = sem("amix_done")
        ah_ready = sem("ah_ready")
        z_done = sem("z_done")
        prod_done = sem("prod_done")
        s_ready = sem("s_ready")
        out_sem = sem("out_sem")
        later_in = sem("later_in")
        pick_ready = sem("pick_ready")
        splits_ready = sem("splits_ready")
        sT_copied = sem("sT_copied")
        att_h_done = sem("att_h_done")
        att_hT_ready = sem("att_hT_ready")
        att_qkv_done = sem("att_qkv_done")
        att_qk_ready = sem("att_qk_ready")
        att_v_ready = sem("att_v_ready")
        att_s_done = sem("att_s_done")
        att_d_ready = sem("att_d_ready")
        att_e_ready = sem("att_e_ready")
        att_eT_done = sem("att_eT_done")
        att_eT_ready = sem("att_eT_ready")
        att_o_done = sem("att_o_done")
        ln_var_ready = sem("ln_var_ready")
        ln_rstd_ready = sem("ln_rstd_ready")
        hN_ready = sem("hN_ready")
        x2_ready = sem("x2_ready")
        xT_done = sem("xT_done")
        xT_ready = sem("xT_ready")
        lg_done = sem("lg_done")
        lg_d_ready = sem("lg_d_ready")
        lg_e_ready = sem("lg_e_ready")
        w2_ready = sem("w2_ready")
        wT_done = sem("wT_done")
        wT_ready = sem("wT_ready")
        bc_done = sem("bc_done")
        z_ready = sem("z_ready")
        lat_done = sem("lat_done")
        latT_ready = sem("latT_ready")
        proj_done = sem("proj_done")
        gx2_ready = sem("gx2_ready")
        gxT_done = sem("gxT_done")
        gxT_ready = sem("gxT_ready")
        kn_done = sem("kn_done")
        k_rms_in = sem("k_rms_in")
        k_rms_out = sem("k_rms_out")
        k2_ready = sem("k2_ready")
        kT_done = sem("kT_done")
        kbd_ready = sem("kbd_ready")
        vT_done = sem("vT_done")
        vbd_ready = sem("vbd_ready")
        q_done = sem("q_done")
        q_rope_ready = sem("q_rope_ready")
        q_sq_ready = sem("q_sq_ready")
        norm_done = sem("norm_done")
        q_rms_in = sem("q_rms_in")
        q_rms_out = sem("q_rms_out")
        vw_done = sem("vw_done")
        vw_ready = sem("vw_ready")
        att2_s_done = sem("att2_s_done")
        att2_d_ready = sem("att2_d_ready")
        att2_dr_ready = sem("att2_dr_ready")
        att2_e_ready = sem("att2_e_ready")
        att2_p_ready = sem("att2_p_ready")
        pT_done = sem("pT_done")
        pT_ready = sem("pT_ready")
        att2_o_done = sem("att2_o_done")
        m2_ready = sem("m2_ready")
        mT_done = sem("mT_done")
        mT_ready = sem("mT_ready")
        r_done = sem("r_done")
        r_d_ready = sem("r_d_ready")
        r_e_ready = sem("r_e_ready")
        h1_done = sem("h1_done")
        h1_ready = sem("h1_ready")
        y2_done = sem("y2_done")
        q_sum_ready = sem("q_sum_ready")

        LATER = [("att_w", att_w[:]), ("gate_wT", gate_wT[:]), ("lat_w", lat_w[:]),
                 ("out_wT", out_wT[:]), ("ident2", ident2[:]), ("q_w", q_w), ("kv_w", kv_w[:]),
                 ("wo_w", wo_w[:]), ("trig_f", trig_f[:]), ("trig_t", trig_t[:]),
                 ("head_of", head_of[:]), ("mask", mask_in[:]), ("r_w", r_w[:]), ("e1_w", e1_w),
                 ("e1_b", e1_b[:]), ("e2_w", e2_w[:])]

        LATER_IN = 16 * (len(LATER) + 1)

        CONSTS = [("ident", ident[:]), ("cols", cols[:]), ("cols64", cols64[:]), ("AT", AT[:]),
                  ("A", A_nat[:]), ("w0_blocks", w0_raw), ("W1", w1_raw[:]), ("W2", w2_raw[:])]

        LAYER_STEPS = 3
        block = ctx.enter_context(nc.Block())

        def flat(ap):
            return ap.rearrange("p a b -> p (a b)")

        def per_block(ap, width=D):
            if ap.shape[1] == CHUNK_BLOCKS and width != CHUNK_BLOCKS:
                return ap.unsqueeze(2).to_broadcast([P, CHUNK_BLOCKS, width])
            return ap.unsqueeze(1).to_broadcast([P, CHUNK_BLOCKS, width])

        def row(name, width=D):
            return rows[:, ROW_AT[name]:ROW_AT[name] + width]

        def hN_chunk(c):
            return hN[:, bass.ds(c * CHUNK_BLOCKS, CHUNK_BLOCKS), :]

        @block.sync
        def _(sp):
            for name, tile in CONSTS:
                sp.dma_start(tile, t[name]).then_inc(consts_in, 16)

            def load_x(b, par):
                sp.dma_start(x_t[:, par], t["x"][:, bass.ds((b * 2 + par) * (ITER * C0), ITER * C0)]
                             ).then_inc(x_in[par], 16)

            load_x(0, 0)
            load_x(0, 1)
            sp.dma_start(rows[:], t["rows"].partition_broadcast(P)).then_inc(later_in, 16)
            for name, tile in LATER:
                sp.dma_start(tile, t[name]).then_inc(later_in, 16)
            with sp.Fori(1, BATCHES) as b:
                for par in range(2):
                    sp.wait_ge(x_copied, b * 2 + (par - 1))
                    load_x(b, par)
            for n in range(CHUNKS):
                sp.wait_ge(hN_ready, LAYER_STEPS * CHUNKS + n + 1)
                blocks = slice(n * CHUNK_BLOCKS, (n + 1) * CHUNK_BLOCKS)
                sp.dma_start(t["out"][:, blocks], hN[:, blocks]).then_inc(out_sem, 16)
            sp.wait_ge(out_sem, CHUNKS * 16)

        @block.gpsimd
        def _(pool):
            order = Chain(pool, pool_order)
            pool.memset(ones[:], 1.0).then_inc(ones_set, 1)
            order(pool.memset(half_neg[:], -0.5))
            order(pool.memset(x_rep[:], 0.0))
            pool.memset(h0_sb[:], 0.0).then_inc(h0_zeroed, 1)

            def copy_x(b, par, first):
                pool.wait_ge(x_in[par], b * 16 + 16)
                if not first:
                    pool.wait_ge(y_done, b * 2 + (par - 1))
                    pool.sem_inc(pool_gate, 1)
                for g in range(ITER // GROUP):
                    ins = pool.tensor_copy(
                        x_rep[:, par, g, :, 0:GROUP * C0],
                        x_t[:, par, g * GROUP * C0:(g + 1) * GROUP * C0].unsqueeze(1).to_broadcast(
                            [V, P // ROWS, GROUP * C0]))
                ins.then_inc(x_copied, 1)

            pool.wait_ge(bn_var, 1)
            order.wait()
            pool.tensor_tensor(bn_scale[:, 0:3], bn_tmp[:, 0:3], half_neg[:, 0:3],
                               ALU.pow).then_inc(bn_rsqrt, 1)
            copy_x(0, 0, True)
            copy_x(0, 1, True)
            pool.wait_ge(later_in, LATER_IN)
            pool.tensor_copy(pick[:], ident2[:].unsqueeze(2).to_broadcast([P, EXPERTS0, D])).then_inc(pick_ready, 1)
            order(pool.tensor_copy(ident_bf[:], ident[:]))
            order(pool.tensor_copy(mask_bf[:], mask_in[:]))
            order(pool.tensor_scalar(qk_gain[:], row("q_norm"), D ** -0.5, None, ALU.mult))
            splits = ((q_wh[:], q_wl[:], q_w), (kv_wh[:], kv_wl[:], kv_w[:]),
                      (r_wh[:], r_wl[:], r_w[:]), (e1_wh[:], e1_wl[:], e1_w))
            for high, low, raw in splits:
                order(pool.tensor_copy(high, raw))
            order.wait()
            order(pool.tensor_tensor(qk_gain[:], qk_gain[:], row("k_norm"), ALU.mult))
            for high, low, raw in splits:
                last = pool.tensor_tensor(low, raw, high.bitcast(F32), ALU.subtract)
                last.then_inc(splits_ready, 1)
            with pool.Fori(1, BATCHES) as b:
                copy_x(b, 0, False)
                copy_x(b, 1, False)

            ln = Tally()

            def ln_root():
                n = ln.next()
                pool.wait_ge(ln_var_ready, n)
                pool.tensor_tensor(ln_rstd[:], ln_var[:], half_neg[:, 0:CHUNK_BLOCKS],
                                   ALU.pow).then_inc(ln_rstd_ready, 1)

            with pool.Fori(0, CHUNKS) as c:
                ln.enter(c, 1)
                ln_root()
            ln.leave(CHUNKS)
            with pool.Fori(0, CHUNKS) as c:
                ln.enter(c, 2)
                ln_root()
                ln_root()
            ln.leave(CHUNKS)
            with pool.Fori(0, CHUNKS) as c:
                ln.enter(c, 1)
                pool.wait_ge(k_rms_in, c + 1)
                pool.tensor_tensor(k_rms[:], k_var[:], half_neg[:, 0:CHUNK_BLOCKS],
                                   ALU.pow).then_inc(k_rms_out, 1)
                pool.wait_ge(q_rms_in, c + 1)
                pool.tensor_tensor(q_rms[:], q_var[:], half_neg[:, 0:CHUNK_BLOCKS * HEADS],
                                   ALU.pow).then_inc(q_rms_out, 1)
                for j in range(CHUNK_BLOCKS):
                    pool.wait_ge(q_rms_out, c + 1)
                    pool.wait_ge(att2_d_ready, c * CHUNK_BLOCKS + (j + 1))
                    view = p_sc[:, j % 2].rearrange("p (h s) -> p h s", s=SEQ)
                    pool.tensor_tensor(view, view, q_rms[:, j * HEADS:(j + 1) * HEADS].unsqueeze(2)
                                       .to_broadcast([P, HEADS, SEQ]), ALU.mult).then_inc(att2_dr_ready, 1)
                ln_root()
            ln.leave(CHUNKS)
            with pool.Fori(0, CHUNKS) as c:
                ln.enter(c, 2)
                ln_root()
                ln_root()
            ln.leave(CHUNKS)

        @block.tensor
        def _(pe):
            pe.wait_ge(ones_set, 1)
            pe.wait_ge(diag_ready, 1)
            nc.tensor.matmul(mix_ps[:, 0:512], ones[:], diag[:, 0:4].rearrange("p a b -> p (a b)"),
                             start=True, stop=True)
            nc.tensor.matmul(z_ps[0][:, 0:P], ones[:], diag[:, 4],
                             start=True, stop=True).then_inc(rows_done, 1)
            nc.tensor.matmul(y_ps[:, 0:V], ones[0:V, :], A_nat[:], start=True,
                             stop=True).then_inc(abar_done, 1)
            pe.wait_ge(weights_ready, 1)

            def y_product(b, par):
                pe.wait_ge(x_copied, b * 2 + (par + 1))
                for g in range(ITER // GROUP):
                    ins = nc.tensor.matmul(
                        y_ps[:, g * V:(g + 1) * V],
                        x_rep[:, par, g].rearrange("v q r -> v (q r)"),
                        AT[0:V, :], start=(g == 0), stop=True, skip_group_check=True)
                ins.then_inc(y_done, 1)

            def layer0(k):
                par, g, half = (k // 8) % 2, (k % 8) // 2, k % 2
                nc.tensor.matmul(h0_ps[k % 2][0:V, :], y_hl[:, par, g, :],
                                 w0_hl[:, half * 512:(half + 1) * 512],
                                 start=True, stop=True).then_inc(l0_done, 1)

            def node_mix(k, lo, hi):
                for j in range(lo, hi):
                    ins = nc.tensor.matmul(ah_ps[k % 2][:, j * V:(j + 1) * V],
                                           h0_sb[:, k % 2, j * CH:(j + 1) * CH], AT[:],
                                           start=(j == 0), stop=True, skip_group_check=True)
                return ins

            def layer1(k, count):
                pe.wait_ge(ah_ready, count)
                nc.tensor.matmul(z_ps[k % 2][:, 0:UNIT * V], w1_s[:], ah_sb[:, k % 2, :],
                                 start=True, stop=True).then_inc(z_done, 1)

            def norms(p):
                for j in range(CHUNK_BLOCKS):
                    at = j * HEADS + 2 * p
                    ins = nc.tensor.matmul(bank[7][:, at:at + 2], q_sq[:, p % 2, j * P:(j + 1) * P],
                                           head_of[:], start=(p == 0 and j == 0), stop=True,
                                           skip_group_check=True)
                return ins

            def batch(b, first, last):
                for k in range(UNITS):
                    u = b * UNITS + k
                    pe.wait_ge(h0_ready, u + 1)
                    node_mix(k, 0, 2)
                    if not (last and k == UNITS - 1):
                        if k % 8 == 7:
                            pe.wait_ge(y_ready, b * 2 + (k // 8 + 2))
                        layer0((k + 1) % UNITS)
                    node_mix(k, 2, UNIT).then_inc(amix_done, 1)
                    if k == 2:
                        y_product(b, 1)
                    if k == 10 and not last:
                        y_product(b + 1, 0)
                    if not (first and k == 0):
                        if not (first and k < 3):
                            pe.wait_ge(prod_done, u - 2)
                        layer1((k - 1) % UNITS, u)

            y_product(0, 0)
            pe.wait_ge(y_ready, 1)
            layer0(0)
            batch(0, True, False)
            with pe.Fori(1, BATCHES - 1) as b:
                batch(b, False, False)
            batch(BATCHES - 1, False, True)
            pe.wait_ge(prod_done, BATCHES * UNITS - 2)
            layer1(UNITS - 1, BATCHES * UNITS)

            pe.wait_ge(later_in, LATER_IN)
            pe.wait_ge(pick_ready, 1)
            pe.wait_ge(splits_ready, 4)
            mm = nc.tensor.matmul

            with pe.Fori(0, CHUNKS) as c:
                pe.wait_ge(sT_copied, c + 1)
                for j in range(CHUNK_BLOCKS):
                    mm(bank[1][:, j * D:(j + 1) * D], s_chunk[:, j * P:(j + 1) * P], w2_s[:],
                       start=(j == 0), stop=True, skip_group_check=True)
                mm(bank[0][0:D, :], w2_s[:], s_chunk[:], start=True, stop=True).then_inc(att_h_done, 1)
                pe.wait_ge(att_hT_ready, c + 1)
                pe.sem_inc(pe_gate, 1)
                mm(bank[2][0:D, :], att_w[:, 0:D], hT[:], start=True, stop=True)
                mm(bank[3][0:D, :], att_w[:, D:2 * D], hT[:], start=True, stop=True).then_inc(att_qkv_done, 1)
                for b2 in range(CB):
                    ins = mm(bank[4][0:SEQ, b2 * D:(b2 + 1) * D], hT[:, b2 * SEQ:(b2 + 1) * SEQ],
                             att_w[:, 2 * D:3 * D], start=(b2 == 0), stop=True, skip_group_check=True)
                ins.then_inc(att_qkv_done, 1)
                pe.wait_ge(att_qk_ready, c * 2 + 2)
                pe.sem_inc(pe_gate, 1)
                for b2 in range(CB):
                    at = (b2 % 2) * SEQ
                    ins = mm(bank[5][at:at + SEQ, (b2 // 2) * SEQ:(b2 // 2 + 1) * SEQ],
                             qT[:, b2 * SEQ:(b2 + 1) * SEQ], kT[:, b2 * SEQ:(b2 + 1) * SEQ],
                             start=(b2 < 2), stop=True, skip_group_check=True)
                ins.then_inc(att_s_done, 1)
                pe.wait_ge(att_e_ready, c + 1)
                pe.sem_inc(pe_gate, 1)
                for j in range(CHUNK_BLOCKS):
                    ins = nc.tensor.transpose(bank[6][0:SEQ, j * P:(j + 1) * P], sc_e[:, j], ident[:])
                ins.then_inc(att_eT_done, 1)
                pe.wait_ge(att_eT_ready, c + 1)
                pe.wait_ge(att_v_ready, c + 1)
                pe.sem_inc(pe_gate, 1)
                for b2 in range(CB):
                    at = (b2 % 2) * SEQ
                    ins = mm(bank[7][at:at + SEQ, (b2 // 2) * D:(b2 // 2 + 1) * D],
                             eT[:, b2 // 2, at:at + SEQ], v_sb[:, b2],
                             start=(b2 < 2), stop=True, skip_group_check=True)
                ins.then_inc(att_o_done, 1)

            with pe.Fori(0, CHUNKS) as c:
                pe.wait_ge(x2_ready, c + 1)
                for j in range(CHUNK_BLOCKS):
                    ins = nc.tensor.transpose(bank[0][:, j * P:(j + 1) * P], flat(x2[:, j]), ident[:])
                ins.then_inc(xT_done, 1)
                pe.wait_ge(xT_ready, c + 1)
                for j in range(CHUNK_BLOCKS):
                    ins = mm(bank[1][:, j * EXPERTS0:(j + 1) * EXPERTS0], xT2[0:D, j * P:(j + 1) * P],
                             gate_wT[:], start=(j == 0), stop=True, skip_group_check=True)
                ins.then_inc(lg_done, 1)
                pe.wait_ge(w2_ready, c + 1)
                for j in range(CHUNK_BLOCKS):
                    ins = nc.tensor.transpose(bank[2][:, j * P:(j + 1) * P], flat(w2x[:, j]), ident[:])
                ins.then_inc(wT_done, 1)
                pe.wait_ge(wT_ready, c + 1)

                def spread(p):
                    mm(bank[3 + p % 2][:], flat(pick[:, 2 * p:2 * p + 2]), wT_hl[:],
                       start=True, stop=True).then_inc(bc_done, 1)

                spread(0)
                spread(1)
                for p in range(EXPERTS0 // 2):
                    pe.wait_ge(z_ready, c * (EXPERTS0 // 2) + (p + 1))
                    ins = mm(bank[5][0:D, :], lat_w[:, p], zT[:, p % 2], start=(p == 0),
                             stop=(p == EXPERTS0 // 2 - 1))
                    ins.then_inc(lat_done, 1)
                    if p + 2 < EXPERTS0 // 2:
                        spread(p + 2)
                pe.wait_ge(latT_ready, c + 1)
                for j in range(CHUNK_BLOCKS):
                    ins = mm(bank[6][:, j * D:(j + 1) * D], latT[:, j * P:(j + 1) * P], out_wT[:],
                             start=(j == 0), stop=True, skip_group_check=True)
                ins.then_inc(proj_done, 1)

            def att2_scores(c, j):
                n = c * CHUNK_BLOCKS + j
                if j >= 1:
                    pe.wait_ge(att2_d_ready, n)
                for half in range(2):
                    mm(bank[4 + half][:], ident_bf[:], mask_bf[:], start=True, stop=False,
                       skip_group_check=True)
                for b2 in range(2):
                    toks = (2 * j + b2) * SEQ
                    for p in range(PAIRS):
                        ins = mm(bank[4 + p // 4][b2 * SEQ:(b2 + 1) * SEQ, (p % 4) * P:(p % 4 + 1) * P],
                                 qr[:, p * CT + toks:p * CT + toks + SEQ], flat(k_bd[:, 2 * j + b2]),
                                 start=False, stop=(p % 4 == 3), skip_group_check=True)
                ins.then_inc(att2_s_done, 1)

            def att2_transpose(c, j):
                n = c * CHUNK_BLOCKS + j
                pe.wait_ge(att2_p_ready, n + 1)
                if j >= 1:
                    pe.wait_ge(pT_ready, n)
                for p in range(PAIRS):
                    ins = nc.tensor.transpose(bank[6 + p // 4][:, (p % 4) * P:(p % 4 + 1) * P],
                                              p_sc[:, j % 2, p * P:(p + 1) * P], ident[:])
                ins.then_inc(pT_done, 1)

            def att2_out(c, j):
                pe.wait_ge(pT_ready, c * CHUNK_BLOCKS + (j + 1))
                for b2 in range(2):
                    for p in range(PAIRS):
                        ins = mm(bank[0][b2 * SEQ:(b2 + 1) * SEQ, j * D:(j + 1) * D],
                                 pT[:, j % 2, p * P + b2 * SEQ:p * P + (b2 + 1) * SEQ],
                                 vw[:, 2 * j + b2, p * D:(p + 1) * D],
                                 start=(p == 0 and j == 0), stop=(p == PAIRS - 1), skip_group_check=True)
                ins.then_inc(att2_o_done, 1)

            with pe.Fori(0, CHUNKS) as c:
                pe.wait_ge(gx2_ready, c + 1)
                pe.wait_ge(hN_ready, c + 2 * CHUNKS)
                for j in range(CHUNK_BLOCKS):
                    ins = nc.tensor.transpose(bank[0][:, j * P:(j + 1) * P], flat(x2[:, j]), ident[:])
                ins.then_inc(gxT_done, 1)
                pe.wait_ge(gxT_ready, c + 1)
                for j in range(CHUNK_BLOCKS):
                    xs = xT_hl[:, j * P:(j + 1) * P]
                    at = slice(j * 2 * D, (j + 1) * 2 * D)
                    mm(bank[3][:, at], xs, kv_wh[:, 0:2 * D], start=(j == 0), stop=False, skip_group_check=True)
                    ins = mm(bank[3][:, at], xs, kv_wl[:, 0:2 * D], start=False, stop=True, skip_group_check=True)
                ins.then_inc(kn_done, 1)
                mm(bank[0][:], kv_wh[:, 2 * D:4 * D], xT_hl[:], start=True, stop=False)
                mm(bank[0][:], kv_wl[:, 2 * D:4 * D], xT_hl[:], start=False, stop=True).then_inc(vT_done, 1)
                for p in range(PAIRS):
                    if p >= 1:
                        pe.wait_ge(q_rope_ready, c * 2 * PAIRS + 2 * p)
                        pe.wait_ge(q_sq_ready, c * PAIRS + p)
                    for s2 in range(2):
                        mm(bank[1 + s2][:], q_wh[:, s2, p * P:(p + 1) * P], xT_hl[:], start=True, stop=False)
                        mm(bank[1 + s2][:], q_wl[:, s2, p * P:(p + 1) * P], xT_hl[:], start=False,
                           stop=True).then_inc(q_done, 1)
                    if p >= 1:
                        norms(p - 1)
                pe.wait_ge(q_sq_ready, c * PAIRS + PAIRS)
                norms(PAIRS - 1).then_inc(norm_done, 1)
                pe.wait_ge(k2_ready, c + 1)
                pe.wait_ge(vbd_ready, c + 1)
                for j in range(CHUNK_BLOCKS):
                    ins = nc.tensor.transpose(bank[0][:, j * P:(j + 1) * P], flat(x2[:, j]), ident[:])
                ins.then_inc(kT_done, 1)
                pe.wait_ge(q_rope_ready, (c + 1) * 2 * PAIRS)
                for b2 in range(CB):
                    if b2 >= 2:
                        pe.wait_ge(vw_ready, c * CB + (b2 - 1))
                    mm(bank[1 + b2 % 2][:], flat(v_bd[:, b2]), flat(wo_w[:]), start=True,
                       stop=True).then_inc(vw_done, 1)
                pe.wait_ge(kbd_ready, c + 1)
                pe.wait_ge(q_sum_ready, c * PAIRS + PAIRS)
                att2_scores(c, 0)
                for j in range(CHUNK_BLOCKS):
                    if j + 1 < CHUNK_BLOCKS:
                        att2_scores(c, j + 1)
                    att2_transpose(c, j)
                    if j == 0:
                        pe.wait_ge(vw_ready, c * CB + CB)
                    att2_out(c, j)

            with pe.Fori(0, CHUNKS) as c:
                pe.wait_ge(m2_ready, c + 1)
                for j in range(CHUNK_BLOCKS):
                    ins = nc.tensor.transpose(bank[0][:, j * P:(j + 1) * P], flat(x2[:, j]), ident[:])
                ins.then_inc(mT_done, 1)
                pe.wait_ge(mT_ready, c + 1)
                for j in range(CHUNK_BLOCKS):
                    xs = xT_hl[:, j * P:(j + 1) * P]
                    at = slice(j * EXPERTS1, (j + 1) * EXPERTS1)
                    mm(bank[1][:, at], xs, r_wh[:], start=(j == 0), stop=False, skip_group_check=True)
                    ins = mm(bank[1][:, at], xs, r_wl[:], start=False, stop=True, skip_group_check=True)
                ins.then_inc(r_done, 1)

                def second(e):
                    pe.wait_ge(h1_ready, c * EXPERTS1 + (e + 1))
                    for j in range(CHUNK_BLOCKS):
                        ins = mm(bank[4 + j][:, e * D:(e + 1) * D], hid[:, e % 2, j * P:(j + 1) * P],
                                 e2_w[:, e], start=(e == 0), stop=True, skip_group_check=True)
                    return ins

                for e in range(EXPERTS1):
                    if e >= 2:
                        pe.wait_ge(h1_ready, c * EXPERTS1 + (e - 1))
                    mm(bank[2 + e % 2][:], e1_wh[:, e * HID1:(e + 1) * HID1], xT_hl[:], start=True, stop=False)
                    mm(bank[2 + e % 2][:], e1_wl[:, e * HID1:(e + 1) * HID1], xT_hl[:], start=False,
                       stop=True).then_inc(h1_done, 1)
                    if e >= 1:
                        second(e - 1)
                second(EXPERTS1 - 1).then_inc(y2_done, 1)

        @block.scalar
        def _(act):
            def hidden(k):
                nc.scalar.activation(h0_sb[0:V, k % 2, :], h0_ps[k % 2][0:V, :],
                                     ACT.Relu).then_inc(h0_ready, 1)

            def batch(b, first, last):
                for k in range(UNITS):
                    u = b * UNITS + k
                    if not (last and k == UNITS - 1):
                        act.wait_ge(l0_done, u + 2)
                        if not (first and k == 0):
                            act.wait_ge(amix_done, u)
                        hidden((k + 1) % UNITS)
                    act.wait_ge(amix_done, u + 1)
                    if not (first and k < 2):
                        act.wait_ge(z_done, u - 1)
                    nc.scalar.activation(ah_sb[:, k % 2, :], ah_ps[k % 2][:, 0:UNIT * V],
                                         ACT.Copy).then_inc(ah_ready, 1)

            act.wait_ge(h0_zeroed, 1)
            act.wait_ge(l0_done, 1)
            hidden(0)
            batch(0, True, False)
            with act.Fori(1, BATCHES - 1) as b:
                batch(b, False, False)
            batch(BATCHES - 1, False, True)

            go = nc.scalar.activation
            with act.Fori(0, CHUNKS) as c:
                act.wait_ge(att_h_done, c + 1)
                go(hT[:], bank[0][0:D, :], ACT.Identity, bias=bn_bias[0:D, 2:3]).then_inc(att_hT_ready, 1)
                act.wait_ge(att_qkv_done, c * 2 + 1)
                go(qT[:], bank[2][0:D, :], ACT.Identity, bias=cols64[0:D, 5:6]).then_inc(att_qk_ready, 1)
                go(kT[:], bank[3][0:D, :], ACT.Identity, bias=cols64[0:D, 6:7]).then_inc(att_qk_ready, 1)
                act.wait_ge(att_qkv_done, c * 2 + 2)
                go(flat(v_sb[:]), bank[4][0:SEQ, :], ACT.Copy).then_inc(att_v_ready, 1)
                act.wait_ge(att_d_ready, c + 1)
                go(sc_e[:], sc[:], ACT.Exp, scale=D ** -0.5).then_inc(att_e_ready, 1)
                act.wait_ge(att_eT_done, c + 1)
                go(flat(eT[:]), bank[6][0:SEQ, :], ACT.Copy).then_inc(att_eT_ready, 1)

            def twice(c, layer, ready):
                act.wait_ge(hN_ready, c + (layer * CHUNKS + 1))
                go(x2[:], hN_chunk(c).unsqueeze(2).to_broadcast([P, CHUNK_BLOCKS, 2, D]),
                   ACT.Copy).then_inc(ready, 1)

            with act.Fori(0, CHUNKS) as c:
                twice(c, 0, x2_ready)
                act.wait_ge(xT_done, c + 1)
                go(xT2[:], bank[0][:], ACT.Copy).then_inc(xT_ready, 1)
                act.wait_ge(lg_d_ready, c + 1)
                go(sc_e[:], sc[:], ACT.Exp).then_inc(lg_e_ready, 1)
                act.wait_ge(lat_done, (c + 1) * (EXPERTS0 // 2))
                go(latT[:], bank[5][0:D, :], ACT.Copy).then_inc(latT_ready, 1)

            def att2_exp(c, j):
                act.wait_ge(att2_dr_ready, c * CHUNK_BLOCKS + (j + 1))
                go(p_sc[:, j % 2], p_sc[:, j % 2], ACT.Exp).then_inc(att2_e_ready, 1)

            def att2_copy(c, j):
                act.wait_ge(pT_done, c * CHUNK_BLOCKS + (j + 1))
                if j >= 2:
                    act.wait_ge(att2_o_done, c * CHUNK_BLOCKS + (j - 1))
                half = PAIRS * P // 2
                order(go(pT[:, j % 2, 0:half], bank[6][:], ACT.Copy))
                go(pT[:, j % 2, half:], bank[7][:], ACT.Copy).then_inc(pT_ready, 1)

            order = Chain(act, act_order)
            with act.Fori(0, CHUNKS) as c:
                order.enter(c, CHUNK_BLOCKS)
                twice(c, 1, gx2_ready)
                for p in range(PAIRS):
                    act.wait_ge(q_done, c * 2 * PAIRS + (2 * p + 1))
                    go(q_sq[:, p % 2], bank[1][:], ACT.Square).then_inc(q_sq_ready, 1)
                for b2 in range(CB):
                    act.wait_ge(vw_done, c * CB + (b2 + 1))
                    go(vw[:, b2], bank[1 + b2 % 2][:], ACT.Copy).then_inc(vw_ready, 1)
                att2_exp(c, 0)
                for j in range(CHUNK_BLOCKS):
                    if j + 1 < CHUNK_BLOCKS:
                        att2_exp(c, j + 1)
                    att2_copy(c, j)
            order.leave(CHUNKS)

            with act.Fori(0, CHUNKS) as c:
                act.wait_ge(r_d_ready, c + 1)
                go(sc_e[:, :, 0:EXPERTS1], sc[:, :, 0:EXPERTS1], ACT.Exp).then_inc(r_e_ready, 1)
                for e in range(EXPERTS1):
                    act.wait_ge(h1_done, c * EXPERTS1 + (e + 1))
                    go(hid[:, e % 2], bank[2 + e % 2][:], ACT.Gelu,
                       bias=e1_b[:, e:e + 1]).then_inc(h1_ready, 1)

        @block.vector
        def _(dve):
            vec = nc.vector
            order = Chain(dve, dve_order)
            dve.wait_ge(consts_in, 16 * len(CONSTS))
            order(vec.memset(bn_tmp[:], 1.0))
            order(vec.memset(bn_bias[:], 0.0))
            order.wait()
            order(vec.tensor_scalar(bn_tmp[:, 0:2], cols[:, 4:10:5], EPS_BN, None, ALU.add))
            order.wait()
            vec.tensor_scalar(bn_tmp[0:D, 2:3], cols64[0:D, 4:5], EPS_BN, None,
                              ALU.add).then_inc(bn_var, 1)
            dve.wait_ge(bn_rsqrt, 1)
            order(vec.tensor_tensor(bn_scale[:, 0:2], bn_scale[:, 0:2], cols[:, 1:7:5], ALU.mult))
            order(vec.tensor_tensor(bn_scale[0:D, 2:3], bn_scale[0:D, 2:3], cols64[0:D, 1:2], ALU.mult))
            order(vec.tensor_tensor(bn_bias[:, 0:2], cols[:, 0:6:5], cols[:, 3:9:5], ALU.subtract))
            order(vec.tensor_tensor(bn_bias[0:D, 2:3], cols64[0:D, 0:1], cols64[0:D, 3:4], ALU.subtract))
            order.wait()
            order(vec.tensor_tensor(bn_bias[:, 0:3], bn_bias[:, 0:3], bn_scale[:, 0:3], ALU.mult))
            order.wait()
            order(vec.tensor_tensor(bn_bias[:, 0:2], bn_bias[:, 0:2], cols[:, 2:8:5], ALU.add))
            order(vec.tensor_tensor(bn_bias[0:D, 2:3], bn_bias[0:D, 2:3], cols64[0:D, 2:3], ALU.add))
            order.wait()
            order(vec.tensor_scalar(neg_b1[:], bn_bias[:, 1:2], -1.0, None, ALU.mult))
            for n, col in enumerate((bn_scale[:, 0:1], bn_bias[:, 0:1], bn_scale[:, 1:2])):
                order(vec.tensor_scalar(diag[:, n], ident[:], col, None, ALU.mult))
            order(vec.tensor_scalar(diag[:, 3], ident[:], bn_scale[:, 2:3], None, ALU.mult))
            order.wait()
            vec.tensor_scalar(diag[:, 4], ident[:], bn_bias[:, 2:3], None,
                              ALU.mult).then_inc(diag_ready, 1)
            dve.wait_ge(rows_done, 1)
            order(vec.tensor_copy(rows_b[:, 0:4].rearrange("p a b -> p (a b)"), mix_ps[:, 0:512]))
            order(vec.tensor_copy(rows_b[:, 4], z_ps[0][:, 0:P]))
            dve.wait_ge(abar_done, 1)
            order(vec.tensor_scalar(abar[:], y_ps[:, 0:V], NODES_INV, None, ALU.mult))
            order.wait()
            order(vec.tensor_reduce(a_sum[:], abar[:], AX_X, ALU.add))
            order(vec.tensor_tensor(w1_s[:], w1_raw[:], rows_b[:, 2], ALU.mult))
            order(vec.tensor_tensor(w2_s[:], w2_raw[:], rows_b[:, 3, 0:D], ALU.mult))
            per_token = "p (j c) -> p j c"
            order(vec.tensor_tensor(
                w0_tmp.rearrange(per_token, j=GROUP), w0_raw.rearrange(per_token, j=GROUP),
                rows_b[:, 0:1, :].to_broadcast([P, GROUP, CH]), ALU.mult))
            order.wait()
            order(vec.tensor_tensor(s_corr[:], a_sum[:], bn_bias[:, 1:2], ALU.mult))
            order(vec.scalar_tensor_tensor(
                w0_tmp.rearrange(per_token, j=GROUP),
                rows_b[:, 1:2, :].to_broadcast([P, GROUP, CH]), cols[:, 10:11],
                w0_tmp.rearrange(per_token, j=GROUP), ALU.mult, ALU.add))
            order.wait()
            order(vec.tensor_copy(w0_hl[:], w0_tmp))
            order.wait()
            order(vec.tensor_tensor(w0_hl[32:64], w0_tmp[32:64], w0_hl[32:64].bitcast(F32),
                                    ALU.subtract))
            order.wait()
            vec.tensor_tensor(w0_hl[96:128], w0_tmp[96:128], w0_hl[96:128].bitcast(F32),
                              ALU.subtract).then_inc(weights_ready, 1)

            abar_u = abar[:].unsqueeze(1).to_broadcast([CH, UNIT, V])

            def y_split(b, par):
                dve.wait_ge(y_done, b * 2 + (par + 1))
                flat = y_hl[:, par].rearrange("p g v -> p (g v)")
                vec.tensor_scalar(flat, y_ps[:, 0:ITER // GROUP * V], cols[:, 10:11],
                                  None, ALU.add).then_inc(y_high, 1)
                dve.wait_ge(y_high, b * 2 + (par + 1))
                vec.tensor_tensor(flat[64:128], y_ps[64:128, 0:ITER // GROUP * V],
                                  flat[64:128].bitcast(F32), ALU.subtract).then_inc(y_ready, 1)

            def node_sum(b, k, first):
                slot = (k // 4) % 2
                dve.wait_ge(z_done, b * UNITS + (k + 1))
                if k % 4 == 0 and not (first and k < 8):
                    dve.wait_ge(s_ready, b * 4 + (k // 4 - 1))
                vec.scalar_tensor_tensor(
                    prod[:, slot, k % 4].rearrange("p (j v) -> p j v", v=V),
                    z_ps[k % 2][:, 0:UNIT * V].rearrange("p (j v) -> p j v", v=V), neg_b1[:, 0:1],
                    abar_u, ALU.max, ALU.mult).then_inc(prod_done, 1)
                if k % 4 == 3:
                    dve.wait_ge(prod_done, b * UNITS + (k + 1))
                    vec.tensor_reduce(
                        sT[:, bass.ds(b * SEQ + 4 * (k - 3), 16)],
                        prod[:, slot].rearrange("p q (j v) -> p (q j) v", v=V),
                        AX_X, ALU.add).then_inc(s_ready, 1)

            def batch(b, first, last):
                for k in range(UNITS):
                    if k > 0:
                        node_sum(b, k - 1, first)
                    elif not first:
                        node_sum(b - 1, UNITS - 1, False)
                    if k == 3:
                        y_split(b, 1)
                    if k == 11 and not last:
                        y_split(b + 1, 0)

            y_split(0, 0)
            batch(0, True, False)
            with dve.Fori(1, BATCHES - 1) as b:
                batch(b, False, False)
            batch(BATCHES - 1, False, True)
            node_sum(BATCHES - 1, UNITS - 1, False)

            tt, stt, ts = vec.tensor_tensor, vec.scalar_tensor_tensor, vec.tensor_scalar
            ln = Tally()

            def normalize(src, dst, after=None):
                n = ln.next()
                order.wait()
                order(vec.tensor_reduce(ln_mean[:], src, AX_X, ALU.add))
                order.wait()
                order(ts(ln_mean[:], ln_mean[:], -1.0 / D, None, ALU.mult))
                order.wait()
                order(tt(xc[:], src, per_block(ln_mean[:]), ALU.add))
                order.wait()
                order(tt(xsq[:], xc[:], xc[:], ALU.mult))
                order.wait()
                order(vec.tensor_reduce(ln_var[:], xsq[:], AX_X, ALU.add))
                order.wait()
                ts(ln_var[:], ln_var[:], 1.0 / D, EPS_LN, ALU.mult, ALU.add).then_inc(ln_var_ready, 1)
                dve.wait_ge(ln_rstd_ready, n)
                ins = tt(dst, xc[:], per_block(ln_rstd[:]), ALU.mult)
                if after is None:
                    order(ins)
                else:
                    ins.then_inc(after, 1)

            def layer(body, per_trip, norms_per_trip, index):
                with dve.Fori(0, CHUNKS) as c:
                    order.enter(c, per_trip)
                    ln.enter(c, norms_per_trip)
                    body(c)
                order.leave(CHUNKS)
                ln.leave(CHUNKS)
                dve.wait_ge(hN_ready, (index + 1) * CHUNKS)

            def attention(c):
                ts(s_chunk[:], sT[:, bass.ds(c * CT, CT)], s_corr[:, 0:1], None, ALU.add).then_inc(sT_copied, 1)
                dve.wait_ge(att_h_done, c + 1)
                order(tt(x_tok[:], bank[1][:, 0:CHUNK_BLOCKS * D].rearrange("p (j d) -> p j d", d=D),
                         per_block(rows_b[:, 4, 0:D]), ALU.add))
                dve.wait_ge(att_s_done, c + 1)
                scores = bank[5][:, 0:CHUNK_BLOCKS * SEQ].rearrange("p (j s) -> p j s", s=SEQ)
                order(vec.tensor_reduce(row_max[:], scores, AX_X, ALU.max))
                order.wait()
                tt(sc[:], scores, per_block(row_max[:]), ALU.subtract).then_inc(att_d_ready, 1)
                dve.wait_ge(att_e_ready, c + 1)
                order(vec.tensor_reduce(row_sum[:], sc_e[:], AX_X, ALU.add))
                order.wait()
                order(vec.reciprocal(row_inv[:], row_sum[:]))
                order(tt(x_tok[:], x_tok[:], per_block(row("bv")), ALU.add))
                order.wait()
                dve.wait_ge(att_o_done, c + 1)
                order(tt(res[:], bank[7][:, 0:CHUNK_BLOCKS * D].rearrange("p (j d) -> p j d", d=D),
                         per_block(row_inv[:]), ALU.mult))
                order.wait()
                order(tt(res[:], res[:], x_tok[:], ALU.add))
                normalize(res[:], hN_chunk(c), hN_ready)

            dve.wait_ge(later_in, LATER_IN)
            dve.wait_ge(s_ready, BATCHES * 4)
            layer(attention, N_ATT, 1, 0)

            def split_xT(done, ready, c):
                dve.wait_ge(done, c + 1)
                order(vec.tensor_copy(xT_hl[:], bank[0][:]))
                order.wait()
                tt(xT_hl[D:P], bank[0][D:P, :], xT_hl[D:P].bitcast(F32), ALU.subtract).then_inc(ready, 1)

            def lattice(c):
                dve.wait_ge(lg_done, c + 1)
                order(vec.tensor_copy(lg[:], bank[1][:, 0:CHUNK_BLOCKS * EXPERTS0].rearrange(
                    "p (j e) -> p j e", e=EXPERTS0)))
                order.wait()
                order(vec.tensor_reduce(top_max[:], lg[:], AX_X, ALU.max))
                for j in range(CHUNK_BLOCKS):
                    order(vec.max(top[:, j], lg[:, j]))
                order.wait()
                order(vec.memset(top[:, :, TOP0:8], BIG))
                order.wait()
                tt(sc[:], lg[:], per_block(top_max[:]), ALU.subtract).then_inc(lg_d_ready, 1)
                for j in range(CHUNK_BLOCKS):
                    order(vec.match_replace(left[:, j], top[:, j], lg[:, j], -BIG))
                order.wait()
                order(tt(left[:], left[:], lg[:], ALU.not_equal))
                order.wait()
                dve.wait_ge(lg_e_ready, c + 1)
                order(tt(left[:], left[:], sc_e[:], ALU.mult))
                order.wait()
                order(vec.tensor_reduce(row_sum[:], left[:], AX_X, ALU.add))
                order.wait()
                order(vec.reciprocal(row_inv[:], row_sum[:]))
                order.wait()
                order(tt(w2x[:, :, 0], left[:], per_block(row_inv[:]), ALU.mult))
                tt(w2x[:, :, 1], left[:], per_block(row_inv[:]), ALU.mult).then_inc(w2_ready, 1)
                dve.wait_ge(wT_done, c + 1)
                order(vec.tensor_copy(wT_hl[:], bank[2][:]))
                order.wait()
                tt(wT_hl[D:P], bank[2][D:P, :], wT_hl[D:P].bitcast(F32), ALU.subtract).then_inc(wT_ready, 1)
                dve.wait_ge(xT_ready, c + 1)
                for p in range(EXPERTS0 // 2):
                    n = c * (EXPERTS0 // 2) + (p + 1)
                    dve.wait_ge(bc_done, n)
                    if p >= 2:
                        dve.wait_ge(lat_done, c * (EXPERTS0 // 2) + (p - 1))
                    tt(zT[:, p % 2], bank[3 + p % 2][:], xT2[:], ALU.mult).then_inc(z_ready, 1)
                dve.wait_ge(proj_done, c + 1)
                order(tt(res[:], bank[6][:, 0:CHUNK_BLOCKS * D].rearrange("p (j d) -> p j d", d=D),
                         per_block(row("out_b")), ALU.add))
                order.wait()
                order(tt(res[:], res[:], hN_chunk(c), ALU.add))
                normalize(res[:], res[:])
                order.wait()
                order(tt(res[:], res[:], per_block(row("ln_g")), ALU.mult))
                order.wait()
                order(tt(res[:], res[:], per_block(row("ln_b")), ALU.add))
                order.wait()
                order(tt(res[:], res[:], hN_chunk(c), ALU.add))
                normalize(res[:], hN_chunk(c), hN_ready)

            layer(lattice, N_LAT, 2, 1)

            def tok_trig(n):
                return trig_t[:, n].unsqueeze(1).to_broadcast([P, CHUNK_BLOCKS, D])

            def feat_trig(n):
                return trig_f[:, n].unsqueeze(1).to_broadcast([P, CB, SEQ])

            def by_batch(ap):
                return ap.rearrange("p (b s) -> p b s", s=SEQ)

            def scores_max(c, j):
                dve.wait_ge(att2_s_done, c * CHUNK_BLOCKS + (j + 1))
                for half in range(2):
                    order(vec.tensor_reduce(
                        p_max[:, j % 2, half * PAIRS:(half + 1) * PAIRS],
                        bank[4 + half][:].rearrange("p (h s) -> p h s", s=SEQ), AX_X, ALU.max))
                order.wait()
                if j >= 2:
                    dve.wait_ge(pT_done, c * CHUNK_BLOCKS + (j - 1))
                for half in range(2):
                    ins = tt(p_sc[:, j % 2, half * CT:(half + 1) * CT].rearrange("p (h s) -> p h s", s=SEQ),
                             bank[4 + half][:].rearrange("p (h s) -> p h s", s=SEQ),
                             p_max[:, j % 2, half * PAIRS:(half + 1) * PAIRS].unsqueeze(2).to_broadcast(
                                 [P, PAIRS, SEQ]), ALU.subtract)
                    if half == 0:
                        order(ins)
                ins.then_inc(att2_d_ready, 1)

            def weights(c, j):
                dve.wait_ge(att2_e_ready, c * CHUNK_BLOCKS + (j + 1))
                view = p_sc[:, j % 2].rearrange("p (h s) -> p h s", s=SEQ)
                order(vec.tensor_reduce(p_sum[:, j % 2], view, AX_X, ALU.add))
                order.wait()
                order(vec.reciprocal(p_inv[:, j % 2], p_sum[:, j % 2]))
                order.wait()
                tt(view, view, p_inv[:, j % 2].unsqueeze(2).to_broadcast([P, HEADS, SEQ]),
                   ALU.mult).then_inc(att2_p_ready, 1)

            def rotary(c):
                split_xT(gxT_done, gxT_ready, c)
                dve.wait_ge(kn_done, c + 1)
                kk = bank[3][:].rearrange("p (j s d) -> p j s d", s=2, d=D)
                order(tt(k_t[:], kk[:, :, 0], tok_trig(0), ALU.mult))
                order(tt(k_s[:], kk[:, :, 1], tok_trig(1), ALU.mult))
                order.wait()
                order(tt(k_t[:], k_t[:], k_s[:], ALU.add))
                order.wait()
                order(tt(k_s[:], k_t[:], k_t[:], ALU.mult))
                order.wait()
                order(vec.tensor_reduce(k_var[:], k_s[:], AX_X, ALU.add))
                order.wait()
                ts(k_var[:], k_var[:], 1.0 / D, EPS_RMS, ALU.mult, ALU.add).then_inc(k_rms_in, 1)
                dve.wait_ge(vT_done, c + 1)
                order(vec.tensor_copy(v_bd[0:D, :, 0], by_batch(bank[0][0:D, :])))
                vec.tensor_copy(v_bd[D:P, :, 1], by_batch(bank[0][D:P, :])).then_inc(vbd_ready, 1)
                order(tt(k_t[:], k_t[:], per_block(qk_gain[:]), ALU.mult))
                order.wait()
                dve.wait_ge(k_rms_out, c + 1)
                order(tt(x2[:, :, 0], k_t[:], per_block(k_rms[:]), ALU.mult))
                tt(x2[:, :, 1], k_t[:], per_block(k_rms[:]), ALU.mult).then_inc(k2_ready, 1)
                for p in range(PAIRS):
                    n = c * 2 * PAIRS + 2 * p
                    dve.wait_ge(q_sq_ready, c * PAIRS + (p + 1))
                    if p >= 2:
                        dve.wait_ge(q_sum_ready, c * PAIRS + (p - 1))
                    tt(by_batch(rope_c[:, p % 2]), by_batch(bank[1][:]), feat_trig(0),
                       ALU.mult).then_inc(q_rope_ready, 1)
                    dve.wait_ge(q_done, n + 2)
                    tt(by_batch(rope_s[:, p % 2]), by_batch(bank[2][:]), feat_trig(1),
                       ALU.mult).then_inc(q_rope_ready, 1)
                    dve.wait_ge(q_rope_ready, n + 2)
                    tt(qr[:, p * CT:(p + 1) * CT], rope_c[:, p % 2], rope_s[:, p % 2],
                       ALU.add).then_inc(q_sum_ready, 1)
                dve.wait_ge(norm_done, c + 1)
                ts(q_var[:], bank[7][:, 0:CHUNK_BLOCKS * HEADS], 1.0 / D, EPS_RMS, ALU.mult,
                   ALU.add).then_inc(q_rms_in, 1)
                dve.wait_ge(kT_done, c + 1)
                order(vec.tensor_copy(k_bd[0:D, :, 0], by_batch(bank[0][0:D, :])))
                vec.tensor_copy(k_bd[D:P, :, 1], by_batch(bank[0][D:P, :])).then_inc(kbd_ready, 1)
                scores_max(c, 0)
                for j in range(CHUNK_BLOCKS):
                    if j + 1 < CHUNK_BLOCKS:
                        scores_max(c, j + 1)
                    weights(c, j)
                dve.wait_ge(att2_o_done, (c + 1) * CHUNK_BLOCKS)
                order(tt(res[:], bank[0][:, 0:CHUNK_BLOCKS * D].rearrange("p (j d) -> p j d", d=D),
                         hN_chunk(c), ALU.add))
                normalize(res[:], hN_chunk(c), hN_ready)

            order(vec.memset(k_bd, 0.0))
            order(vec.memset(v_bd, 0.0))
            order.wait()
            layer(rotary, N_ROT, 1, 2)

            def gelu(c):
                normalize(hN_chunk(c), res[:])
                order.wait()
                order(tt(res[:], res[:], per_block(row("gamma")), ALU.mult))
                order.wait()
                order(tt(x2[:, :, 0], res[:], per_block(row("beta")), ALU.add))
                tt(x2[:, :, 1], res[:], per_block(row("beta")), ALU.add).then_inc(m2_ready, 1)
                split_xT(mT_done, mT_ready, c)
                dve.wait_ge(r_done, c + 1)
                rl = lg[:, :, 0:EXPERTS1]
                order(tt(rl, bank[1][:, 0:CHUNK_BLOCKS * EXPERTS1].rearrange("p (j e) -> p j e", e=EXPERTS1),
                         per_block(row("br", EXPERTS1), EXPERTS1), ALU.add))
                order.wait()
                order(vec.tensor_reduce(top_max[:], rl, AX_X, ALU.max))
                for j in range(CHUNK_BLOCKS):
                    order(vec.max(top[:, j], rl[:, j]))
                order.wait()
                order(vec.memset(top[:, :, 2:8], BIG))
                order.wait()
                tt(sc[:, :, 0:EXPERTS1], rl, per_block(top_max[:], EXPERTS1), ALU.subtract).then_inc(r_d_ready, 1)
                sel = left[:, :, 0:EXPERTS1]
                for j in range(CHUNK_BLOCKS):
                    order(vec.match_replace(sel[:, j], top[:, j], rl[:, j], -BIG))
                order.wait()
                order(tt(sel, sel, rl, ALU.not_equal))
                order.wait()
                dve.wait_ge(r_e_ready, c + 1)
                order(tt(sel, sel, sc_e[:, :, 0:EXPERTS1], ALU.mult))
                order.wait()
                order(vec.tensor_reduce(row_sum[:], sel, AX_X, ALU.add))
                order.wait()
                order(vec.reciprocal(row_inv[:], row_sum[:]))
                order.wait()
                order(tt(wf[:], sel, per_block(row_inv[:], EXPERTS1), ALU.mult))
                order.wait()
                dve.wait_ge(y2_done, c + 1)
                for j in range(CHUNK_BLOCKS):
                    m = moe[:, j % 2].rearrange("p (e d) -> p e d", d=D)
                    order(tt(moe[:, j % 2], bank[4 + j][:], row("b2", EXPERTS1 * D), ALU.add))
                    order.wait()
                    order(tt(m, m, wf[:, j].unsqueeze(2).to_broadcast([P, EXPERTS1, D]), ALU.mult))
                    order.wait()
                    order(vec.tensor_reduce(res[:, j], moe[:, j % 2].rearrange("p (e d) -> p d e", d=D),
                                            AX_X, ALU.add))
                order.wait()
                order(tt(res[:], res[:], hN_chunk(c), ALU.add))
                normalize(res[:], hN_chunk(c), hN_ready)

            layer(gelu, N_GELU, 2, 3)



def _layout(inputs):
    import numpy as np
    f = {k: np.asarray(v) for k, v in inputs.items()}
    a = {}
    a["x"] = f["x"].reshape(TOKENS, V, C0).transpose(1, 0, 2).reshape(V, TOKENS * C0)
    a["ident"] = np.eye(P, dtype=np.float32)
    cols = np.zeros((P, 16), np.float32)
    for layer in range(2):
        for n, name in enumerate(("b", "g", "be", "m", "v")):
            cols[:, 5 * layer + n] = f[f"L0_tok_{name}{layer}"]
    cols[BIAS_ROW, 10] = cols[ROWS + BIAS_ROW, 10] = 1.0
    a["cols"] = cols
    cols64 = np.zeros((P, 8), np.float32)
    for n, name in enumerate(("b", "g", "be", "m", "v")):
        cols64[0:D, n] = f[f"L0_tok_{name}2"]
    cols64[0:D, 5], cols64[0:D, 6] = f["L0_attn_bq"], f["L0_attn_bk"]
    a["cols64"] = cols64
    a["A"] = f["L0_tok_A"]
    a["AT"] = np.zeros((P, V), np.float32)
    a["AT"][0:V] = f["L0_tok_A"].T
    w0 = np.zeros((P // ROWS, ROWS, GROUP, CH), np.float32)
    for j in range(GROUP):
        w0[:, C0 * j:C0 * (j + 1), j] = f["L0_tok_W0"]
    a["w0_blocks"] = w0.reshape(P, GROUP * CH)
    a["W1"], a["W2"] = f["L0_tok_W1"], f["L0_tok_W2"]
    rowv = np.concatenate([f["L0_attn_bv"], f["L0_ffn_out_b"], f["L0_ffn_ln_g"], f["L0_ffn_ln_b"],
                           f["L1_attn_q_norm_w"], f["L1_attn_k_norm_w"], f["L1_ffn_gamma"],
                           f["L1_ffn_beta"], f["L1_ffn_b2"].reshape(-1), f["L1_ffn_br"]])
    a["rows"] = rowv.reshape(ROW_WIDTH)
    a["att_w"] = np.concatenate([f["L0_attn_Wq"], f["L0_attn_Wk"], f["L0_attn_Wv"]], 1)
    a["gate_wT"] = f["L0_ffn_gate_w"].T
    a["lat_w"] = f["L0_ffn_lattice_weights"].reshape(EXPERTS0 // 2, 2 * D, D).transpose(1, 0, 2)
    a["out_wT"] = f["L0_ffn_out_w"].T
    a["ident2"] = np.concatenate([np.eye(D, dtype=np.float32)] * 2, 0)
    swap = np.arange(D).reshape(D // 2, 2)[:, ::-1].reshape(-1)
    wqT = f["L1_attn_wq"].T.reshape(D, HEADS, D)
    q_w = np.stack([wqT.reshape(D, -1), wqT[:, :, swap].reshape(D, -1)], 1)
    a["q_w"] = np.concatenate([q_w, q_w], 0)
    wkT, wvT = f["L1_attn_wkv"][0:D].T, f["L1_attn_wkv"][D:].T
    kv = np.concatenate([wkT, wkT[:, swap], wvT, wvT], 1)
    a["kv_w"] = np.concatenate([kv, kv], 0)
    a["wo_w"] = f["L1_attn_wo"].reshape(D, PAIRS, 2, D).transpose(2, 3, 1, 0).reshape(P, PAIRS, D)
    freqs = np.float32(10000.0) ** (np.float32(-2.0) * np.arange(D // 2, dtype=np.float32) / np.float32(D))
    theta = np.arange(SEQ, dtype=np.float32)[:, None] * freqs[None, :].astype(np.float32)
    cos = np.repeat(np.cos(theta), 2, axis=1).astype(np.float32)
    sin = np.repeat(np.sin(theta), 2, axis=1).astype(np.float32)
    sin[:, 0::2] *= -1
    a["trig_f"] = np.concatenate([np.stack([cos.T, sin.T], 1)] * 2, 0)
    a["trig_t"] = np.concatenate([np.stack([cos, sin], 1)] * 2, 0)
    head_of = np.zeros((P, 2), np.float32)
    head_of[0:D, 0] = head_of[D:P, 1] = 1.0
    a["head_of"] = head_of
    above = np.where(np.arange(SEQ)[None, :] > np.arange(SEQ)[:, None], MASKED, 0.0).astype(np.float32)
    a["mask"] = np.tile(above, (2, CT // SEQ))
    twice = lambda m: np.concatenate([m, m], 0)
    a["r_w"] = twice(f["L1_ffn_Wr"])
    a["e1_w"] = twice(f["L1_ffn_W1"].transpose(1, 0, 2).reshape(D, EXPERTS1 * HID1))
    a["e1_b"] = f["L1_ffn_b1"].T
    a["e2_w"] = f["L1_ffn_W2"].transpose(1, 0, 2)
    return {k: np.ascontiguousarray(v) for k, v in a.items()}

def kernel(**inputs):
    import numpy as _np
    import concourse.bacc as _bacc
    from concourse import mybir as _mybir
    from concourse.bass_utils import run_bass_kernel_spmd as _run

    nc = _bacc.Bacc("TRN2", target_bir_lowering=False, num_devices=1)
    arrays, args = {}, {}
    for name, a in _layout(inputs).items():
        arrays[f"in_{name}_dram"] = a
        args[name] = nc.dram_tensor(f"in_{name}_dram", a.shape, _mybir.dt.from_np(a.dtype),
                                    kind="ExternalInput").ap()
    args["out"] = nc.dram_tensor("out_0_dram", (P, BLOCKS, D), _mybir.dt.float32,
                                 kind="ExternalOutput").ap()
    build(nc, args)
    r = _run(nc, [arrays], core_ids=[0])
    got = _np.asarray(r.results[0]["out_0_dram"])
    return got.transpose(1, 0, 2).reshape(BATCHES, SEQ, D)
```

```python
from contextlib import ExitStack

import concourse.bass as bass
from concourse import mybir

F32 = mybir.dt.float32
F32R = mybir.dt.float32r
BF16 = mybir.dt.bfloat16
ALU = mybir.AluOpType
ACT = mybir.ActivationFunctionType
AX_X = mybir.AxisListType.X

P = 128
BATCHES = 64
SEQ = 64
TOKENS = BATCHES * SEQ
V = 75
C0 = 3
CH = 128
D = 64
EPS_BN = 1e-5

NODES_INV = 1.0 / V
EPS_LN = 1e-5
EPS_RMS = 1.1920929e-07
CHUNK_BLOCKS = 4
BLOCKS = TOKENS // P
CHUNKS = BLOCKS // CHUNK_BLOCKS
CT = CHUNK_BLOCKS * P
CB = CT // SEQ
EXPERTS0 = 64
TOP0 = 6
HEADS = 16
PAIRS = HEADS // 2
EXPERTS1 = 8
HID1 = 128
BIG = 3.0e38
MASKED = -1.0e30

UNIT = 4
GROUP = 8
ITER = 32
UNITS = SEQ // UNIT
ROWS = 32
BIAS_ROW = GROUP * C0


N_ATT, N_LAT, N_ROT, N_GELU = 12, 66, 56, 76

class Chain:

    def __init__(self, eng, sem):
        self.eng, self.sem, self.base, self.trip, self.k = eng, sem, 0, 0, 0

    def enter(self, i, per_trip):
        self.base, self.trip, self.k, self.per = self.base + self.k, i * per_trip, 0, per_trip

    def leave(self, trips):
        assert self.k == self.per, (self.k, self.per)
        self.base, self.trip, self.k = self.base + trips * self.per, 0, 0

    def __call__(self, ins):
        ins.then_inc(self.sem, 1)
        self.k += 1
        return self.trip + (self.base + self.k)

    def wait(self, mark=None):
        self.eng.wait_ge(self.sem, self.trip + (self.base + self.k) if mark is None else mark)


ROW_NAMES = ("bv", "out_b", "ln_g", "ln_b", "q_norm", "k_norm", "gamma", "beta")
ROW_AT = {name: n * D for n, name in enumerate(ROW_NAMES)}
ROW_AT["b2"] = len(ROW_NAMES) * D
ROW_AT["br"] = ROW_AT["b2"] + EXPERTS1 * D
ROW_WIDTH = ROW_AT["br"] + EXPERTS1


def build(nc, t):
    with ExitStack() as ctx:
        def sb(name, shape, dt=F32):
            return ctx.enter_context(nc.sbuf_tensor(name, shape, dt))

        def sem(name):
            return ctx.enter_context(nc.semaphore(name))

        bank = [ctx.enter_context(nc.psum_tensor(f"bank{i}", [P, 512], F32)) for i in range(8)]

        ident = sb("ident", [P, P])
        cols = sb("cols", [P, 16])
        cols64 = sb("cols64", [P, 8])
        AT = sb("AT", [P, V])
        A_nat = sb("A_nat", [V, V])
        ones = sb("ones", [P, P])
        w0_hl = sb("w0_hl", [P, GROUP * CH], F32R)
        w1_raw = sb("w1_raw", [CH, CH])
        w1_s = sb("w1_s", [CH, CH])
        w2_raw = sb("w2_raw", [CH, D])
        w2_s = sb("w2_s", [CH, D])
        half_neg = sb("half_neg", [P, 64])
        bn_scale = sb("bn_scale", [P, 4])
        bn_bias = sb("bn_bias", [P, 4])
        bn_tmp = sb("bn_tmp", [P, 4])
        neg_b1 = sb("neg_b1", [P, 1])
        diag = sb("diag", [P, 5, P])
        rows_b = sb("rows_b", [P, 5, P])
        abar = sb("abar", [P, V])
        a_sum = sb("a_sum", [P, 1])
        s_corr = sb("s_corr", [P, 1])

        x_t = sb("x_t", [V, 2, ITER * C0])
        x_rep = sb("x_rep", [V, 2, ITER // GROUP, P // ROWS, ROWS])
        y_hl = sb("y_hl", [P, 2, ITER // GROUP, V], F32R)
        h0_sb = sb("h0_sb", [P, 2, UNIT * CH])
        ah_sb = sb("ah_sb", [CH, 2, UNIT * V])
        prod_bd = sb("prod_bd", [P, 2 * 4 * UNIT * V])
        prod = prod_bd[:].rearrange("p (s q n) -> p s q n", s=2, q=4)
        sT = sb("sT", [CH, TOKENS])


        rows = sb("rows", [P, ROW_WIDTH])
        att_w = sb("att_w", [D, 3 * D])
        gate_wT = sb("gate_wT", [D, EXPERTS0])
        lat_w = sb("lat_w", [P, EXPERTS0 // 2, D])
        out_wT = sb("out_wT", [D, D])
        pick = sb("pick", [P, EXPERTS0, D], F32R)
        ident2 = sb("ident2", [P, D])
        q_wh = sb("q_wh", [P, 2, HEADS * D], F32R)
        q_wl = sb("q_wl", [P, 2, HEADS * D], F32R)
        kv_w = sb("kv_w", [P, 4 * D])
        kv_wh = sb("kv_wh", [P, 4 * D], F32R)
        kv_wl = sb("kv_wl", [P, 4 * D], F32R)
        wo_w = sb("wo_w", [P, PAIRS, D])
        trig_f = sb("trig_f", [P, 2, SEQ])
        trig_t = sb("trig_t", [P, 2, D])
        qk_gain = sb("qk_gain", [P, D])
        head_of = sb("head_of", [P, 2])
        ident_bf = sb("ident_bf", [P, P], BF16)
        mask_bf = sb("mask_bf", [P, CT], BF16)
        mask_in = sb("mask_in", [P, CT])
        r_w = sb("r_w", [P, EXPERTS1])
        r_wh = sb("r_wh", [P, EXPERTS1], F32R)
        r_wl = sb("r_wl", [P, EXPERTS1], F32R)
        e1_wh = sb("e1_wh", [P, EXPERTS1 * HID1], F32R)
        e1_wl = sb("e1_wl", [P, EXPERTS1 * HID1], F32R)
        e1_b = sb("e1_b", [P, EXPERTS1])
        e2_w = sb("e2_w", [P, EXPERTS1, D])

        hN = sb("hN", [P, BLOCKS, D])
        s_chunk = sb("s_chunk", [CH, CT])
        hT = sb("hT", [D, CT])
        x_tok = sb("x_tok", [P, CHUNK_BLOCKS, D])
        qT = sb("qT", [D, CT])
        kT = sb("kT", [D, CT])
        v_sb = sb("v_sb", [SEQ, CB, D])
        xc = sb("xc", [P, CHUNK_BLOCKS, D])
        xsq = sb("xsq", [P, CHUNK_BLOCKS, D])
        res = sb("res", [P, CHUNK_BLOCKS, D])
        ln_mean = sb("ln_mean", [P, CHUNK_BLOCKS])
        ln_var = sb("ln_var", [P, CHUNK_BLOCKS])
        ln_rstd = sb("ln_rstd", [P, CHUNK_BLOCKS])
        row_max = sb("row_max", [P, CHUNK_BLOCKS])
        row_sum = sb("row_sum", [P, CHUNK_BLOCKS])
        row_inv = sb("row_inv", [P, CHUNK_BLOCKS])
        sc = sb("sc", [P, CHUNK_BLOCKS, D])
        sc_e = sb("sc_e", [P, CHUNK_BLOCKS, D])
        eT = sb("eT", [SEQ, CHUNK_BLOCKS, P])
        x2 = sb("x2", [P, CHUNK_BLOCKS, 2, D])
        xT2 = sb("xT2", [P, CT])
        lg = sb("lg", [P, CHUNK_BLOCKS, EXPERTS0])
        top = sb("top", [P, CHUNK_BLOCKS, 8])
        top_max = sb("top_max", [P, CHUNK_BLOCKS])
        left = sb("left", [P, CHUNK_BLOCKS, EXPERTS0])
        w2x = sb("w2x", [P, CHUNK_BLOCKS, 2, EXPERTS0])
        wT_hl = sb("wT_hl", [P, CT], F32R)
        zT = sb("zT", [P, 2, CT])
        latT = sb("latT", [P, CT])
        xT_hl = sb("xT_hl", [P, CT], F32R)
        rope_c = zT
        rope_s = sb("rope_s", [P, 2, CT])
        q_sq = sb("q_sq", [P, 2, CT])
        qr = [[sT[:, p * CT:(p + 1) * CT] for p in range(PAIRS)],
              [h0_sb[:, 0], h0_sb[:, 1], s_chunk[:], ah_sb[:].rearrange("p s n -> p (s n)")[:, 0:CT],
               diag[:, 0:4].rearrange("p a b -> p (a b)"), rows_b[:, 0:4].rearrange("p a b -> p (a b)"),
               mask_in[:], latT[:]]]
        k_t = sb("k_t", [P, CHUNK_BLOCKS, D])
        k_s = sb("k_s", [P, CHUNK_BLOCKS, D])
        k_var = sb("k_var", [P, CHUNK_BLOCKS])
        k_rms = sb("k_rms", [P, CHUNK_BLOCKS])
        q_var = sb("q_var", [P, CHUNK_BLOCKS * HEADS])
        q_rms = sb("q_rms", [P, CHUNK_BLOCKS * HEADS])
        bd_store = [prod_bd[:, 0:4 * CT], lat_w[:].rearrange("p a d -> p (a d)")]
        k_bd = [m[:, 0:2 * CT].rearrange("p (b h s) -> p b h s", b=CB, h=2) for m in bd_store]
        v_bd = [m[:, 2 * CT:4 * CT].rearrange("p (b h s) -> p b h s", b=CB, h=2) for m in bd_store]
        vw = sb("vw", [P, CB, PAIRS * D])
        q_w = vw[:, 0:4, :].rearrange("p b n -> p (b n)").rearrange("p (s n) -> p s n", s=2)
        e1_w = vw[:, 4:6, :].rearrange("p b n -> p (b n)")
        p_max = sb("p_max", [P, 2, HEADS])
        p_sum = sb("p_sum", [P, 2, HEADS])
        p_inv = sb("p_inv", [P, 2, HEADS])
        p_sc = sb("p_sc", [P, 2, HEADS * SEQ])
        w0_tmp = p_sc[:, 0, :]
        pT = sb("pT", [P, 2, PAIRS * P])
        w0_raw = pT[:, 0, :]
        hid = rope_s
        wf = sb("wf", [P, 2, CHUNK_BLOCKS, EXPERTS1])
        mT_hl = [xT_hl, wT_hl]
        lat_x = [xT2[:], rope_s[:, 0]]
        lat_w_hl = [wT_hl, xT_hl]
        lat_z = [zT[:, 0], zT[:, 1], q_sq[:, 0], q_sq[:, 1]]
        spread_ps = [bank[2], bank[3], bank[4], bank[7]]
        lat_ps = [bank[5], bank[6]]
        moe = [q_sq[:, 0], q_sq[:, 1], zT[:, 0], zT[:, 1]]

        y_ps = bank[0]
        h0_ps = [bank[1], bank[2]]
        ah_ps = [bank[3], bank[4]]
        z_ps = [bank[5], bank[6]]
        mix_ps = bank[7]

        consts_in = sem("consts_in")
        x_in = [sem("x_in0"), sem("x_in1")]
        pool_order, dve_order, act_order = sem("pool_order"), sem("dve_order"), sem("act_order")
        pe_gate, pool_gate = sem("pe_gate"), sem("pool_gate")
        ones_set = sem("ones_set")
        bn_var = sem("bn_var")
        bn_rsqrt = sem("bn_rsqrt")
        diag_ready = sem("diag_ready")
        rows_done = sem("rows_done")
        abar_done = sem("abar_done")
        weights_ready = sem("weights_ready")
        h0_zeroed = sem("h0_zeroed")
        x_copied = sem("x_copied")
        y_done = sem("y_done")
        y_high = sem("y_high")
        y_ready = sem("y_ready")
        l0_done = sem("l0_done")
        h0_ready = sem("h0_ready")
        amix_done = sem("amix_done")
        ah_ready = sem("ah_ready")
        z_done = sem("z_done")
        prod_done = sem("prod_done")
        s_ready = sem("s_ready")
        out_sem = sem("out_sem")
        later_in = sem("later_in")
        pick_ready = sem("pick_ready")
        splits_ready = sem("splits_ready")
        sT_copied = sem("sT_copied")
        att_h_done = sem("att_h_done")
        att_hT_ready = sem("att_hT_ready")
        att_qkv_done = sem("att_qkv_done")
        att_qk_ready = sem("att_qk_ready")
        att_v_ready = sem("att_v_ready")
        att_s_done = sem("att_s_done")
        att_d_ready = sem("att_d_ready")
        att_e_ready = sem("att_e_ready")
        att_eT_done = sem("att_eT_done")
        att_eT_ready = sem("att_eT_ready")
        att_o_done = sem("att_o_done")
        ln_var_ready = sem("ln_var_ready")
        ln_rstd_ready = sem("ln_rstd_ready")
        hN_ready = sem("hN_ready")
        x2_ready = sem("x2_ready")
        xT_done = sem("xT_done")
        xT_ready = sem("xT_ready")
        lg_done = sem("lg_done")
        lg_d_ready = sem("lg_d_ready")
        lg_e_ready = sem("lg_e_ready")
        w2_ready = sem("w2_ready")
        wT_done = sem("wT_done")
        wT_ready = sem("wT_ready")
        bc_done = sem("bc_done")
        z_ready = sem("z_ready")
        lat_done = sem("lat_done")
        latT_ready = sem("latT_ready")
        proj_done = sem("proj_done")
        gx2_ready = sem("gx2_ready")
        gxT_done = sem("gxT_done")
        gxT_ready = sem("gxT_ready")
        kn_done = sem("kn_done")
        kn_read = sem("kn_read")
        bd_zeroed = sem("bd_zeroed")
        p_inv_ready = sem("p_inv_ready")
        o_read = sem("o_read")
        k_rms_in = sem("k_rms_in")
        k_rms_out = sem("k_rms_out")
        k2_ready = sem("k2_ready")
        kT_done = sem("kT_done")
        kbd_ready = sem("kbd_ready")
        vT_done = sem("vT_done")
        vbd_ready = sem("vbd_ready")
        q_done = sem("q_done")
        q_rope_ready = sem("q_rope_ready")
        q_sq_ready = sem("q_sq_ready")
        norm_done = sem("norm_done")
        q_rms_in = sem("q_rms_in")
        q_rms_out = sem("q_rms_out")
        vw_done = sem("vw_done")
        vw_ready = sem("vw_ready")
        att2_s_done = sem("att2_s_done")
        att2_d_ready = sem("att2_d_ready")
        att2_dr_ready = sem("att2_dr_ready")
        att2_e_ready = sem("att2_e_ready")
        att2_p_ready = sem("att2_p_ready")
        pT_done = sem("pT_done")
        pT_ready = sem("pT_ready")
        att2_o_done = sem("att2_o_done")
        m2_ready = sem("m2_ready")
        mT_done = sem("mT_done")
        mT_ready = sem("mT_ready")
        r_done = sem("r_done")
        r_d_ready = sem("r_d_ready")
        r_e_ready = sem("r_e_ready")
        h1_done = sem("h1_done")
        h1_ready = sem("h1_ready")
        y2_done = sem("y2_done")
        y2_read = sem("y2_read")
        moe_ready = sem("moe_ready")
        q_sum_ready = sem("q_sum_ready")

        LATER = [("att_w", att_w[:]), ("gate_wT", gate_wT[:]), ("lat_w", lat_w[:]),
                 ("out_wT", out_wT[:]), ("ident2", ident2[:]), ("q_w", q_w), ("kv_w", kv_w[:]),
                 ("wo_w", wo_w[:]), ("trig_f", trig_f[:]), ("trig_t", trig_t[:]),
                 ("head_of", head_of[:]), ("mask", mask_in[:]), ("r_w", r_w[:]), ("e1_w", e1_w),
                 ("e1_b", e1_b[:]), ("e2_w", e2_w[:])]

        LATER_IN = 16 * (len(LATER) + 1)

        CONSTS = [("ident", ident[:]), ("cols", cols[:]), ("cols64", cols64[:]), ("AT", AT[:]),
                  ("A", A_nat[:]), ("w0_blocks", w0_raw), ("W1", w1_raw[:]), ("W2", w2_raw[:])]

        LAYER_STEPS = 3
        ATT_NORMS, ROT_NORMS, GELU_NORMS = CHUNKS, 3 * CHUNKS, 4 * CHUNKS
        EPAIRS = EXPERTS0 // 2
        PAIRS_OF_STEP = ((0, 1), (2, 3, 4), (5, 6, 7), ())
        block = ctx.enter_context(nc.Block())

        def flat(ap):
            return ap.rearrange("p a b -> p (a b)")

        def per_block(ap, width=D):
            if ap.shape[1] == CHUNK_BLOCKS and width != CHUNK_BLOCKS:
                return ap.unsqueeze(2).to_broadcast([P, CHUNK_BLOCKS, width])
            return ap.unsqueeze(1).to_broadcast([P, CHUNK_BLOCKS, width])

        def row(name, width=D):
            return rows[:, ROW_AT[name]:ROW_AT[name] + width]

        def hN_chunk(c):
            return hN[:, bass.ds(c * CHUNK_BLOCKS, CHUNK_BLOCKS), :]

        @block.sync
        def _(sp):
            for name, tile in CONSTS:
                sp.dma_start(tile, t[name]).then_inc(consts_in, 16)

            def load_x(b, par):
                sp.dma_start(x_t[:, par], t["x"][:, bass.ds((b * 2 + par) * (ITER * C0), ITER * C0)]
                             ).then_inc(x_in[par], 16)

            load_x(0, 0)
            load_x(0, 1)
            sp.dma_start(rows[:], t["rows"].partition_broadcast(P)).then_inc(later_in, 16)
            for name, tile in LATER:
                sp.dma_start(tile, t[name]).then_inc(later_in, 16)
            with sp.Fori(1, BATCHES) as b:
                for par in range(2):
                    sp.wait_ge(x_copied, b * 2 + (par - 1))
                    load_x(b, par)
            for n in range(CHUNKS):
                sp.wait_ge(hN_ready, LAYER_STEPS * CHUNKS + n + 1)
                blocks = slice(n * CHUNK_BLOCKS, (n + 1) * CHUNK_BLOCKS)
                sp.dma_start(t["out"][:, blocks], hN[:, blocks]).then_inc(out_sem, 16)
            sp.wait_ge(out_sem, CHUNKS * 16)

        @block.gpsimd
        def _(pool):
            order = Chain(pool, pool_order)
            pool.memset(ones[:], 1.0).then_inc(ones_set, 1)
            order(pool.memset(half_neg[:], -0.5))
            order(pool.memset(x_rep[:], 0.0))
            pool.memset(h0_sb[:], 0.0).then_inc(h0_zeroed, 1)

            def copy_x(b, par, first):
                pool.wait_ge(x_in[par], b * 16 + 16)
                if not first:
                    pool.wait_ge(y_done, b * 2 + (par - 1))
                    pool.sem_inc(pool_gate, 1)
                for g in range(ITER // GROUP):
                    ins = pool.tensor_copy(
                        x_rep[:, par, g, :, 0:GROUP * C0],
                        x_t[:, par, g * GROUP * C0:(g + 1) * GROUP * C0].unsqueeze(1).to_broadcast(
                            [V, P // ROWS, GROUP * C0]))
                ins.then_inc(x_copied, 1)

            pool.wait_ge(bn_var, 1)
            order.wait()
            pool.tensor_tensor(bn_scale[:, 0:3], bn_tmp[:, 0:3], half_neg[:, 0:3],
                               ALU.pow).then_inc(bn_rsqrt, 1)
            copy_x(0, 0, True)
            copy_x(0, 1, True)
            pool.wait_ge(later_in, LATER_IN)
            pool.tensor_copy(pick[:], ident2[:].unsqueeze(2).to_broadcast([P, EXPERTS0, D])).then_inc(pick_ready, 1)
            order(pool.tensor_copy(ident_bf[:], ident[:]))
            order(pool.tensor_copy(mask_bf[:], mask_in[:]))
            order(pool.tensor_scalar(qk_gain[:], row("q_norm"), D ** -0.5, None, ALU.mult))
            splits = ((q_wh[:], q_wl[:], q_w), (kv_wh[:], kv_wl[:], kv_w[:]),
                      (r_wh[:], r_wl[:], r_w[:]), (e1_wh[:], e1_wl[:], e1_w))
            for high, low, raw in splits:
                order(pool.tensor_copy(high, raw))
            order.wait()
            order(pool.tensor_tensor(qk_gain[:], qk_gain[:], row("k_norm"), ALU.mult))
            for high, low, raw in splits:
                last = pool.tensor_tensor(low, raw, high.bitcast(F32), ALU.subtract)
                last.then_inc(splits_ready, 1)
            with pool.Fori(1, BATCHES) as b:
                copy_x(b, 0, False)
                copy_x(b, 1, False)

            def ln_root(n):
                pool.wait_ge(ln_var_ready, n)
                pool.tensor_tensor(ln_rstd[:], ln_var[:], half_neg[:, 0:CHUNK_BLOCKS],
                                   ALU.pow).then_inc(ln_rstd_ready, 1)

            with pool.Fori(0, CHUNKS) as c:
                ln_root(c + 1)
            with pool.Fori(0, CHUNKS) as c:
                ln_root(c * 2 + (ATT_NORMS + 1))
                ln_root(c * 2 + (ATT_NORMS + 2))

            def heads(j):
                return p_sc[:, j % 2].rearrange("p (h s) -> p h s", s=SEQ)

            def over_keys(ap):
                return ap.unsqueeze(2).to_broadcast([P, HEADS, SEQ])

            def q_root(c, j, first):
                if j == 0:
                    pool.wait_ge(q_rms_in, c + 1)
                if not first:
                    pool.wait_ge(att2_dr_ready, c * CHUNK_BLOCKS + (j - CHUNK_BLOCKS + 1))
                at = slice(j * HEADS, (j + 1) * HEADS)
                pool.tensor_tensor(q_rms[:, at], q_var[:, at], half_neg[:, 0:HEADS],
                                   ALU.pow).then_inc(q_rms_out, 1)

            def k_root(c):
                pool.wait_ge(k_rms_in, c + 1)
                pool.tensor_tensor(k_rms[:], k_var[:], half_neg[:, 0:CHUNK_BLOCKS],
                                   ALU.pow).then_inc(k_rms_out, 1)

            def scale(c, j):
                pool.wait_ge(q_rms_out, c * CHUNK_BLOCKS + (j + 1))
                pool.wait_ge(att2_d_ready, c * CHUNK_BLOCKS + (j + 1))
                pool.tensor_tensor(heads(j), heads(j), over_keys(q_rms[:, j * HEADS:(j + 1) * HEADS]),
                                   ALU.mult).then_inc(att2_dr_ready, 1)

            def softmax_divide(c, j):
                pool.wait_ge(p_inv_ready, c * CHUNK_BLOCKS + (j + 1))
                pool.tensor_tensor(heads(j), heads(j), over_keys(p_inv[:, j % 2]),
                                   ALU.mult).then_inc(att2_p_ready, 1)

            def chunk_step(b, prev, front):
                f = b + 1
                for j in range(CHUNK_BLOCKS):
                    if j > 0:
                        softmax_divide(b, j - 1)
                    elif prev:
                        softmax_divide(b - 1, CHUNK_BLOCKS - 1)
                    scale(b, j)
                    if front and j == 1:
                        k_root(f)
                    if j + 1 < CHUNK_BLOCKS:
                        q_root(b, j + 1, not prev)
                if front:
                    q_root(f, 0, False)
                if prev:
                    ln_root(b + ROT_NORMS)

            k_root(0)
            q_root(0, 0, True)
            chunk_step(0, False, True)
            with pool.Fori(1, CHUNKS - 1) as c:
                chunk_step(c, True, True)
            chunk_step(CHUNKS - 1, True, False)
            softmax_divide(CHUNKS - 1, CHUNK_BLOCKS - 1)
            ln_root(CHUNKS + ROT_NORMS)

            def gelu_step(c, par, back, front):
                b = c - 1
                if front:
                    ln_root(c * 2 + (GELU_NORMS + 1) if back else GELU_NORMS + 2)
                if back:
                    pool.wait_ge(y2_read, b + 1)
                    for j in range(CHUNK_BLOCKS):
                        m = moe[j].rearrange("p (e d) -> p e d", d=D)
                        pool.tensor_tensor(m, m, wf[:, 1 - par, j].unsqueeze(2).to_broadcast(
                            [P, EXPERTS1, D]), ALU.mult).then_inc(moe_ready, 1)
                    ln_root(c * 2 + (GELU_NORMS + (2 if front else 1)))

            ln_root(GELU_NORMS + 1)
            gelu_step(0, 0, False, True)
            with pool.Fori(0, CHUNKS // 2 - 1) as i:
                gelu_step(i * 2 + 1, 1, True, True)
                gelu_step(i * 2 + 2, 0, True, True)
            gelu_step(CHUNKS - 1, 1, True, False)
            pool.wait_ge(y2_read, CHUNKS)
            for j in range(CHUNK_BLOCKS):
                m = moe[j].rearrange("p (e d) -> p e d", d=D)
                pool.tensor_tensor(m, m, wf[:, 1, j].unsqueeze(2).to_broadcast([P, EXPERTS1, D]),
                                   ALU.mult).then_inc(moe_ready, 1)
            ln_root(2 * CHUNKS + GELU_NORMS)

        @block.tensor
        def _(pe):
            pe.wait_ge(ones_set, 1)
            pe.wait_ge(diag_ready, 1)
            nc.tensor.matmul(mix_ps[:, 0:512], ones[:], diag[:, 0:4].rearrange("p a b -> p (a b)"),
                             start=True, stop=True)
            nc.tensor.matmul(z_ps[0][:, 0:P], ones[:], diag[:, 4],
                             start=True, stop=True).then_inc(rows_done, 1)
            nc.tensor.matmul(y_ps[:, 0:V], ones[0:V, :], A_nat[:], start=True,
                             stop=True).then_inc(abar_done, 1)
            pe.wait_ge(weights_ready, 1)

            def y_product(b, par):
                pe.wait_ge(x_copied, b * 2 + (par + 1))
                for g in range(ITER // GROUP):
                    ins = nc.tensor.matmul(
                        y_ps[:, g * V:(g + 1) * V],
                        x_rep[:, par, g].rearrange("v q r -> v (q r)"),
                        AT[0:V, :], start=(g == 0), stop=True, skip_group_check=True)
                ins.then_inc(y_done, 1)

            def layer0(k):
                par, g, half = (k // 8) % 2, (k % 8) // 2, k % 2
                nc.tensor.matmul(h0_ps[k % 2][0:V, :], y_hl[:, par, g, :],
                                 w0_hl[:, half * 512:(half + 1) * 512],
                                 start=True, stop=True).then_inc(l0_done, 1)

            def node_mix(k, lo, hi):
                for j in range(lo, hi):
                    ins = nc.tensor.matmul(ah_ps[k % 2][:, j * V:(j + 1) * V],
                                           h0_sb[:, k % 2, j * CH:(j + 1) * CH], AT[:],
                                           start=(j == 0), stop=True, skip_group_check=True)
                return ins

            def layer1(k, count):
                pe.wait_ge(ah_ready, count)
                nc.tensor.matmul(z_ps[k % 2][:, 0:UNIT * V], w1_s[:], ah_sb[:, k % 2, :],
                                 start=True, stop=True).then_inc(z_done, 1)

            def norms(p):
                for j in range(CHUNK_BLOCKS):
                    at = j * HEADS + 2 * p
                    ins = nc.tensor.matmul(bank[7][:, at:at + 2], q_sq[:, p % 2, j * P:(j + 1) * P],
                                           head_of[:], start=(p == 0 and j == 0), stop=True,
                                           skip_group_check=True)
                return ins

            def batch(b, first, last):
                for k in range(UNITS):
                    u = b * UNITS + k
                    pe.wait_ge(h0_ready, u + 1)
                    node_mix(k, 0, 2)
                    if not (last and k == UNITS - 1):
                        if k % 8 == 7:
                            pe.wait_ge(y_ready, b * 2 + (k // 8 + 2))
                        layer0((k + 1) % UNITS)
                    node_mix(k, 2, UNIT).then_inc(amix_done, 1)
                    if k == 2:
                        y_product(b, 1)
                    if k == 10 and not last:
                        y_product(b + 1, 0)
                    if not (first and k == 0):
                        if not (first and k < 3):
                            pe.wait_ge(prod_done, u - 2)
                        layer1((k - 1) % UNITS, u)

            y_product(0, 0)
            pe.wait_ge(y_ready, 1)
            layer0(0)
            batch(0, True, False)
            with pe.Fori(1, BATCHES - 1) as b:
                batch(b, False, False)
            batch(BATCHES - 1, False, True)
            pe.wait_ge(prod_done, BATCHES * UNITS - 2)
            layer1(UNITS - 1, BATCHES * UNITS)

            pe.wait_ge(later_in, LATER_IN)
            pe.wait_ge(pick_ready, 1)
            pe.wait_ge(splits_ready, 4)
            mm = nc.tensor.matmul

            with pe.Fori(0, CHUNKS) as c:
                pe.wait_ge(sT_copied, c + 1)
                for j in range(CHUNK_BLOCKS):
                    mm(bank[1][:, j * D:(j + 1) * D], s_chunk[:, j * P:(j + 1) * P], w2_s[:],
                       start=(j == 0), stop=True, skip_group_check=True)
                mm(bank[0][0:D, :], w2_s[:], s_chunk[:], start=True, stop=True).then_inc(att_h_done, 1)
                pe.wait_ge(att_hT_ready, c + 1)
                pe.sem_inc(pe_gate, 1)
                mm(bank[2][0:D, :], att_w[:, 0:D], hT[:], start=True, stop=True)
                mm(bank[3][0:D, :], att_w[:, D:2 * D], hT[:], start=True, stop=True).then_inc(att_qkv_done, 1)
                for b2 in range(CB):
                    ins = mm(bank[4][0:SEQ, b2 * D:(b2 + 1) * D], hT[:, b2 * SEQ:(b2 + 1) * SEQ],
                             att_w[:, 2 * D:3 * D], start=(b2 == 0), stop=True, skip_group_check=True)
                ins.then_inc(att_qkv_done, 1)
                pe.wait_ge(att_qk_ready, c * 2 + 2)
                pe.sem_inc(pe_gate, 1)
                for b2 in range(CB):
                    at = (b2 % 2) * SEQ
                    ins = mm(bank[5][at:at + SEQ, (b2 // 2) * SEQ:(b2 // 2 + 1) * SEQ],
                             qT[:, b2 * SEQ:(b2 + 1) * SEQ], kT[:, b2 * SEQ:(b2 + 1) * SEQ],
                             start=(b2 < 2), stop=True, skip_group_check=True)
                ins.then_inc(att_s_done, 1)
                pe.wait_ge(att_e_ready, c + 1)
                pe.sem_inc(pe_gate, 1)
                for j in range(CHUNK_BLOCKS):
                    ins = nc.tensor.transpose(bank[6][0:SEQ, j * P:(j + 1) * P], sc_e[:, j], ident[:])
                ins.then_inc(att_eT_done, 1)
                pe.wait_ge(att_eT_ready, c + 1)
                pe.wait_ge(att_v_ready, c + 1)
                pe.sem_inc(pe_gate, 1)
                for b2 in range(CB):
                    at = (b2 % 2) * SEQ
                    ins = mm(bank[7][at:at + SEQ, (b2 // 2) * D:(b2 // 2 + 1) * D],
                             eT[:, b2 // 2, at:at + SEQ], v_sb[:, b2],
                             start=(b2 < 2), stop=True, skip_group_check=True)
                ins.then_inc(att_o_done, 1)

            def lattice_T(c):
                pe.wait_ge(x2_ready, c + 1)
                for j in range(CHUNK_BLOCKS):
                    ins = nc.tensor.transpose(bank[0][:, j * P:(j + 1) * P], flat(x2[:, j]), ident[:])
                ins.then_inc(xT_done, 1)

            def gate(c, par):
                pe.wait_ge(xT_ready, c + 1)
                for j in range(CHUNK_BLOCKS):
                    ins = mm(bank[1][:, j * EXPERTS0:(j + 1) * EXPERTS0], lat_x[par][0:D, j * P:(j + 1) * P],
                             gate_wT[:], start=(j == 0), stop=True, skip_group_check=True)
                ins.then_inc(lg_done, 1)

            def scores_T(c):
                pe.wait_ge(w2_ready, c + 1)
                for j in range(CHUNK_BLOCKS):
                    ins = nc.tensor.transpose(bank[0][:, j * P:(j + 1) * P], flat(w2x[:, j]), ident[:])
                ins.then_inc(wT_done, 1)

            def spread(c, par, p):
                if p == 0:
                    pe.wait_ge(wT_ready, c + 1)
                mm(spread_ps[p % 4][:], flat(pick[:, 2 * p:2 * p + 2]), lat_w_hl[par][:],
                   start=True, stop=True).then_inc(bc_done, 1)

            def project(c):
                pe.wait_ge(latT_ready, c + 1)
                for j in range(CHUNK_BLOCKS):
                    ins = mm(bank[1][:, j * D:(j + 1) * D], latT[0:D, j * P:(j + 1) * P], out_wT[:],
                             start=(j == 0), stop=True, skip_group_check=True)
                ins.then_inc(proj_done, 1)

            def lattice_step(c, par, back, front):
                for p in range(EPAIRS):
                    pe.wait_ge(z_ready, c * EPAIRS + (p + 1))
                    mm(lat_ps[par][0:D, :], lat_w[:, p], lat_z[p % 4], start=(p == 0),
                       stop=(p == EPAIRS - 1)).then_inc(lat_done, 1)
                    if p + 4 < EPAIRS:
                        spread(c, par, p + 4)
                    elif front:
                        spread(c + 1, 1 - par, p + 4 - EPAIRS)
                    if p == 2 and back:
                        project(c - 1)
                    if p == 7 and front:
                        lattice_T(c + 1)
                    if p == 11 and front:
                        gate(c + 1, 1 - par)
                    if p == 23 and front:
                        scores_T(c + 1)

            lattice_T(0)
            gate(0, 0)
            scores_T(0)
            for p in range(4):
                spread(0, 0, p)
            lattice_step(0, 0, False, True)
            with pe.Fori(0, CHUNKS // 2 - 1) as i:
                lattice_step(i * 2 + 1, 1, True, True)
                lattice_step(i * 2 + 2, 0, True, True)
            lattice_step(CHUNKS - 1, 1, True, False)
            project(CHUNKS - 1)

            def scores(c, par, j, first=False):
                n = c * CHUNK_BLOCKS + j
                if j == 0:
                    pe.wait_ge(kbd_ready, c * 2 + 2)
                    pe.wait_ge(q_sum_ready, (c + 1) * PAIRS)
                if not first:
                    pe.wait_ge(att2_d_ready, n)
                for half in range(2):
                    mm(bank[4 + half][:], ident_bf[:], mask_bf[:], start=True, stop=False,
                       skip_group_check=True)
                for b2 in range(2):
                    toks = (2 * j + b2) * SEQ
                    for p in range(PAIRS):
                        ins = mm(bank[4 + p // 4][b2 * SEQ:(b2 + 1) * SEQ, (p % 4) * P:(p % 4 + 1) * P],
                                 qr[par][p][:, toks:toks + SEQ], flat(k_bd[par][:, 2 * j + b2]),
                                 start=False, stop=(p % 4 == 3), skip_group_check=True)
                ins.then_inc(att2_s_done, 1)

            def weights_T(c, j, half, first=False):
                n = c * CHUNK_BLOCKS + j
                if half == 0:
                    pe.wait_ge(att2_p_ready, n + 1)
                if not first:
                    pe.wait_ge(pT_ready, n * 2 + half)
                for p in range(half * 4, half * 4 + 4):
                    ins = nc.tensor.transpose(bank[6][:, (p % 4) * P:(p % 4 + 1) * P],
                                              p_sc[:, j % 2, p * P:(p + 1) * P], ident[:])
                ins.then_inc(pT_done, 1)

            def values_out(c, j, first=False):
                pe.wait_ge(pT_ready, (c * CHUNK_BLOCKS + (j + 1)) * 2)
                pe.wait_ge(vw_ready, c * CB + (2 * j + 2))
                if j == 0 and not first:
                    pe.wait_ge(o_read, c)
                for b2 in range(2):
                    for p in range(PAIRS):
                        ins = mm(bank[0][b2 * SEQ:(b2 + 1) * SEQ, j * D:(j + 1) * D],
                                 pT[:, j % 2, p * P + b2 * SEQ:p * P + (b2 + 1) * SEQ],
                                 vw[:, 2 * j + b2, p * D:(p + 1) * D],
                                 start=(p == 0 and j == 0), stop=(p == PAIRS - 1), skip_group_check=True)
                ins.then_inc(att2_o_done, 1)

            def value_proj(c, par, b2):
                if b2 == 2:
                    pe.wait_ge(vw_ready, c * CB + 2)
                elif b2 > 0:
                    pe.wait_ge(vw_ready, c * CB + b2)
                else:
                    pe.wait_ge(kbd_ready, c * 2 + 2)
                mm(bank[3][:], flat(v_bd[par][:, b2]), flat(wo_w[:]), start=True,
                   stop=True).then_inc(vw_done, 1)

            def chunk_T(c, first=False):
                pe.wait_ge(gx2_ready, c + 1)
                if not first:
                    pe.wait_ge(q_rms_in, c)
                for j in range(CHUNK_BLOCKS):
                    ins = nc.tensor.transpose(bank[7][:, j * P:(j + 1) * P], flat(x2[:, j]), ident[:])
                ins.then_inc(gxT_done, 1)

            def values_T(c):
                mm(bank[7][:], kv_wh[:, 2 * D:4 * D], xT_hl[:], start=True, stop=False)
                mm(bank[7][:], kv_wl[:, 2 * D:4 * D], xT_hl[:], start=False, stop=True).then_inc(vT_done, 1)

            def keys(c, first=False):
                if not first:
                    pe.wait_ge(vw_ready, (c - 1) * CB + 2)
                for j in range(CHUNK_BLOCKS):
                    xs = xT_hl[:, j * P:(j + 1) * P]
                    at = slice(j * 2 * D, (j + 1) * 2 * D)
                    mm(bank[3][:, at], xs, kv_wh[:, 0:2 * D], start=(j == 0), stop=False, skip_group_check=True)
                    ins = mm(bank[3][:, at], xs, kv_wl[:, 0:2 * D], start=False, stop=True, skip_group_check=True)
                ins.then_inc(kn_done, 1)

            def queries(c, p, first=False):
                if p == 0:
                    pe.wait_ge(gxT_ready, c + 1)
                if not first:
                    pe.wait_ge(q_sq_ready, c * PAIRS + p)
                    pe.wait_ge(q_rope_ready, c * 2 * PAIRS + 2 * p)
                for s2 in range(2):
                    mm(bank[1 + s2][:], q_wh[:, s2, p * P:(p + 1) * P], xT_hl[:], start=True, stop=False)
                    mm(bank[1 + s2][:], q_wl[:, s2, p * P:(p + 1) * P], xT_hl[:], start=False,
                       stop=True).then_inc(q_done, 1)

            def q_norms(c, p):
                if p == 0:
                    pe.wait_ge(vbd_ready, c * 2 + 2)
                pe.wait_ge(q_sq_ready, c * PAIRS + (p + 1))
                ins = norms(p)
                if p == PAIRS - 1:
                    ins.then_inc(norm_done, 1)

            def keys_T(c, first=False):
                pe.wait_ge(k2_ready, c + 1)
                if not first:
                    pe.wait_ge(vw_ready, c * CB)
                for j in range(CHUNK_BLOCKS):
                    ins = nc.tensor.transpose(bank[3][:, j * P:(j + 1) * P], flat(w2x[:, j]), ident[:])
                ins.then_inc(kT_done, 1)

            def chunk_step(b, prev, front, par):
                f = b + 1
                bp = 0 if not prev else 1 - par
                if front:
                    chunk_T(f)
                scores(b, bp, 0, not prev)
                value_proj(b, bp, 0)
                if prev:
                    weights_T(b - 1, 3, 0)
                if front:
                    queries(f, 0)
                    values_T(f)
                if prev:
                    weights_T(b - 1, 3, 1)
                value_proj(b, bp, 1)
                if front:
                    queries(f, 1)
                if prev:
                    values_out(b - 1, 3)
                if front:
                    keys(f)
                    q_norms(f, 0)
                for j in (1, 2):
                    scores(b, bp, j)
                    if front:
                        queries(f, 3 * j - 1)
                    weights_T(b, j - 1, 0, not prev and j == 1)
                    if front and j == 1:
                        pe.wait_ge(kn_read, f + 1)
                    value_proj(b, bp, 2 * j)
                    if front:
                        q_norms(f, 3 * j - 2)
                        queries(f, 3 * j)
                    weights_T(b, j - 1, 1)
                    value_proj(b, bp, 2 * j + 1)
                    if front:
                        q_norms(f, 3 * j - 1)
                        queries(f, 3 * j + 1)
                    values_out(b, j - 1, not prev)
                    if front:
                        q_norms(f, 3 * j)
                if front:
                    q_norms(f, PAIRS - 1)
                scores(b, bp, 3)
                value_proj(b, bp, 6)
                weights_T(b, 2, 0)
                value_proj(b, bp, 7)
                weights_T(b, 2, 1)
                if front:
                    keys_T(f)
                values_out(b, 2)

            chunk_T(0, True)
            queries(0, 0, True)
            values_T(0)
            keys(0, True)
            for p in range(PAIRS):
                if p > 0:
                    queries(0, p)
                if p > 0:
                    q_norms(0, p - 1)
            q_norms(0, PAIRS - 1)
            keys_T(0, True)
            chunk_step(0, False, True, 1)
            with pe.Fori(0, CHUNKS // 2 - 1) as i:
                chunk_step(i * 2 + 1, True, True, 0)
                chunk_step(i * 2 + 2, True, True, 1)
            chunk_step(CHUNKS - 1, True, False, 0)
            weights_T(CHUNKS - 1, 3, 0)
            weights_T(CHUNKS - 1, 3, 1)
            values_out(CHUNKS - 1, 3)

            def rows_T(c):
                pe.wait_ge(m2_ready, c + 1)
                for j in range(CHUNK_BLOCKS):
                    ins = nc.tensor.transpose(bank[0][:, j * P:(j + 1) * P], flat(x2[:, j]), ident[:])
                ins.then_inc(mT_done, 1)

            def router(c, par):
                pe.wait_ge(mT_ready, c + 1)
                for j in range(CHUNK_BLOCKS):
                    xs = mT_hl[par][:, j * P:(j + 1) * P]
                    at = slice(j * EXPERTS1, (j + 1) * EXPERTS1)
                    mm(bank[1][:, at], xs, r_wh[:], start=(j == 0), stop=False, skip_group_check=True)
                    ins = mm(bank[1][:, at], xs, r_wl[:], start=False, stop=True, skip_group_check=True)
                ins.then_inc(r_done, 1)

            def second(c, e):
                pe.wait_ge(h1_ready, c * EXPERTS1 + (e + 1))
                for j in range(CHUNK_BLOCKS):
                    ins = mm(bank[4 + j][:, e * D:(e + 1) * D], hid[:, e % 2, j * P:(j + 1) * P],
                             e2_w[:, e], start=(e == 0), stop=True, skip_group_check=True)
                return ins

            def gelu_step(c, par, back, front):
                for e in range(EXPERTS1):
                    if back or e >= 2:
                        pe.wait_ge(h1_ready, c * EXPERTS1 + (e - 1))
                    mm(bank[2 + e % 2][:], e1_wh[:, e * HID1:(e + 1) * HID1], mT_hl[par][:], start=True,
                       stop=False)
                    mm(bank[2 + e % 2][:], e1_wl[:, e * HID1:(e + 1) * HID1], mT_hl[par][:], start=False,
                       stop=True).then_inc(h1_done, 1)
                    if e == 1 and back:
                        pe.wait_ge(y2_read, c)
                    if e >= 1:
                        second(c, e - 1)
                    if e == 3 and front:
                        rows_T(c + 1)
                second(c, EXPERTS1 - 1).then_inc(y2_done, 1)
                if front:
                    router(c + 1, 1 - par)

            rows_T(0)
            router(0, 0)
            gelu_step(0, 0, False, True)
            with pe.Fori(0, CHUNKS // 2 - 1) as i:
                gelu_step(i * 2 + 1, 1, True, True)
                gelu_step(i * 2 + 2, 0, True, True)
            gelu_step(CHUNKS - 1, 1, True, False)

        @block.scalar
        def _(act):
            def hidden(k):
                nc.scalar.activation(h0_sb[0:V, k % 2, :], h0_ps[k % 2][0:V, :],
                                     ACT.Relu).then_inc(h0_ready, 1)

            def batch(b, first, last):
                for k in range(UNITS):
                    u = b * UNITS + k
                    if not (last and k == UNITS - 1):
                        act.wait_ge(l0_done, u + 2)
                        if not (first and k == 0):
                            act.wait_ge(amix_done, u)
                        hidden((k + 1) % UNITS)
                    act.wait_ge(amix_done, u + 1)
                    if not (first and k < 2):
                        act.wait_ge(z_done, u - 1)
                    nc.scalar.activation(ah_sb[:, k % 2, :], ah_ps[k % 2][:, 0:UNIT * V],
                                         ACT.Copy).then_inc(ah_ready, 1)

            act.wait_ge(h0_zeroed, 1)
            act.wait_ge(l0_done, 1)
            hidden(0)
            batch(0, True, False)
            with act.Fori(1, BATCHES - 1) as b:
                batch(b, False, False)
            batch(BATCHES - 1, False, True)

            go = nc.scalar.activation
            with act.Fori(0, CHUNKS) as c:
                act.wait_ge(att_h_done, c + 1)
                go(hT[:], bank[0][0:D, :], ACT.Identity, bias=bn_bias[0:D, 2:3]).then_inc(att_hT_ready, 1)
                act.wait_ge(att_qkv_done, c * 2 + 1)
                go(qT[:], bank[2][0:D, :], ACT.Identity, bias=cols64[0:D, 5:6]).then_inc(att_qk_ready, 1)
                go(kT[:], bank[3][0:D, :], ACT.Identity, bias=cols64[0:D, 6:7]).then_inc(att_qk_ready, 1)
                act.wait_ge(att_qkv_done, c * 2 + 2)
                go(flat(v_sb[:]), bank[4][0:SEQ, :], ACT.Copy).then_inc(att_v_ready, 1)
                act.wait_ge(att_d_ready, c + 1)
                go(sc_e[:], sc[:], ACT.Exp, scale=D ** -0.5).then_inc(att_e_ready, 1)
                act.wait_ge(att_eT_done, c + 1)
                go(flat(eT[:]), bank[6][0:SEQ, :], ACT.Copy).then_inc(att_eT_ready, 1)

            def twice(c, layer, ready):
                go(x2[:], hN_chunk(c).unsqueeze(2).to_broadcast([P, CHUNK_BLOCKS, 2, D]),
                   ACT.Copy).then_inc(ready, 1)

            def lattice_front(c, par):
                twice(c, 0, x2_ready)
                act.wait_ge(xT_done, c + 1)
                go(lat_x[par], bank[0][:], ACT.Copy).then_inc(xT_ready, 1)
                act.wait_ge(lg_d_ready, c + 1)
                go(sc_e[:], sc[:], ACT.Exp).then_inc(lg_e_ready, 1)

            def lattice_out(c, par):
                act.wait_ge(lat_done, (c + 1) * EPAIRS)
                go(latT[0:D], lat_ps[par][0:D, :], ACT.Copy).then_inc(latT_ready, 1)

            act.wait_ge(hN_ready, CHUNKS)
            lattice_front(0, 0)
            lattice_front(1, 1)
            with act.Fori(0, CHUNKS // 2 - 1) as i:
                lattice_out(i * 2, 0)
                lattice_front(i * 2 + 2, 0)
                lattice_out(i * 2 + 1, 1)
                lattice_front(i * 2 + 3, 1)
            lattice_out(CHUNKS - 2, 0)
            lattice_out(CHUNKS - 1, 1)

            def softmax_exp(c, j):
                act.wait_ge(att2_dr_ready, c * CHUNK_BLOCKS + (j + 1))
                go(p_sc[:, j % 2], p_sc[:, j % 2], ACT.Exp).then_inc(att2_e_ready, 1)

            def copy_pT(c, j, half, early=False):
                act.wait_ge(pT_done, (c * CHUNK_BLOCKS + j) * 2 + (half + 1))
                if half == 0 and not early:
                    act.wait_ge(att2_o_done, c * CHUNK_BLOCKS + (j - 1))
                go(pT[:, j % 2, half * CT:(half + 1) * CT], bank[6][:], ACT.Copy).then_inc(pT_ready, 1)

            def copy_vw(c, b2):
                act.wait_ge(vw_done, c * CB + (b2 + 1))
                go(vw[:, b2], bank[3][:], ACT.Copy).then_inc(vw_ready, 1)

            def square(c, p):
                act.wait_ge(q_done, c * 2 * PAIRS + (2 * p + 1))
                go(q_sq[:, p % 2], bank[1][:], ACT.Square).then_inc(q_sq_ready, 1)

            def block_diagonal(done, ready, src, dst, c):
                act.wait_ge(done, c + 1)
                for h in range(2):
                    at = slice(h * D, (h + 1) * D)
                    go(dst[at, :, h], src[at, :].rearrange("p (b s) -> p b s", s=SEQ),
                       ACT.Copy).then_inc(ready, 1)

            def rows_twice(c, first=False):
                if not first:
                    act.wait_ge(gxT_done, c)
                go(x2[:], hN_chunk(c).unsqueeze(2).to_broadcast([P, CHUNK_BLOCKS, 2, D]),
                   ACT.Copy).then_inc(gx2_ready, 1)

            def chunk_step(b, prev, front, par, more=True):
                f = b + 1
                copy_vw(b, 0)
                if prev:
                    copy_pT(b - 1, 3, 0)
                if front:
                    square(f, 0)
                    block_diagonal(vT_done, vbd_ready, bank[7], v_bd[par], f)
                if prev:
                    copy_pT(b - 1, 3, 1)
                copy_vw(b, 1)
                if front:
                    square(f, 1)
                softmax_exp(b, 0)
                for j in (1, 2):
                    if front:
                        square(f, 3 * j - 1)
                    copy_pT(b, j - 1, 0, not prev)
                    copy_vw(b, 2 * j)
                    if front:
                        square(f, 3 * j)
                    copy_pT(b, j - 1, 1)
                    copy_vw(b, 2 * j + 1)
                    if front:
                        square(f, 3 * j + 1)
                    softmax_exp(b, j)
                copy_vw(b, 6)
                copy_pT(b, 2, 0)
                copy_vw(b, 7)
                copy_pT(b, 2, 1)
                if front:
                    block_diagonal(kT_done, kbd_ready, bank[3], k_bd[par], f)
                if front and more:
                    rows_twice(f + 1)
                softmax_exp(b, 3)

            act.wait_ge(hN_ready, 2 * CHUNKS)
            rows_twice(0, True)
            square(0, 0)
            act.wait_ge(bd_zeroed, 1)
            block_diagonal(vT_done, vbd_ready, bank[7], v_bd[0], 0)
            for p in range(1, PAIRS):
                square(0, p)
            block_diagonal(kT_done, kbd_ready, bank[3], k_bd[0], 0)
            rows_twice(1)
            chunk_step(0, False, True, 1)
            with act.Fori(0, CHUNKS // 2 - 2) as i:
                chunk_step(i * 2 + 1, True, True, 0)
                chunk_step(i * 2 + 2, True, True, 1)
            chunk_step(CHUNKS - 3, True, True, 0)
            chunk_step(CHUNKS - 2, True, True, 1, False)
            chunk_step(CHUNKS - 1, True, False, 0)
            copy_pT(CHUNKS - 1, 3, 0)
            copy_pT(CHUNKS - 1, 3, 1)

            def router_exp(c):
                act.wait_ge(r_d_ready, c + 1)
                go(sc_e[:, :, 0:EXPERTS1], sc[:, :, 0:EXPERTS1], ACT.Exp).then_inc(r_e_ready, 1)

            def gelu_step(c, front):
                for e in range(EXPERTS1):
                    act.wait_ge(h1_done, c * EXPERTS1 + (e + 1))
                    go(hid[:, e % 2], bank[2 + e % 2][:], ACT.Gelu,
                       bias=e1_b[:, e:e + 1]).then_inc(h1_ready, 1)
                if front:
                    router_exp(c + 1)

            router_exp(0)
            with act.Fori(0, CHUNKS - 1) as c:
                gelu_step(c, True)
            gelu_step(CHUNKS - 1, False)

        @block.vector
        def _(dve):
            vec = nc.vector
            order = Chain(dve, dve_order)
            dve.wait_ge(consts_in, 16 * len(CONSTS))
            order(vec.memset(bn_tmp[:], 1.0))
            order(vec.memset(bn_bias[:], 0.0))
            order.wait()
            order(vec.tensor_scalar(bn_tmp[:, 0:2], cols[:, 4:10:5], EPS_BN, None, ALU.add))
            order.wait()
            vec.tensor_scalar(bn_tmp[0:D, 2:3], cols64[0:D, 4:5], EPS_BN, None,
                              ALU.add).then_inc(bn_var, 1)
            dve.wait_ge(bn_rsqrt, 1)
            order(vec.tensor_tensor(bn_scale[:, 0:2], bn_scale[:, 0:2], cols[:, 1:7:5], ALU.mult))
            order(vec.tensor_tensor(bn_scale[0:D, 2:3], bn_scale[0:D, 2:3], cols64[0:D, 1:2], ALU.mult))
            order(vec.tensor_tensor(bn_bias[:, 0:2], cols[:, 0:6:5], cols[:, 3:9:5], ALU.subtract))
            order(vec.tensor_tensor(bn_bias[0:D, 2:3], cols64[0:D, 0:1], cols64[0:D, 3:4], ALU.subtract))
            order.wait()
            order(vec.tensor_tensor(bn_bias[:, 0:3], bn_bias[:, 0:3], bn_scale[:, 0:3], ALU.mult))
            order.wait()
            order(vec.tensor_tensor(bn_bias[:, 0:2], bn_bias[:, 0:2], cols[:, 2:8:5], ALU.add))
            order(vec.tensor_tensor(bn_bias[0:D, 2:3], bn_bias[0:D, 2:3], cols64[0:D, 2:3], ALU.add))
            order.wait()
            order(vec.tensor_scalar(neg_b1[:], bn_bias[:, 1:2], -1.0, None, ALU.mult))
            for n, col in enumerate((bn_scale[:, 0:1], bn_bias[:, 0:1], bn_scale[:, 1:2])):
                order(vec.tensor_scalar(diag[:, n], ident[:], col, None, ALU.mult))
            order(vec.tensor_scalar(diag[:, 3], ident[:], bn_scale[:, 2:3], None, ALU.mult))
            order.wait()
            vec.tensor_scalar(diag[:, 4], ident[:], bn_bias[:, 2:3], None,
                              ALU.mult).then_inc(diag_ready, 1)
            dve.wait_ge(rows_done, 1)
            order(vec.tensor_copy(rows_b[:, 0:4].rearrange("p a b -> p (a b)"), mix_ps[:, 0:512]))
            order(vec.tensor_copy(rows_b[:, 4], z_ps[0][:, 0:P]))
            dve.wait_ge(abar_done, 1)
            order(vec.tensor_scalar(abar[:], y_ps[:, 0:V], NODES_INV, None, ALU.mult))
            order.wait()
            order(vec.tensor_reduce(a_sum[:], abar[:], AX_X, ALU.add))
            order(vec.tensor_tensor(w1_s[:], w1_raw[:], rows_b[:, 2], ALU.mult))
            order(vec.tensor_tensor(w2_s[:], w2_raw[:], rows_b[:, 3, 0:D], ALU.mult))
            per_token = "p (j c) -> p j c"
            order(vec.tensor_tensor(
                w0_tmp.rearrange(per_token, j=GROUP), w0_raw.rearrange(per_token, j=GROUP),
                rows_b[:, 0:1, :].to_broadcast([P, GROUP, CH]), ALU.mult))
            order.wait()
            order(vec.tensor_tensor(s_corr[:], a_sum[:], bn_bias[:, 1:2], ALU.mult))
            order(vec.scalar_tensor_tensor(
                w0_tmp.rearrange(per_token, j=GROUP),
                rows_b[:, 1:2, :].to_broadcast([P, GROUP, CH]), cols[:, 10:11],
                w0_tmp.rearrange(per_token, j=GROUP), ALU.mult, ALU.add))
            order.wait()
            order(vec.tensor_copy(w0_hl[:], w0_tmp))
            order.wait()
            order(vec.tensor_tensor(w0_hl[32:64], w0_tmp[32:64], w0_hl[32:64].bitcast(F32),
                                    ALU.subtract))
            order.wait()
            vec.tensor_tensor(w0_hl[96:128], w0_tmp[96:128], w0_hl[96:128].bitcast(F32),
                              ALU.subtract).then_inc(weights_ready, 1)

            abar_u = abar[:].unsqueeze(1).to_broadcast([CH, UNIT, V])

            def y_split(b, par):
                dve.wait_ge(y_done, b * 2 + (par + 1))
                flat = y_hl[:, par].rearrange("p g v -> p (g v)")
                vec.tensor_scalar(flat, y_ps[:, 0:ITER // GROUP * V], cols[:, 10:11],
                                  None, ALU.add).then_inc(y_high, 1)
                dve.wait_ge(y_high, b * 2 + (par + 1))
                vec.tensor_tensor(flat[64:128], y_ps[64:128, 0:ITER // GROUP * V],
                                  flat[64:128].bitcast(F32), ALU.subtract).then_inc(y_ready, 1)

            def node_sum(b, k, first):
                slot = (k // 4) % 2
                dve.wait_ge(z_done, b * UNITS + (k + 1))
                if k % 4 == 0 and not (first and k < 8):
                    dve.wait_ge(s_ready, b * 4 + (k // 4 - 1))
                vec.scalar_tensor_tensor(
                    prod[:, slot, k % 4].rearrange("p (j v) -> p j v", v=V),
                    z_ps[k % 2][:, 0:UNIT * V].rearrange("p (j v) -> p j v", v=V), neg_b1[:, 0:1],
                    abar_u, ALU.max, ALU.mult).then_inc(prod_done, 1)
                if k % 4 == 3:
                    dve.wait_ge(prod_done, b * UNITS + (k + 1))
                    vec.tensor_reduce(
                        sT[:, bass.ds(b * SEQ + 4 * (k - 3), 16)],
                        prod[:, slot].rearrange("p q (j v) -> p (q j) v", v=V),
                        AX_X, ALU.add).then_inc(s_ready, 1)

            def batch(b, first, last):
                for k in range(UNITS):
                    if k > 0:
                        node_sum(b, k - 1, first)
                    elif not first:
                        node_sum(b - 1, UNITS - 1, False)
                    if k == 3:
                        y_split(b, 1)
                    if k == 11 and not last:
                        y_split(b + 1, 0)

            y_split(0, 0)
            batch(0, True, False)
            with dve.Fori(1, BATCHES - 1) as b:
                batch(b, False, False)
            batch(BATCHES - 1, False, True)
            node_sum(BATCHES - 1, UNITS - 1, False)

            tt, stt, ts = vec.tensor_tensor, vec.scalar_tensor_tensor, vec.tensor_scalar

            def normalize(n, src, dst, after=None):
                center(src)
                variance()
                normalized(n, dst, after)

            def center(src):
                order.wait()
                order(vec.tensor_reduce(ln_mean[:], src, AX_X, ALU.add))
                order.wait()
                order(ts(ln_mean[:], ln_mean[:], -1.0 / D, None, ALU.mult))
                order.wait()
                order(tt(xc[:], src, per_block(ln_mean[:]), ALU.add))

            def variance():
                order.wait()
                order(tt(xsq[:], xc[:], xc[:], ALU.mult))
                order.wait()
                order(vec.tensor_reduce(ln_var[:], xsq[:], AX_X, ALU.add))
                order.wait()
                ts(ln_var[:], ln_var[:], 1.0 / D, EPS_LN, ALU.mult, ALU.add).then_inc(ln_var_ready, 1)

            def normalized(n, dst, after=None):
                dve.wait_ge(ln_rstd_ready, n)
                ins = tt(dst, xc[:], per_block(ln_rstd[:]), ALU.mult)
                if after is None:
                    order(ins)
                else:
                    ins.then_inc(after, 1)

            def layer(body, per_trip, index):
                with dve.Fori(0, CHUNKS) as c:
                    order.enter(c, per_trip)
                    body(c)
                order.leave(CHUNKS)
                dve.wait_ge(hN_ready, (index + 1) * CHUNKS)

            def attention(c):
                ts(s_chunk[:], sT[:, bass.ds(c * CT, CT)], s_corr[:, 0:1], None, ALU.add).then_inc(sT_copied, 1)
                dve.wait_ge(att_h_done, c + 1)
                order(tt(x_tok[:], bank[1][:, 0:CHUNK_BLOCKS * D].rearrange("p (j d) -> p j d", d=D),
                         per_block(rows_b[:, 4, 0:D]), ALU.add))
                dve.wait_ge(att_s_done, c + 1)
                scores = bank[5][:, 0:CHUNK_BLOCKS * SEQ].rearrange("p (j s) -> p j s", s=SEQ)
                order(vec.tensor_reduce(row_max[:], scores, AX_X, ALU.max))
                order.wait()
                tt(sc[:], scores, per_block(row_max[:]), ALU.subtract).then_inc(att_d_ready, 1)
                dve.wait_ge(att_e_ready, c + 1)
                order(vec.tensor_reduce(row_sum[:], sc_e[:], AX_X, ALU.add))
                order.wait()
                order(vec.reciprocal(row_inv[:], row_sum[:]))
                order(tt(x_tok[:], x_tok[:], per_block(row("bv")), ALU.add))
                order.wait()
                dve.wait_ge(att_o_done, c + 1)
                order(tt(res[:], bank[7][:, 0:CHUNK_BLOCKS * D].rearrange("p (j d) -> p j d", d=D),
                         per_block(row_inv[:]), ALU.mult))
                order.wait()
                order(tt(res[:], res[:], x_tok[:], ALU.add))
                normalize(c + 1, res[:], hN_chunk(c), hN_ready)

            dve.wait_ge(later_in, LATER_IN)
            dve.wait_ge(s_ready, BATCHES * 4)
            layer(attention, N_ATT, 0)

            def split_xT(done, ready, c, bank_x, xT_hl=xT_hl):
                dve.wait_ge(done, c + 1)
                order(vec.tensor_copy(xT_hl[:], bank_x[:]))
                order.wait()
                tt(xT_hl[D:P], bank_x[D:P, :], xT_hl[D:P].bitcast(F32), ALU.subtract).then_inc(ready, 1)

            def gate_max(c):
                dve.wait_ge(lg_done, c + 1)
                order(vec.tensor_copy(lg[:], bank[1][:, 0:CHUNK_BLOCKS * EXPERTS0].rearrange(
                    "p (j e) -> p j e", e=EXPERTS0)))
                order.wait()
                order(vec.tensor_reduce(top_max[:], lg[:], AX_X, ALU.max))

            def gate_top():
                for j in range(CHUNK_BLOCKS):
                    order(vec.max(top[:, j], lg[:, j]))
                order.wait()
                order(vec.memset(top[:, :, TOP0:8], BIG))

            def gate_select():
                order.wait()
                tt(sc[:], lg[:], per_block(top_max[:]), ALU.subtract).then_inc(lg_d_ready, 1)
                for j in range(CHUNK_BLOCKS):
                    order(vec.match_replace(left[:, j], top[:, j], lg[:, j], -BIG))

            def gate_mask():
                order.wait()
                order(tt(left[:], left[:], lg[:], ALU.not_equal))

            def gate_weights(c):
                order.wait()
                dve.wait_ge(lg_e_ready, c + 1)
                order(tt(left[:], left[:], sc_e[:], ALU.mult))
                order.wait()
                order(vec.tensor_reduce(row_sum[:], left[:], AX_X, ALU.add))
                order.wait()
                order(vec.reciprocal(row_inv[:], row_sum[:]))

            def gate_divide():
                order.wait()
                order(tt(w2x[:, :, 0], left[:], per_block(row_inv[:]), ALU.mult))
                tt(w2x[:, :, 1], left[:], per_block(row_inv[:]), ALU.mult).then_inc(w2_ready, 1)

            def gate_split(c, par):
                split_xT(wT_done, wT_ready, c, bank[0], lat_w_hl[par])

            def lattice_step(c, par, back, front):
                b, f = c - 1, c + 1
                for p in range(EPAIRS):
                    n = c * EPAIRS + (p + 1)
                    dve.wait_ge(bc_done, n)
                    if back or p >= 4:
                        dve.wait_ge(lat_done, n - 4)
                    tt(lat_z[p % 4], spread_ps[p % 4][:], lat_x[par], ALU.mult).then_inc(z_ready, 1)
                    if back:
                        if p == 4:
                            dve.wait_ge(proj_done, b + 1)
                            order(tt(res[:], bank[1][:, 0:CHUNK_BLOCKS * D].rearrange("p (j d) -> p j d", d=D),
                                     per_block(row("out_b")), ALU.add))
                            order.wait()
                            order(tt(res[:], res[:], hN_chunk(b), ALU.add))
                        if p == 6:
                            center(res[:])
                        if p == 7:
                            variance()
                        if p == 9:
                            normalized(b * 2 + (ATT_NORMS + 1), res[:])
                        if p == 10:
                            order.wait()
                            order(tt(res[:], res[:], per_block(row("ln_g")), ALU.mult))
                        if p == 11:
                            order.wait()
                            order(tt(res[:], res[:], per_block(row("ln_b")), ALU.add))
                        if p == 12:
                            order.wait()
                            order(tt(res[:], res[:], hN_chunk(b), ALU.add))
                        if p == 16:
                            center(res[:])
                        if p == 18:
                            variance()
                        if p == 25:
                            normalized(b * 2 + (ATT_NORMS + 2), hN_chunk(b), hN_ready)
                    if front:
                        if p == 14:
                            gate_max(f)
                        if p == 15:
                            gate_top()
                        if p == 17:
                            gate_select()
                        if p == 19:
                            gate_mask()
                        if p == 20:
                            gate_weights(f)
                        if p == 22:
                            gate_divide()
                        if p == 27:
                            gate_split(f, 1 - par)

            gate_max(0)
            gate_top()
            gate_select()
            gate_mask()
            gate_weights(0)
            gate_divide()
            gate_split(0, 0)
            dve.wait_ge(xT_ready, 1)
            lattice_step(0, 0, False, True)
            with dve.Fori(0, CHUNKS // 2 - 1) as i:
                order.enter(i, N_LAT)
                lattice_step(i * 2 + 1, 1, True, True)
                lattice_step(i * 2 + 2, 0, True, True)
            order.leave(CHUNKS // 2 - 1)
            lattice_step(CHUNKS - 1, 1, True, False)
            b = CHUNKS - 1
            dve.wait_ge(proj_done, CHUNKS)
            order(tt(res[:], bank[1][:, 0:CHUNK_BLOCKS * D].rearrange("p (j d) -> p j d", d=D),
                     per_block(row("out_b")), ALU.add))
            order.wait()
            order(tt(res[:], res[:], hN_chunk(b), ALU.add))
            normalize(b * 2 + (ATT_NORMS + 1), res[:], res[:])
            order.wait()
            order(tt(res[:], res[:], per_block(row("ln_g")), ALU.mult))
            order.wait()
            order(tt(res[:], res[:], per_block(row("ln_b")), ALU.add))
            order.wait()
            order(tt(res[:], res[:], hN_chunk(b), ALU.add))
            normalize(b * 2 + (ATT_NORMS + 2), res[:], hN_chunk(b), hN_ready)
            dve.wait_ge(hN_ready, 2 * CHUNKS)

            def tok_trig(n):
                return trig_t[:, n].unsqueeze(1).to_broadcast([P, CHUNK_BLOCKS, D])

            def feat_trig(n):
                return trig_f[:, n].unsqueeze(1).to_broadcast([P, CB, SEQ])

            def by_batch(ap):
                return ap.rearrange("p (b s) -> p b s", s=SEQ)

            def scores_max(c, j, early=False):
                dve.wait_ge(att2_s_done, c * CHUNK_BLOCKS + (j + 1))
                for half in range(2):
                    order(vec.tensor_reduce(
                        p_max[:, j % 2, half * PAIRS:(half + 1) * PAIRS],
                        bank[4 + half][:].rearrange("p (h s) -> p h s", s=SEQ), AX_X, ALU.max))
                order.wait()
                if not early:
                    dve.wait_ge(pT_done, (c * CHUNK_BLOCKS + (j - 1)) * 2)
                for half in range(2):
                    ins = tt(p_sc[:, j % 2, half * CT:(half + 1) * CT].rearrange("p (h s) -> p h s", s=SEQ),
                             bank[4 + half][:].rearrange("p (h s) -> p h s", s=SEQ),
                             p_max[:, j % 2, half * PAIRS:(half + 1) * PAIRS].unsqueeze(2).to_broadcast(
                                 [P, PAIRS, SEQ]), ALU.subtract)
                    if half == 0:
                        order(ins)
                ins.then_inc(att2_d_ready, 1)

            def softmax_sum(c, j, early=False):
                dve.wait_ge(att2_e_ready, c * CHUNK_BLOCKS + (j + 1))
                order(vec.tensor_reduce(p_sum[:, j % 2], p_sc[:, j % 2].rearrange("p (h s) -> p h s", s=SEQ),
                                        AX_X, ALU.add))
                order.wait()
                if not early:
                    dve.wait_ge(att2_p_ready, c * CHUNK_BLOCKS + (j - 1))
                vec.reciprocal(p_inv[:, j % 2], p_sum[:, j % 2]).then_inc(p_inv_ready, 1)

            def key_norm(c):
                dve.wait_ge(kn_done, c + 1)
                kk = bank[3][:].rearrange("p (j s d) -> p j s d", s=2, d=D)
                order(tt(k_t[:], kk[:, :, 0], tok_trig(0), ALU.mult))
                tt(k_s[:], kk[:, :, 1], tok_trig(1), ALU.mult).then_inc(kn_read, 1)
                order.wait()
                dve.wait_ge(kn_read, c + 1)
                order(tt(k_t[:], k_t[:], k_s[:], ALU.add))
                order.wait()
                order(tt(k_s[:], k_t[:], k_t[:], ALU.mult))
                order.wait()
                order(vec.tensor_reduce(k_var[:], k_s[:], AX_X, ALU.add))
                order.wait()
                ts(k_var[:], k_var[:], 1.0 / D, EPS_RMS, ALU.mult, ALU.add).then_inc(k_rms_in, 1)

            def key_scale(c, first=False):
                order(tt(k_t[:], k_t[:], per_block(qk_gain[:]), ALU.mult))
                order.wait()
                if not first:
                    dve.wait_ge(kT_done, c)
                dve.wait_ge(k_rms_out, c + 1)
                order(tt(w2x[:, :, 0], k_t[:], per_block(k_rms[:]), ALU.mult))
                tt(w2x[:, :, 1], k_t[:], per_block(k_rms[:]), ALU.mult).then_inc(k2_ready, 1)

            def rope(c, par, p):
                n = c * 2 * PAIRS + 2 * p
                dve.wait_ge(q_sq_ready, c * PAIRS + (p + 1))
                tt(by_batch(rope_c[:, p % 2]), by_batch(bank[1][:]), feat_trig(0),
                   ALU.mult).then_inc(q_rope_ready, 1)
                dve.wait_ge(q_done, n + 2)
                tt(by_batch(rope_s[:, p % 2]), by_batch(bank[2][:]), feat_trig(1),
                   ALU.mult).then_inc(q_rope_ready, 1)
                dve.wait_ge(q_rope_ready, n + 2)
                tt(qr[par][p], rope_c[:, p % 2], rope_s[:, p % 2],
                   ALU.add).then_inc(q_sum_ready, 1)

            def query_var(c, first=False):
                dve.wait_ge(norm_done, c + 1)
                if not first:
                    dve.wait_ge(q_rms_out, c * CHUNK_BLOCKS)
                ts(q_var[:], bank[7][:, 0:CHUNK_BLOCKS * HEADS], 1.0 / D, EPS_RMS, ALU.mult,
                   ALU.add).then_inc(q_rms_in, 1)

            def take_out(c):
                dve.wait_ge(att2_o_done, (c + 1) * CHUNK_BLOCKS)
                tt(res[:], bank[0][:, 0:CHUNK_BLOCKS * D].rearrange("p (j d) -> p j d", d=D),
                   hN_chunk(c), ALU.add).then_inc(o_read, 1)

            def finish(c):
                dve.wait_ge(o_read, c + 1)
                normalize(c + (ROT_NORMS + 1), res[:], hN_chunk(c), hN_ready)

            def chunk_step(b, prev, front, par):
                f = b + 1
                if prev:
                    softmax_sum(b - 1, 3)
                if front:
                    split_xT(gxT_done, gxT_ready, f, bank[7])
                scores_max(b, 0, not prev)
                if front:
                    rope(f, par, 0)
                    rope(f, par, 1)
                    key_norm(f)
                if prev:
                    take_out(b - 1)
                for j in (1, 2):
                    softmax_sum(b, j - 1, not prev)
                    scores_max(b, j, not prev and j == 1)
                    if front:
                        for p in PAIRS_OF_STEP[j]:
                            rope(f, par, p)
                        if j == 2:
                            key_scale(f)
                softmax_sum(b, 2)
                scores_max(b, 3)
                if front:
                    query_var(f)
                if prev:
                    finish(b - 1)

            for m in bd_store:
                ins = vec.memset(m, 0.0)
                if m is bd_store[0]:
                    order(ins)
            ins.then_inc(bd_zeroed, 1)
            split_xT(gxT_done, gxT_ready, 0, bank[7])
            key_norm_after = 1
            for p in range(PAIRS):
                rope(0, 0, p)
                if p == key_norm_after:
                    key_norm(0)
            key_scale(0, True)
            query_var(0, True)
            chunk_step(0, False, True, 1)
            with dve.Fori(0, CHUNKS // 2 - 1) as i:
                order.enter(i, N_ROT)
                chunk_step(i * 2 + 1, True, True, 0)
                chunk_step(i * 2 + 2, True, True, 1)
            order.leave(CHUNKS // 2 - 1)
            chunk_step(CHUNKS - 1, True, False, None)
            softmax_sum(CHUNKS - 1, 3)
            take_out(CHUNKS - 1)
            finish(CHUNKS - 1)
            dve.wait_ge(hN_ready, 3 * CHUNKS)

            def gelu_rows(c, n):
                normalize(n, hN_chunk(c), x_tok[:])
                order.wait()
                order(tt(x_tok[:], x_tok[:], per_block(row("gamma")), ALU.mult))
                order.wait()
                order(tt(x2[:, :, 0], x_tok[:], per_block(row("beta")), ALU.add))
                tt(x2[:, :, 1], x_tok[:], per_block(row("beta")), ALU.add).then_inc(m2_ready, 1)

            def route(c, par):
                dve.wait_ge(r_done, c + 1)
                rl = lg[:, :, 0:EXPERTS1]
                order(tt(rl, bank[1][:, 0:CHUNK_BLOCKS * EXPERTS1].rearrange("p (j e) -> p j e", e=EXPERTS1),
                         per_block(row("br", EXPERTS1), EXPERTS1), ALU.add))
                order.wait()
                order(vec.tensor_reduce(top_max[:], rl, AX_X, ALU.max))
                for j in range(CHUNK_BLOCKS):
                    order(vec.max(top[:, j], rl[:, j]))
                order.wait()
                order(vec.memset(top[:, :, 2:8], BIG))
                order.wait()
                tt(sc[:, :, 0:EXPERTS1], rl, per_block(top_max[:], EXPERTS1), ALU.subtract).then_inc(r_d_ready, 1)
                sel = left[:, :, 0:EXPERTS1]
                for j in range(CHUNK_BLOCKS):
                    order(vec.match_replace(sel[:, j], top[:, j], rl[:, j], -BIG))
                order.wait()
                order(tt(sel, sel, rl, ALU.not_equal))

            def route_weights(c, par):
                sel = left[:, :, 0:EXPERTS1]
                order.wait()
                dve.wait_ge(r_e_ready, c + 1)
                order(tt(sel, sel, sc_e[:, :, 0:EXPERTS1], ALU.mult))
                order.wait()
                order(vec.tensor_reduce(row_sum[:], sel, AX_X, ALU.add))
                order.wait()
                order(vec.reciprocal(row_inv[:], row_sum[:]))
                order.wait()
                order(tt(wf[:, par], sel, per_block(row_inv[:], EXPERTS1), ALU.mult))

            def take_outputs(c):
                dve.wait_ge(y2_done, c + 1)
                for j in range(CHUNK_BLOCKS):
                    ins = tt(moe[j], bank[4 + j][:], row("b2", EXPERTS1 * D), ALU.add)
                    if j + 1 < CHUNK_BLOCKS:
                        order(ins)
                ins.then_inc(y2_read, 1)

            def combine(c, n):
                for j in range(CHUNK_BLOCKS):
                    dve.wait_ge(moe_ready, c * CHUNK_BLOCKS + (j + 1))
                    order(vec.tensor_reduce(res[:, j], moe[j].rearrange("p (e d) -> p d e", d=D),
                                            AX_X, ALU.add))
                order.wait()
                order(tt(res[:], res[:], hN_chunk(c), ALU.add))
                normalize(n, res[:], hN_chunk(c), hN_ready)

            def gelu_step(c, par, back, front):
                if back:
                    order.wait()
                    take_outputs(c - 1)
                if front:
                    gelu_rows(c + 1, c * 2 + (GELU_NORMS + 1) if back else GELU_NORMS + 2)
                    split_xT(mT_done, mT_ready, c + 1, bank[0], mT_hl[1 - par])
                if back:
                    combine(c - 1, c * 2 + (GELU_NORMS + (2 if front else 1)))
                if front:
                    route(c + 1, 1 - par)
                    route_weights(c + 1, 1 - par)

            gelu_rows(0, GELU_NORMS + 1)
            split_xT(mT_done, mT_ready, 0, bank[0], mT_hl[0])
            route(0, 0)
            route_weights(0, 0)
            gelu_step(0, 0, False, True)
            with dve.Fori(0, CHUNKS // 2 - 1) as i:
                order.enter(i, N_GELU)
                gelu_step(i * 2 + 1, 1, True, True)
                gelu_step(i * 2 + 2, 0, True, True)
            order.leave(CHUNKS // 2 - 1)
            gelu_step(CHUNKS - 1, 1, True, False)
            take_outputs(CHUNKS - 1)
            combine(CHUNKS - 1, 2 * CHUNKS + GELU_NORMS)


def _layout(inputs):
    import numpy as np
    f = {k: np.asarray(v) for k, v in inputs.items()}
    a = {}
    a["x"] = f["x"].reshape(TOKENS, V, C0).transpose(1, 0, 2).reshape(V, TOKENS * C0)
    a["ident"] = np.eye(P, dtype=np.float32)
    cols = np.zeros((P, 16), np.float32)
    for layer in range(2):
        for n, name in enumerate(("b", "g", "be", "m", "v")):
            cols[:, 5 * layer + n] = f[f"L0_tok_{name}{layer}"]
    cols[BIAS_ROW, 10] = cols[ROWS + BIAS_ROW, 10] = 1.0
    a["cols"] = cols
    cols64 = np.zeros((P, 8), np.float32)
    for n, name in enumerate(("b", "g", "be", "m", "v")):
        cols64[0:D, n] = f[f"L0_tok_{name}2"]
    cols64[0:D, 5], cols64[0:D, 6] = f["L0_attn_bq"], f["L0_attn_bk"]
    a["cols64"] = cols64
    a["A"] = f["L0_tok_A"]
    a["AT"] = np.zeros((P, V), np.float32)
    a["AT"][0:V] = f["L0_tok_A"].T
    w0 = np.zeros((P // ROWS, ROWS, GROUP, CH), np.float32)
    for j in range(GROUP):
        w0[:, C0 * j:C0 * (j + 1), j] = f["L0_tok_W0"]
    a["w0_blocks"] = w0.reshape(P, GROUP * CH)
    a["W1"], a["W2"] = f["L0_tok_W1"], f["L0_tok_W2"]
    rowv = np.concatenate([f["L0_attn_bv"], f["L0_ffn_out_b"], f["L0_ffn_ln_g"], f["L0_ffn_ln_b"],
                           f["L1_attn_q_norm_w"], f["L1_attn_k_norm_w"], f["L1_ffn_gamma"],
                           f["L1_ffn_beta"], f["L1_ffn_b2"].reshape(-1), f["L1_ffn_br"]])
    a["rows"] = rowv.reshape(ROW_WIDTH)
    a["att_w"] = np.concatenate([f["L0_attn_Wq"], f["L0_attn_Wk"], f["L0_attn_Wv"]], 1)
    a["gate_wT"] = f["L0_ffn_gate_w"].T
    a["lat_w"] = f["L0_ffn_lattice_weights"].reshape(EXPERTS0 // 2, 2 * D, D).transpose(1, 0, 2)
    a["out_wT"] = f["L0_ffn_out_w"].T
    a["ident2"] = np.concatenate([np.eye(D, dtype=np.float32)] * 2, 0)
    swap = np.arange(D).reshape(D // 2, 2)[:, ::-1].reshape(-1)
    wqT = f["L1_attn_wq"].T.reshape(D, HEADS, D)
    q_w = np.stack([wqT.reshape(D, -1), wqT[:, :, swap].reshape(D, -1)], 1)
    a["q_w"] = np.concatenate([q_w, q_w], 0)
    wkT, wvT = f["L1_attn_wkv"][0:D].T, f["L1_attn_wkv"][D:].T
    kv = np.concatenate([wkT, wkT[:, swap], wvT, wvT], 1)
    a["kv_w"] = np.concatenate([kv, kv], 0)
    a["wo_w"] = f["L1_attn_wo"].reshape(D, PAIRS, 2, D).transpose(2, 3, 1, 0).reshape(P, PAIRS, D)
    freqs = np.float32(10000.0) ** (np.float32(-2.0) * np.arange(D // 2, dtype=np.float32) / np.float32(D))
    theta = np.arange(SEQ, dtype=np.float32)[:, None] * freqs[None, :].astype(np.float32)
    cos = np.repeat(np.cos(theta), 2, axis=1).astype(np.float32)
    sin = np.repeat(np.sin(theta), 2, axis=1).astype(np.float32)
    sin[:, 0::2] *= -1
    a["trig_f"] = np.concatenate([np.stack([cos.T, sin.T], 1)] * 2, 0)
    a["trig_t"] = np.concatenate([np.stack([cos, sin], 1)] * 2, 0)
    head_of = np.zeros((P, 2), np.float32)
    head_of[0:D, 0] = head_of[D:P, 1] = 1.0
    a["head_of"] = head_of
    above = np.where(np.arange(SEQ)[None, :] > np.arange(SEQ)[:, None], MASKED, 0.0).astype(np.float32)
    a["mask"] = np.tile(above, (2, CT // SEQ))
    twice = lambda m: np.concatenate([m, m], 0)
    a["r_w"] = twice(f["L1_ffn_Wr"])
    a["e1_w"] = twice(f["L1_ffn_W1"].transpose(1, 0, 2).reshape(D, EXPERTS1 * HID1))
    a["e1_b"] = f["L1_ffn_b1"].T
    a["e2_w"] = f["L1_ffn_W2"].transpose(1, 0, 2)
    return {k: np.ascontiguousarray(v) for k, v in a.items()}

def kernel(**inputs):
    import numpy as _np
    import concourse.bacc as _bacc
    from concourse import mybir as _mybir
    from concourse.bass_utils import run_bass_kernel_spmd as _run

    nc = _bacc.Bacc("TRN2", target_bir_lowering=False, num_devices=1)
    arrays, args = {}, {}
    for name, a in _layout(inputs).items():
        arrays[f"in_{name}_dram"] = a
        args[name] = nc.dram_tensor(f"in_{name}_dram", a.shape, _mybir.dt.from_np(a.dtype),
                                    kind="ExternalInput").ap()
    args["out"] = nc.dram_tensor("out_0_dram", (P, BLOCKS, D), _mybir.dt.float32,
                                 kind="ExternalOutput").ap()
    build(nc, args)
    r = _run(nc, [arrays], core_ids=[0])
    got = _np.asarray(r.results[0]["out_0_dram"])
    return got.transpose(1, 0, 2).reshape(BATCHES, SEQ, D)
```

```python
from contextlib import ExitStack

import concourse.bass as bass
from concourse import mybir

F32 = mybir.dt.float32
F32R = mybir.dt.float32r
BF16 = mybir.dt.bfloat16
ALU = mybir.AluOpType
ACT = mybir.ActivationFunctionType
AX_X = mybir.AxisListType.X

P = 128
BATCHES = 64
SEQ = 64
TOKENS = BATCHES * SEQ
V = 75
C0 = 3
CH = 128
D = 64
EPS_BN = 1e-5

NODES_INV = 1.0 / V
EPS_LN = 1e-5
EPS_RMS = 1.1920929e-07
CHUNK_BLOCKS = 4
BLOCKS = TOKENS // P
CHUNKS = BLOCKS // CHUNK_BLOCKS
CT = CHUNK_BLOCKS * P
CB = CT // SEQ
EXPERTS0 = 64
TOP0 = 6
HEADS = 16
PAIRS = HEADS // 2
EXPERTS1 = 8
HID1 = 128
BIG = 3.0e38
MASKED = -1.0e30

UNIT = 4
GROUP = 8
ITER = 32
UNITS = SEQ // UNIT
ROWS = 32
BIAS_ROW = GROUP * C0


N_ATT, N_LAT, N_ROT, N_GELU = 10, 64, 56, 76


class Chain:

    def __init__(self, eng, sem):
        self.eng, self.sem, self.base, self.trip, self.k = eng, sem, 0, 0, 0

    def enter(self, i, per_trip):
        self.base, self.trip, self.k, self.per = self.base + self.k, i * per_trip, 0, per_trip

    def leave(self, trips):
        assert self.k == self.per, (self.k, self.per)
        self.base, self.trip, self.k = self.base + trips * self.per, 0, 0

    def __call__(self, ins):
        ins.then_inc(self.sem, 1)
        self.k += 1
        return self.trip + (self.base + self.k)

    def wait(self, mark=None):
        self.eng.wait_ge(self.sem, self.trip + (self.base + self.k) if mark is None else mark)


ROW_NAMES = ("bv", "out_b", "ln_g", "ln_b", "q_norm", "k_norm", "gamma", "beta")
ROW_AT = {name: n * D for n, name in enumerate(ROW_NAMES)}
ROW_AT["b2"] = len(ROW_NAMES) * D
ROW_AT["br"] = ROW_AT["b2"] + EXPERTS1 * D
ROW_WIDTH = ROW_AT["br"] + EXPERTS1


def build(nc, t):
    with ExitStack() as ctx:
        def sb(name, shape, dt=F32):
            return ctx.enter_context(nc.sbuf_tensor(name, shape, dt))

        def sem(name):
            return ctx.enter_context(nc.semaphore(name))

        bank = [ctx.enter_context(nc.psum_tensor(f"bank{i}", [P, 512], F32)) for i in range(8)]

        ident = sb("ident", [P, P])
        cols = sb("cols", [P, 16])
        cols64 = sb("cols64", [P, 8])
        AT = sb("AT", [P, V])
        A_nat = sb("A_nat", [V, V])
        ones = sb("ones", [P, P])
        w0_hl = sb("w0_hl", [P, GROUP * CH], F32R)
        w1_raw = sb("w1_raw", [CH, CH])
        w1_s = sb("w1_s", [CH, CH])
        w2_raw = sb("w2_raw", [CH, D])
        w2_s = sb("w2_s", [CH, D])
        half_neg = sb("half_neg", [P, 64])
        bn_scale = sb("bn_scale", [P, 4])
        bn_bias = sb("bn_bias", [P, 4])
        bn_tmp = sb("bn_tmp", [P, 4])
        act_first = sb("act_first", [P, 1])
        neg_b1 = sb("neg_b1", [P, 1])
        diag = sb("diag", [P, 5, P])
        rows_b = sb("rows_b", [P, 5, P])
        abar = sb("abar", [P, V])
        a_sum = sb("a_sum", [P, 1])
        s_corr = sb("s_corr", [P, 1])

        x_t = sb("x_t", [V, 2, ITER * C0])
        x_rep = sb("x_rep", [V, 2, ITER // GROUP, 2, ROWS])
        y_hl = sb("y_hl", [P, 2, ITER // GROUP, V], F32R)
        h0_sb = sb("h0_sb", [P, 2, UNIT * CH])
        ah_sb = sb("ah_sb", [CH, 2, UNIT * V])
        prod_bd = sb("prod_bd", [P, 2 * 4 * UNIT * V])
        prod = prod_bd[:].rearrange("p (s q n) -> p s q n", s=2, q=4)
        sT = sb("sT", [CH, TOKENS])


        rows = sb("rows", [P, ROW_WIDTH])
        att_w = sb("att_w", [D, 3 * D])
        gate_wT = sb("gate_wT", [D, EXPERTS0])
        lat_w = sb("lat_w", [P, EXPERTS0 // 2, D])
        out_wT = sb("out_wT", [D, D])
        pick = sb("pick", [P, EXPERTS0, D], F32R)
        ident2 = sb("ident2", [P, D])
        q_wh = sb("q_wh", [P, 2, HEADS * D], F32R)
        q_wl = sb("q_wl", [P, 2, HEADS * D], F32R)
        kv_w = sb("kv_w", [P, 4 * D])
        kv_wh = sb("kv_wh", [P, 4 * D], F32R)
        kv_wl = sb("kv_wl", [P, 4 * D], F32R)
        wo_w = sb("wo_w", [P, PAIRS, D])
        trig_f = sb("trig_f", [P, 2, SEQ])
        trig_t = sb("trig_t", [P, 2, D])
        qk_gain = sb("qk_gain", [P, D])
        head_of = sb("head_of", [P, 2])
        ident_bf = sb("ident_bf", [P, P], BF16)
        mask_bf = sb("mask_bf", [P, CT], BF16)
        mask_in = sb("mask_in", [P, CT])
        r_w = sb("r_w", [P, EXPERTS1])
        r_wh = sb("r_wh", [P, EXPERTS1], F32R)
        r_wl = sb("r_wl", [P, EXPERTS1], F32R)
        e1_wh = sb("e1_wh", [P, EXPERTS1 * HID1], F32R)
        e1_wl = sb("e1_wl", [P, EXPERTS1 * HID1], F32R)
        e1_b = sb("e1_b", [P, EXPERTS1])
        e2_w = sb("e2_w", [P, EXPERTS1, D])

        hN = sb("hN", [P, BLOCKS, D])
        s_chunk = sb("s_chunk", [CH, CT])
        hT = sb("hT", [D, CT])
        x_tok = sb("x_tok", [P, CHUNK_BLOCKS, D])
        qT = sb("qT", [D, CT])
        kT = sb("kT", [D, CT])
        v_sb = sb("v_sb", [SEQ, CB, D])
        xc = sb("xc", [P, CHUNK_BLOCKS, D])
        xsq = sb("xsq", [P, CHUNK_BLOCKS, D])
        res = sb("res", [P, CHUNK_BLOCKS, D])
        ln_mean = sb("ln_mean", [P, CHUNK_BLOCKS])
        ln_var = sb("ln_var", [P, CHUNK_BLOCKS])
        ln_rstd = sb("ln_rstd", [P, CHUNK_BLOCKS])
        row_max = sb("row_max", [P, CHUNK_BLOCKS])
        row_sum = sb("row_sum", [P, CHUNK_BLOCKS])
        row_inv = sb("row_inv", [P, CHUNK_BLOCKS])
        sc = sb("sc", [P, CHUNK_BLOCKS, D])
        sc_e = sb("sc_e", [P, CHUNK_BLOCKS, D])
        eT = sb("eT", [SEQ, CHUNK_BLOCKS, P])
        x2 = sb("x2", [P, CHUNK_BLOCKS, 2, D])
        xT2 = sb("xT2", [P, CT])
        lg = sb("lg", [P, CHUNK_BLOCKS, EXPERTS0])
        top = sb("top", [P, CHUNK_BLOCKS, 8])
        top_max = sb("top_max", [P, CHUNK_BLOCKS])
        left = sb("left", [P, CHUNK_BLOCKS, EXPERTS0])
        w2x = sb("w2x", [P, CHUNK_BLOCKS, 2, EXPERTS0])
        wT_hl = sb("wT_hl", [P, CT], F32R)
        zT = sb("zT", [P, 2, CT])
        latT = sb("latT", [P, CT])
        xT_hl = sb("xT_hl", [P, CT], F32R)
        rope_c = zT
        rope_s = sb("rope_s", [P, 2, CT])
        q_sq = sb("q_sq", [P, 2, CT])
        qr = [[sT[:, p * CT:(p + 1) * CT] for p in range(PAIRS)],
              [h0_sb[:, 0], h0_sb[:, 1], s_chunk[:], ah_sb[:].rearrange("p s n -> p (s n)")[:, 0:CT],
               diag[:, 0:4].rearrange("p a b -> p (a b)"), rows_b[:, 0:4].rearrange("p a b -> p (a b)"),
               mask_in[:], latT[:]]]
        k_t = sb("k_t", [P, CHUNK_BLOCKS, D])
        k_s = sb("k_s", [P, CHUNK_BLOCKS, D])
        k_var = sb("k_var", [P, CHUNK_BLOCKS])
        k_rms = sb("k_rms", [P, CHUNK_BLOCKS])
        q_var = sb("q_var", [P, CHUNK_BLOCKS * HEADS])
        q_rms = sb("q_rms", [P, CHUNK_BLOCKS * HEADS])
        bd_store = [prod_bd[:, 0:4 * CT], lat_w[:].rearrange("p a d -> p (a d)")]
        k_bd = [m[:, 0:2 * CT].rearrange("p (b h s) -> p b h s", b=CB, h=2) for m in bd_store]
        v_bd = [m[:, 2 * CT:4 * CT].rearrange("p (b h s) -> p b h s", b=CB, h=2) for m in bd_store]
        vw = sb("vw", [P, CB, PAIRS * D])
        q_w = vw[:, 0:4, :].rearrange("p b n -> p (b n)").rearrange("p (s n) -> p s n", s=2)
        e1_w = vw[:, 4:6, :].rearrange("p b n -> p (b n)")
        p_max = sb("p_max", [P, 2, HEADS])
        p_sum = sb("p_sum", [P, 2, HEADS])
        p_inv = sb("p_inv", [P, 2, HEADS])
        p_sc = sb("p_sc", [P, 2, HEADS * SEQ])
        w0_tmp = p_sc[:, 0, :]
        pT = sb("pT", [P, 2, PAIRS * P])
        w0_raw = pT[:, 0, :]
        hid = rope_s
        wf = sb("wf", [P, 2, CHUNK_BLOCKS, EXPERTS1])
        mT_hl = [xT_hl, wT_hl]
        lat_x = [xT2[:], rope_s[:, 0]]
        lat_w_hl = [wT_hl, xT_hl]
        lat_z = [zT[:, 0], zT[:, 1], q_sq[:, 0], q_sq[:, 1]]
        spread_ps = [bank[2], bank[3], bank[4], bank[7]]
        lat_ps = [bank[5], bank[6]]
        moe = [q_sq[:, 0], q_sq[:, 1], zT[:, 0], zT[:, 1]]

        y_ps = bank[0]
        h0_ps = [bank[1], bank[2]]
        ah_ps = [bank[3], bank[4]]
        z_ps = [bank[5], bank[6]]
        mix_ps = bank[7]

        consts_in = sem("consts_in")
        x_in = [sem("x_in0"), sem("x_in1")]
        pool_order, dve_order, act_order = sem("pool_order"), sem("dve_order"), sem("act_order")
        pe_gate, pool_gate = sem("pe_gate"), sem("pool_gate")
        ones_set = sem("ones_set")
        bn_var = sem("bn_var")
        bn_rsqrt = sem("bn_rsqrt")
        diag_ready = sem("diag_ready")
        rows_done = sem("rows_done")
        abar_done = sem("abar_done")
        weights_ready = sem("weights_ready")
        w1_ready = sem("w1_ready")
        h0_zeroed = sem("h0_zeroed")
        x_copied = sem("x_copied")
        y_done = sem("y_done")
        y_high = sem("y_high")
        y_ready = sem("y_ready")
        l0_done = sem("l0_done")
        h0_ready = sem("h0_ready")
        amix_done = sem("amix_done")
        ah_ready = sem("ah_ready")
        z_done = sem("z_done")
        prod_done = sem("prod_done")
        s_ready = sem("s_ready")
        out_sem = sem("out_sem")
        later_in = sem("later_in")
        pick_ready = sem("pick_ready")
        splits_ready = sem("splits_ready")
        sT_copied = sem("sT_copied")
        att_h_done = sem("att_h_done")
        att_hT_ready = sem("att_hT_ready")
        att_hT_done = sem("att_hT_done")
        att_qk_done = sem("att_qk_done")
        att_v_done = sem("att_v_done")
        att_x_read = sem("att_x_read")
        att_o_read = sem("att_o_read")
        att_qk_ready = sem("att_qk_ready")
        att_v_ready = sem("att_v_ready")
        att_s_done = sem("att_s_done")
        att_d_ready = sem("att_d_ready")
        att_e_ready = sem("att_e_ready")
        att_eT_done = sem("att_eT_done")
        att_eT_ready = sem("att_eT_ready")
        att_o_done = sem("att_o_done")
        ln_var_ready = sem("ln_var_ready")
        ln_rstd_ready = sem("ln_rstd_ready")
        hN_ready = sem("hN_ready")
        x2_ready = sem("x2_ready")
        xT_done = sem("xT_done")
        xT_ready = sem("xT_ready")
        lg_done = sem("lg_done")
        lg_d_ready = sem("lg_d_ready")
        lg_e_ready = sem("lg_e_ready")
        w2_ready = sem("w2_ready")
        wT_done = sem("wT_done")
        wT_ready = sem("wT_ready")
        bc_done = sem("bc_done")
        z_ready = sem("z_ready")
        lat_done = sem("lat_done")
        latT_ready = sem("latT_ready")
        proj_done = sem("proj_done")
        proj_read = sem("proj_read")
        gx2_ready = sem("gx2_ready")
        gxT_done = sem("gxT_done")
        gxT_ready = sem("gxT_ready")
        kn_done = sem("kn_done")
        kn_read = sem("kn_read")
        bd_zeroed = sem("bd_zeroed")
        p_inv_ready = sem("p_inv_ready")
        o_read = sem("o_read")
        k_rms_in = sem("k_rms_in")
        k_rms_out = sem("k_rms_out")
        k2_ready = sem("k2_ready")
        kT_done = sem("kT_done")
        kbd_ready = sem("kbd_ready")
        vT_done = sem("vT_done")
        vbd_ready = sem("vbd_ready")
        q_done = sem("q_done")
        q_rope_ready = sem("q_rope_ready")
        q_sq_ready = sem("q_sq_ready")
        norm_done = sem("norm_done")
        q_rms_in = sem("q_rms_in")
        q_rms_out = sem("q_rms_out")
        vw_done = sem("vw_done")
        vw_ready = sem("vw_ready")
        att2_s_done = sem("att2_s_done")
        att2_d_ready = sem("att2_d_ready")
        att2_dr_ready = sem("att2_dr_ready")
        att2_e_ready = sem("att2_e_ready")
        att2_p_ready = sem("att2_p_ready")
        pT_done = sem("pT_done")
        pT_ready = sem("pT_ready")
        att2_o_done = sem("att2_o_done")
        m2_ready = sem("m2_ready")
        mT_done = sem("mT_done")
        mT_ready = sem("mT_ready")
        r_done = sem("r_done")
        r_d_ready = sem("r_d_ready")
        r_e_ready = sem("r_e_ready")
        h1_done = sem("h1_done")
        h1_ready = sem("h1_ready")
        y2_done = sem("y2_done")
        y2_read = sem("y2_read")
        moe_ready = sem("moe_ready")
        q_sum_ready = sem("q_sum_ready")

        LATER = [("att_w", att_w[:]), ("gate_wT", gate_wT[:]), ("lat_w", lat_w[:]),
                 ("out_wT", out_wT[:]), ("ident2", ident2[:]), ("q_w", q_w), ("kv_w", kv_w[:]),
                 ("wo_w", wo_w[:]), ("trig_f", trig_f[:]), ("trig_t", trig_t[:]),
                 ("head_of", head_of[:]), ("mask", mask_in[:]), ("r_w", r_w[:]), ("e1_w", e1_w),
                 ("e1_b", e1_b[:]), ("e2_w", e2_w[:])]

        LATER_IN = 16 * (len(LATER) + 1)

        CONSTS = [("ident", ident[:]), ("cols", cols[:]), ("cols64", cols64[:]), ("AT", AT[:]),
                  ("A", A_nat[:]), ("w0_blocks", w0_raw), ("W1", w1_raw[:]), ("W2", w2_raw[:])]

        LAYER_STEPS = 3
        ATT_NORMS, ROT_NORMS, GELU_NORMS = CHUNKS, 3 * CHUNKS, 4 * CHUNKS
        EPAIRS = EXPERTS0 // 2
        block = ctx.enter_context(nc.Block())

        def values_bank(b2):
            return bank[2] if b2 == CB - 1 else bank[3]

        def weights_bank(j, half):
            return bank[1] if j == CHUNK_BLOCKS - 2 and half == 1 else bank[6]

        def flat(ap):
            return ap.rearrange("p a b -> p (a b)")

        def per_block(ap, width=D):
            if ap.shape[1] == CHUNK_BLOCKS and width != CHUNK_BLOCKS:
                return ap.unsqueeze(2).to_broadcast([P, CHUNK_BLOCKS, width])
            return ap.unsqueeze(1).to_broadcast([P, CHUNK_BLOCKS, width])

        def row(name, width=D):
            return rows[:, ROW_AT[name]:ROW_AT[name] + width]

        def hN_chunk(c):
            return hN[:, bass.ds(c * CHUNK_BLOCKS, CHUNK_BLOCKS), :]

        @block.sync
        def _(sp):
            for name, tile in CONSTS:
                sp.dma_start(tile, t[name]).then_inc(consts_in, 16)

            def load_x(b, par):
                sp.dma_start(x_t[:, par], t["x"][:, bass.ds((b * 2 + par) * (ITER * C0), ITER * C0)]
                             ).then_inc(x_in[par], 16)

            load_x(0, 0)
            load_x(0, 1)
            sp.dma_start(rows[:], t["rows"].partition_broadcast(P)).then_inc(later_in, 16)
            for name, tile in LATER:
                sp.dma_start(tile, t[name]).then_inc(later_in, 16)
            with sp.Fori(1, BATCHES) as b:
                for par in range(2):
                    sp.wait_ge(x_copied, b * 2 + (par - 1))
                    load_x(b, par)
            for n in range(CHUNKS):
                sp.wait_ge(hN_ready, LAYER_STEPS * CHUNKS + n + 1)
                blocks = slice(n * CHUNK_BLOCKS, (n + 1) * CHUNK_BLOCKS)
                sp.dma_start(t["out"][:, blocks], hN[:, blocks]).then_inc(out_sem, 16)
            sp.wait_ge(out_sem, CHUNKS * 16)

        @block.gpsimd
        def _(pool):
            order = Chain(pool, pool_order)
            pool.memset(ones[:], 1.0).then_inc(ones_set, 1)
            order(pool.memset(half_neg[:], -0.5))
            order(pool.memset(x_rep[:], 0.0))
            pool.memset(h0_sb[:], 0.0).then_inc(h0_zeroed, 1)

            def copy_x(b, par, first):
                pool.wait_ge(x_in[par], b * 16 + 16)
                if not first:
                    pool.wait_ge(y_done, b * 2 + (par - 1))
                    pool.sem_inc(pool_gate, 1)
                for g in range(ITER // GROUP):
                    ins = pool.tensor_copy(
                        x_rep[:, par, g, :, 0:GROUP * C0],
                        x_t[:, par, g * GROUP * C0:(g + 1) * GROUP * C0].unsqueeze(1).to_broadcast(
                            [V, 2, GROUP * C0]))
                ins.then_inc(x_copied, 1)

            pool.wait_ge(bn_var, 1)
            order.wait()
            pool.tensor_tensor(bn_scale[:, 0:3], bn_tmp[:, 0:3], half_neg[:, 0:3],
                               ALU.pow).then_inc(bn_rsqrt, 1)
            copy_x(0, 0, True)
            copy_x(0, 1, True)
            copy_x(1, 0, False)
            copy_x(1, 1, False)
            pool.wait_ge(later_in, LATER_IN)
            pool.tensor_copy(pick[:], ident2[:].unsqueeze(2).to_broadcast([P, EXPERTS0, D])).then_inc(pick_ready, 1)
            copy_x(2, 0, False)
            copy_x(2, 1, False)
            order(pool.tensor_copy(ident_bf[:], ident[:]))
            order(pool.tensor_copy(mask_bf[:], mask_in[:]))
            order(pool.tensor_scalar(qk_gain[:], row("q_norm"), D ** -0.5, None, ALU.mult))
            order.wait()
            order(pool.tensor_tensor(qk_gain[:], qk_gain[:], row("k_norm"), ALU.mult))
            splits = ((q_wh[:], q_wl[:], q_w), (kv_wh[:], kv_wl[:], kv_w[:]),
                      (r_wh[:], r_wl[:], r_w[:]), (e1_wh[:], e1_wl[:], e1_w))
            for n, (high, low, raw) in enumerate(splits):
                copy_x(n + 3, 0, False)
                copy_x(n + 3, 1, False)
                order(pool.tensor_copy(high, raw))
                order.wait()
                pool.tensor_tensor(low, raw, high.bitcast(F32), ALU.subtract).then_inc(splits_ready, 1)
            with pool.Fori(len(splits) + 3, BATCHES) as b:
                copy_x(b, 0, False)
                copy_x(b, 1, False)

            def ln_root(n):
                pool.wait_ge(ln_var_ready, n)
                pool.tensor_tensor(ln_rstd[:], ln_var[:], half_neg[:, 0:CHUNK_BLOCKS],
                                   ALU.pow).then_inc(ln_rstd_ready, 1)

            with pool.Fori(0, CHUNKS) as c:
                ln_root(c + 1)
            pool.wait_ge(s_ready, BATCHES * 4)
            pool.memset(bd_store[0], 0.0).then_inc(bd_zeroed, 1)
            with pool.Fori(0, CHUNKS - 1) as c:
                ln_root(c * 2 + (ATT_NORMS + 1))
                ln_root(c * 2 + (ATT_NORMS + 2))
            pool.wait_ge(lat_done, CHUNKS * EPAIRS)
            pool.memset(bd_store[1], 0.0).then_inc(bd_zeroed, 1)
            ln_root(ROT_NORMS - 1)

            def heads(j):
                return p_sc[:, j % 2].rearrange("p (h s) -> p h s", s=SEQ)

            def over_keys(ap):
                return ap.unsqueeze(2).to_broadcast([P, HEADS, SEQ])

            def q_root(c, j, first):
                if j == 0:
                    pool.wait_ge(q_rms_in, c + 1)
                if not first:
                    pool.wait_ge(att2_dr_ready, c * CHUNK_BLOCKS + (j - CHUNK_BLOCKS + 1))
                at = slice(j * HEADS, (j + 1) * HEADS)
                pool.tensor_tensor(q_rms[:, at], q_var[:, at], half_neg[:, 0:HEADS],
                                   ALU.pow).then_inc(q_rms_out, 1)

            def k_root(c):
                pool.wait_ge(k_rms_in, c + 1)
                pool.tensor_tensor(k_rms[:], k_var[:], half_neg[:, 0:CHUNK_BLOCKS],
                                   ALU.pow).then_inc(k_rms_out, 1)

            def scale(c, j):
                pool.wait_ge(q_rms_out, c * CHUNK_BLOCKS + (j + 1))
                pool.wait_ge(att2_d_ready, c * CHUNK_BLOCKS + (j + 1))
                pool.tensor_tensor(heads(j), heads(j), over_keys(q_rms[:, j * HEADS:(j + 1) * HEADS]),
                                   ALU.mult).then_inc(att2_dr_ready, 1)

            def softmax_divide(c, j):
                pool.wait_ge(p_inv_ready, c * CHUNK_BLOCKS + (j + 1))
                pool.tensor_tensor(heads(j), heads(j), over_keys(p_inv[:, j % 2]),
                                   ALU.mult).then_inc(att2_p_ready, 1)

            def chunk_step(b, prev, front):
                f = b + 1
                for j in range(CHUNK_BLOCKS):
                    if j > 0:
                        softmax_divide(b, j - 1)
                    elif prev:
                        softmax_divide(b - 1, CHUNK_BLOCKS - 1)
                    scale(b, j)
                    if front and j == 1:
                        k_root(f)
                    if j + 1 < CHUNK_BLOCKS:
                        q_root(b, j + 1, not prev)
                    if j == 2 and prev:
                        ln_root(b + ROT_NORMS)
                if front:
                    q_root(f, 0, False)

            k_root(0)
            ln_root(ROT_NORMS)
            q_root(0, 0, True)
            chunk_step(0, False, True)
            with pool.Fori(1, CHUNKS - 1) as c:
                chunk_step(c, True, True)
            chunk_step(CHUNKS - 1, True, False)
            ln_root(GELU_NORMS)
            softmax_divide(CHUNKS - 1, CHUNK_BLOCKS - 1)
            ln_root(GELU_NORMS + 1)

            def gelu_step(c, par, back, front):
                if front:
                    ln_root(c * 2 + (GELU_NORMS + 1) if back else GELU_NORMS + 2)
                if back:
                    ln_root(c * 2 + (GELU_NORMS + (2 if front else 1)))
                pool.wait_ge(y2_read, c + 1)
                for j in range(CHUNK_BLOCKS):
                    m = moe[j].rearrange("p (e d) -> p e d", d=D)
                    pool.tensor_tensor(m, m, wf[:, par, j].unsqueeze(2).to_broadcast(
                        [P, EXPERTS1, D]), ALU.mult).then_inc(moe_ready, 1)

            gelu_step(0, 0, False, True)
            with pool.Fori(0, CHUNKS // 2 - 1) as i:
                gelu_step(i * 2 + 1, 1, True, True)
                gelu_step(i * 2 + 2, 0, True, True)
            gelu_step(CHUNKS - 1, 1, True, False)
            ln_root(2 * CHUNKS + GELU_NORMS)

        @block.tensor
        def _(pe):
            pe.wait_ge(ones_set, 1)
            pe.wait_ge(diag_ready, 1)
            nc.tensor.matmul(mix_ps[:, 0:512], ones[:], diag[:, 0:4].rearrange("p a b -> p (a b)"),
                             start=True, stop=True)
            nc.tensor.matmul(z_ps[0][:, 0:P], ones[:], diag[:, 4],
                             start=True, stop=True).then_inc(rows_done, 1)
            nc.tensor.matmul(z_ps[1][:, 0:V], ones[0:V, :], A_nat[:], start=True,
                             stop=True).then_inc(abar_done, 1)

            def y_product(b, par):
                pe.wait_ge(x_copied, b * 2 + (par + 1))
                for g in range(ITER // GROUP):
                    ins = nc.tensor.matmul(
                        y_ps[0:2 * ROWS, g * V:(g + 1) * V],
                        x_rep[:, par, g].rearrange("v q r -> v (q r)"),
                        AT[0:V, :], start=(g == 0), stop=True, skip_group_check=True)
                ins.then_inc(y_done, 1)

            def layer0(k):
                par, g, half = (k // 8) % 2, (k % 8) // 2, k % 2
                nc.tensor.matmul(h0_ps[k % 2][0:V, :], y_hl[:, par, g, :],
                                 w0_hl[:, half * 512:(half + 1) * 512],
                                 start=True, stop=True).then_inc(l0_done, 1)

            def node_mix(k, lo, hi):
                for j in range(lo, hi):
                    ins = nc.tensor.matmul(ah_ps[k % 2][:, j * V:(j + 1) * V],
                                           h0_sb[:, k % 2, j * CH:(j + 1) * CH], AT[:],
                                           start=(j == 0), stop=True, skip_group_check=True)
                return ins

            def layer1(k, count):
                pe.wait_ge(ah_ready, count)
                nc.tensor.matmul(z_ps[k % 2][:, 0:UNIT * V], w1_s[:], ah_sb[:, k % 2, :],
                                 start=True, stop=True).then_inc(z_done, 1)

            def norms(p):
                for j in range(CHUNK_BLOCKS):
                    at = j * HEADS + 2 * p
                    ins = nc.tensor.matmul(bank[7][:, at:at + 2], q_sq[:, p % 2, j * P:(j + 1) * P],
                                           head_of[:], start=(p == 0 and j == 0), stop=True,
                                           skip_group_check=True)
                return ins

            def batch(b, first, last):
                for k in range(UNITS):
                    u = b * UNITS + k
                    pe.wait_ge(h0_ready, u + 1)
                    node_mix(k, 0, 2)
                    if not (last and k == UNITS - 1):
                        if k % 8 == 7:
                            pe.wait_ge(y_ready, b * 2 + (k // 8 + 2))
                        layer0((k + 1) % UNITS)
                    node_mix(k, 2, UNIT).then_inc(amix_done, 1)
                    if k == 2:
                        y_product(b, 1)
                    if k == 10 and not last:
                        y_product(b + 1, 0)
                    if first and k == 1:
                        pe.wait_ge(w1_ready, 1)
                    if not (first and k == 0):
                        if not (first and k < 3):
                            pe.wait_ge(prod_done, u - 2)
                        layer1((k - 1) % UNITS, u)

            y_product(0, 0)
            pe.wait_ge(weights_ready, 1)
            pe.wait_ge(y_ready, 1)
            layer0(0)
            batch(0, True, False)
            with pe.Fori(1, BATCHES - 1) as b:
                batch(b, False, False)
            batch(BATCHES - 1, False, True)
            pe.wait_ge(prod_done, BATCHES * UNITS - 2)
            layer1(UNITS - 1, BATCHES * UNITS)

            pe.wait_ge(later_in, LATER_IN)
            pe.wait_ge(pick_ready, 1)
            pe.wait_ge(splits_ready, 4)
            mm = nc.tensor.matmul

            def tokens_T(c):
                pe.wait_ge(sT_copied, c + 1)
                mm(bank[0][0:D, :], w2_s[:], s_chunk[:], start=True, stop=True).then_inc(att_hT_done, 1)

            def queries_keys(c):
                pe.wait_ge(att_hT_ready, c + 1)
                pe.sem_inc(pe_gate, 1)
                mm(bank[2][0:D, :], att_w[:, 0:D], hT[:], start=True, stop=True)
                mm(bank[3][0:D, :], att_w[:, D:2 * D], hT[:], start=True, stop=True).then_inc(att_qk_done, 1)

            def tokens_values(c):
                for j in range(CHUNK_BLOCKS):
                    ins = mm(bank[1][:, j * D:(j + 1) * D], s_chunk[:, j * P:(j + 1) * P], w2_s[:],
                             start=(j == 0), stop=True, skip_group_check=True)
                ins.then_inc(att_h_done, 1)
                for b2 in range(CB):
                    ins = mm(bank[4][0:SEQ, b2 * D:(b2 + 1) * D], hT[:, b2 * SEQ:(b2 + 1) * SEQ],
                             att_w[:, 2 * D:3 * D], start=(b2 == 0), stop=True, skip_group_check=True)
                ins.then_inc(att_v_done, 1)

            def attention_step(c, back, front):
                pe.wait_ge(att_qk_ready, c * 2 + 2)
                if back:
                    pe.wait_ge(att_d_ready, c)
                pe.sem_inc(pe_gate, 1)
                for b2 in range(CB):
                    at = (b2 % 2) * SEQ
                    ins = mm(bank[5][at:at + SEQ, (b2 // 2) * SEQ:(b2 // 2 + 1) * SEQ],
                             qT[:, b2 * SEQ:(b2 + 1) * SEQ], kT[:, b2 * SEQ:(b2 + 1) * SEQ],
                             start=(b2 < 2), stop=True, skip_group_check=True)
                ins.then_inc(att_s_done, 1)
                if front:
                    tokens_T(c + 1)
                    queries_keys(c + 1)
                pe.wait_ge(att_e_ready, c + 1)
                pe.sem_inc(pe_gate, 1)
                for j in range(CHUNK_BLOCKS):
                    ins = nc.tensor.transpose(bank[6][0:SEQ, j * P:(j + 1) * P], sc_e[:, j], ident[:])
                ins.then_inc(att_eT_done, 1)
                pe.wait_ge(att_eT_ready, c + 1)
                pe.wait_ge(att_v_ready, c + 1)
                if back:
                    pe.wait_ge(att_o_read, c)
                pe.sem_inc(pe_gate, 1)
                for b2 in range(CB):
                    at = (b2 % 2) * SEQ
                    ins = mm(bank[7][at:at + SEQ, (b2 // 2) * D:(b2 // 2 + 1) * D],
                             eT[:, b2 // 2, at:at + SEQ], v_sb[:, b2],
                             start=(b2 < 2), stop=True, skip_group_check=True)
                ins.then_inc(att_o_done, 1)
                if front:
                    pe.wait_ge(att_x_read, c + 1)
                    tokens_values(c + 1)

            tokens_T(0)
            queries_keys(0)
            tokens_values(0)
            attention_step(0, False, True)
            with pe.Fori(1, CHUNKS - 1) as c:
                attention_step(c, True, True)
            attention_step(CHUNKS - 1, True, False)

            def lattice_T(c):
                pe.wait_ge(x2_ready, c + 1)
                for j in range(CHUNK_BLOCKS):
                    ins = nc.tensor.transpose(bank[0][:, j * P:(j + 1) * P], flat(x2[:, j]), ident[:])
                ins.then_inc(xT_done, 1)

            def gate(c, par):
                pe.wait_ge(xT_ready, c + 1)
                for j in range(CHUNK_BLOCKS):
                    ins = mm(bank[1][:, j * EXPERTS0:(j + 1) * EXPERTS0], lat_x[par][0:D, j * P:(j + 1) * P],
                             gate_wT[:], start=(j == 0), stop=True, skip_group_check=True)
                ins.then_inc(lg_done, 1)

            def scores_T(c):
                pe.wait_ge(w2_ready, c + 1)
                for j in range(CHUNK_BLOCKS):
                    ins = nc.tensor.transpose(bank[0][:, j * P:(j + 1) * P], flat(w2x[:, j]), ident[:])
                ins.then_inc(wT_done, 1)

            def spread(c, par, p):
                if p == 0:
                    pe.wait_ge(wT_ready, c + 1)
                mm(spread_ps[p % 4][:], flat(pick[:, 2 * p:2 * p + 2]), lat_w_hl[par][:],
                   start=True, stop=True).then_inc(bc_done, 1)

            def project(c):
                pe.wait_ge(latT_ready, c + 1)
                for j in range(CHUNK_BLOCKS):
                    ins = mm(bank[1][:, j * D:(j + 1) * D], latT[0:D, j * P:(j + 1) * P], out_wT[:],
                             start=(j == 0), stop=True, skip_group_check=True)
                ins.then_inc(proj_done, 1)

            def lattice_step(c, par, back, front):
                for p in range(EPAIRS):
                    pe.wait_ge(z_ready, c * EPAIRS + (p + 1))
                    mm(lat_ps[par][0:D, :], lat_w[:, p], lat_z[p % 4], start=(p == 0),
                       stop=(p == EPAIRS - 1)).then_inc(lat_done, 1)
                    if p + 4 < EPAIRS:
                        spread(c, par, p + 4)
                    elif front:
                        spread(c + 1, 1 - par, p + 4 - EPAIRS)
                    if p == 2 and back:
                        project(c - 1)
                    if p == 7 and front:
                        lattice_T(c + 1)
                    if p == 11 and front:
                        gate(c + 1, 1 - par)
                    if p == 23 and front:
                        scores_T(c + 1)

            lattice_T(0)
            pe.wait_ge(att_x_read, CHUNKS)
            gate(0, 0)
            scores_T(0)
            pe.wait_ge(att_o_read, CHUNKS)
            for p in range(4):
                spread(0, 0, p)
            lattice_step(0, 0, False, True)
            with pe.Fori(0, CHUNKS // 2 - 1) as i:
                lattice_step(i * 2 + 1, 1, True, True)
                lattice_step(i * 2 + 2, 0, True, True)
            lattice_step(CHUNKS - 1, 1, True, False)
            project(CHUNKS - 1)

            def scores(c, par, j, first=False):
                n = c * CHUNK_BLOCKS + j
                if j == 0:
                    pe.wait_ge(kbd_ready, c * 2 + 2)
                    pe.wait_ge(q_sum_ready, (c + 1) * PAIRS)
                if not first:
                    pe.wait_ge(att2_d_ready, n)
                for half in range(2):
                    mm(bank[4 + half][:], ident_bf[:], mask_bf[:], start=True, stop=False,
                       skip_group_check=True)
                for b2 in range(2):
                    toks = (2 * j + b2) * SEQ
                    for p in range(PAIRS):
                        ins = mm(bank[4 + p // 4][b2 * SEQ:(b2 + 1) * SEQ, (p % 4) * P:(p % 4 + 1) * P],
                                 qr[par][p][:, toks:toks + SEQ], flat(k_bd[par][:, 2 * j + b2]),
                                 start=False, stop=(p % 4 == 3), skip_group_check=True)
                ins.then_inc(att2_s_done, 1)

            def weights_T(c, j, half, first=False):
                n = c * CHUNK_BLOCKS + j
                if half == 0:
                    pe.wait_ge(att2_p_ready, n + 1)
                to = weights_bank(j, half)
                if not first and to is bank[6]:
                    pe.wait_ge(pT_ready, n * 2 + half)
                for p in range(half * 4, half * 4 + 4):
                    ins = nc.tensor.transpose(to[:, (p % 4) * P:(p % 4 + 1) * P],
                                              p_sc[:, j % 2, p * P:(p + 1) * P], ident[:])
                ins.then_inc(pT_done, 1)

            def values_out(c, j, first=False):
                pe.wait_ge(pT_ready, (c * CHUNK_BLOCKS + (j + 1)) * 2)
                pe.wait_ge(vw_ready, c * CB + (2 * j + 2))
                if j == 0 and not first:
                    pe.wait_ge(o_read, c)
                for b2 in range(2):
                    for p in range(PAIRS):
                        ins = mm(bank[0][b2 * SEQ:(b2 + 1) * SEQ, j * D:(j + 1) * D],
                                 pT[:, j % 2, p * P + b2 * SEQ:p * P + (b2 + 1) * SEQ],
                                 vw[:, 2 * j + b2, p * D:(p + 1) * D],
                                 start=(p == 0 and j == 0), stop=(p == PAIRS - 1), skip_group_check=True)
                ins.then_inc(att2_o_done, 1)

            def value_proj(c, par, b2):
                if b2 == 0:
                    pe.wait_ge(kbd_ready, c * 2 + 2)
                elif b2 < CB - 1:
                    pe.wait_ge(vw_ready, c * CB + b2)
                mm(values_bank(b2)[:], flat(v_bd[par][:, b2]), flat(wo_w[:]), start=True,
                   stop=True).then_inc(vw_done, 1)

            def chunk_T(c, first=False):
                pe.wait_ge(gx2_ready, c + 1)
                if not first:
                    pe.wait_ge(q_rms_in, c)
                for j in range(CHUNK_BLOCKS):
                    ins = nc.tensor.transpose(bank[7][:, j * P:(j + 1) * P], flat(x2[:, j]), ident[:])
                ins.then_inc(gxT_done, 1)

            def values_T(c):
                mm(bank[7][:], kv_wh[:, 2 * D:4 * D], xT_hl[:], start=True, stop=False)
                mm(bank[7][:], kv_wl[:, 2 * D:4 * D], xT_hl[:], start=False, stop=True).then_inc(vT_done, 1)

            def keys(c, first=False):
                if not first:
                    pe.wait_ge(vw_ready, (c - 1) * CB + 2)
                for j in range(CHUNK_BLOCKS):
                    xs = xT_hl[:, j * P:(j + 1) * P]
                    at = slice(j * 2 * D, (j + 1) * 2 * D)
                    mm(bank[3][:, at], xs, kv_wh[:, 0:2 * D], start=(j == 0), stop=False, skip_group_check=True)
                    ins = mm(bank[3][:, at], xs, kv_wl[:, 0:2 * D], start=False, stop=True, skip_group_check=True)
                ins.then_inc(kn_done, 1)

            def queries(c, p, first=False):
                if p == 0:
                    pe.wait_ge(gxT_ready, c + 1)
                if not first:
                    pe.wait_ge(q_sq_ready, c * PAIRS + p)
                    pe.wait_ge(q_rope_ready, c * 2 * PAIRS + 2 * p)
                for s2 in range(2):
                    mm(bank[1 + s2][:], q_wh[:, s2, p * P:(p + 1) * P], xT_hl[:], start=True, stop=False)
                    mm(bank[1 + s2][:], q_wl[:, s2, p * P:(p + 1) * P], xT_hl[:], start=False,
                       stop=True).then_inc(q_done, 1)

            def q_norms(c, p):
                if p == 0:
                    pe.wait_ge(vbd_ready, c * 2 + 2)
                pe.wait_ge(q_sq_ready, c * PAIRS + (p + 1))
                ins = norms(p)
                if p == PAIRS - 1:
                    ins.then_inc(norm_done, 1)

            def keys_T(c, first=False):
                pe.wait_ge(k2_ready, c + 1)
                if not first:
                    pe.wait_ge(vw_ready, c * CB - 1)
                for j in range(CHUNK_BLOCKS):
                    ins = nc.tensor.transpose(bank[3][:, j * P:(j + 1) * P], flat(w2x[:, j]), ident[:])
                ins.then_inc(kT_done, 1)

            def chunk_step(b, prev, front, par, more=True):
                f = b + 1
                bp = 0 if not prev else 1 - par
                scores(b, bp, 0, not prev)
                value_proj(b, bp, 0)
                if front:
                    if prev:
                        pe.wait_ge(vw_ready, b * CB)
                        pe.wait_ge(pT_ready, b * 2 * CHUNK_BLOCKS - 2)
                    queries(f, 0)
                if prev:
                    weights_T(b - 1, 3, 0)
                if front:
                    values_T(f)
                if prev:
                    weights_T(b - 1, 3, 1)
                value_proj(b, bp, 1)
                if front:
                    queries(f, 1)
                if prev:
                    values_out(b - 1, 3)
                if front:
                    keys(f)
                    q_norms(f, 0)
                for j in (1, 2):
                    if front:
                        queries(f, 3 * j - 1)
                    scores(b, bp, j)
                    if front and j == 1:
                        pe.wait_ge(kn_read, f + 1)
                    value_proj(b, bp, 2 * j)
                    if front:
                        q_norms(f, 3 * j - 2)
                    weights_T(b, j - 1, 0, not prev and j == 1)
                    if front:
                        queries(f, 3 * j)
                    value_proj(b, bp, 2 * j + 1)
                    if front:
                        q_norms(f, 3 * j - 1)
                    weights_T(b, j - 1, 1)
                    if front:
                        queries(f, 3 * j + 1)
                    values_out(b, j - 1, not prev)
                    if front:
                        q_norms(f, 3 * j)
                if front:
                    q_norms(f, PAIRS - 1)
                scores(b, bp, 3)
                value_proj(b, bp, 6)
                if front:
                    pe.wait_ge(q_rope_ready, (f + 1) * 2 * PAIRS)
                value_proj(b, bp, 7)
                if front and more:
                    chunk_T(f + 1)
                weights_T(b, 2, 0)
                weights_T(b, 2, 1)
                if front:
                    keys_T(f)
                values_out(b, 2)

            chunk_T(0, True)
            pe.wait_ge(proj_read, CHUNKS)
            queries(0, 0, True)
            values_T(0)
            keys(0, True)
            for p in range(PAIRS):
                if p > 0:
                    queries(0, p)
                if p > 0:
                    q_norms(0, p - 1)
            q_norms(0, PAIRS - 1)
            keys_T(0, True)
            chunk_T(1)
            chunk_step(0, False, True, 1)
            with pe.Fori(0, CHUNKS // 2 - 2) as i:
                chunk_step(i * 2 + 1, True, True, 0)
                chunk_step(i * 2 + 2, True, True, 1)
            chunk_step(CHUNKS - 3, True, True, 0)
            chunk_step(CHUNKS - 2, True, True, 1, False)
            chunk_step(CHUNKS - 1, True, False, 0)
            weights_T(CHUNKS - 1, 3, 0)
            weights_T(CHUNKS - 1, 3, 1)
            values_out(CHUNKS - 1, 3)

            def rows_T(c):
                pe.wait_ge(m2_ready, c + 1)
                for j in range(CHUNK_BLOCKS):
                    ins = nc.tensor.transpose(bank[0][:, j * P:(j + 1) * P], flat(x2[:, j]), ident[:])
                ins.then_inc(mT_done, 1)

            def router(c, par):
                pe.wait_ge(mT_ready, c + 1)
                for j in range(CHUNK_BLOCKS):
                    xs = mT_hl[par][:, j * P:(j + 1) * P]
                    at = slice(j * EXPERTS1, (j + 1) * EXPERTS1)
                    mm(bank[1][:, at], xs, r_wh[:], start=(j == 0), stop=False, skip_group_check=True)
                    ins = mm(bank[1][:, at], xs, r_wl[:], start=False, stop=True, skip_group_check=True)
                ins.then_inc(r_done, 1)

            def second(c, e):
                pe.wait_ge(h1_ready, c * EXPERTS1 + (e + 1))
                for j in range(CHUNK_BLOCKS):
                    ins = mm(bank[4 + j][:, e * D:(e + 1) * D], hid[:, e % 2, j * P:(j + 1) * P],
                             e2_w[:, e], start=(e == 0), stop=True, skip_group_check=True)
                return ins

            def gelu_step(c, par, back, front):
                for e in range(EXPERTS1):
                    if back or e >= 2:
                        pe.wait_ge(h1_ready, c * EXPERTS1 + (e - 1))
                    mm(bank[2 + e % 2][:], e1_wh[:, e * HID1:(e + 1) * HID1], mT_hl[par][:], start=True,
                       stop=False)
                    mm(bank[2 + e % 2][:], e1_wl[:, e * HID1:(e + 1) * HID1], mT_hl[par][:], start=False,
                       stop=True).then_inc(h1_done, 1)
                    if e == 1 and back:
                        pe.wait_ge(y2_read, c)
                    if e >= 1:
                        second(c, e - 1)
                    if e == 3 and front:
                        rows_T(c + 1)
                second(c, EXPERTS1 - 1).then_inc(y2_done, 1)
                if front:
                    router(c + 1, 1 - par)

            pe.wait_ge(o_read, CHUNKS)
            rows_T(0)
            router(0, 0)
            gelu_step(0, 0, False, True)
            with pe.Fori(0, CHUNKS // 2 - 1) as i:
                gelu_step(i * 2 + 1, 1, True, True)
                gelu_step(i * 2 + 2, 0, True, True)
            gelu_step(CHUNKS - 1, 1, True, False)

        @block.scalar
        def _(act):
            def hidden(k):
                nc.scalar.activation(h0_sb[0:V, k % 2, :], h0_ps[k % 2][0:V, :],
                                     ACT.Relu).then_inc(h0_ready, 1)

            def batch(b, first, last):
                for k in range(UNITS):
                    u = b * UNITS + k
                    if not (last and k == UNITS - 1):
                        act.wait_ge(l0_done, u + 2)
                        if not (first and k == 0):
                            act.wait_ge(amix_done, u)
                        hidden((k + 1) % UNITS)
                    act.wait_ge(amix_done, u + 1)
                    if not (first and k < 2):
                        act.wait_ge(z_done, u - 1)
                    nc.scalar.activation(ah_sb[:, k % 2, :], ah_ps[k % 2][:, 0:UNIT * V],
                                         ACT.Copy).then_inc(ah_ready, 1)

            act.wait_ge(ones_set, 1)
            nc.scalar.activation(act_first[:], ones[:, 0:1], ACT.Relu).then_inc(act_order, 1)
            act.wait_ge(h0_zeroed, 1)
            act.wait_ge(l0_done, 1)
            hidden(0)
            batch(0, True, False)
            with act.Fori(1, BATCHES - 1) as b:
                batch(b, False, False)
            batch(BATCHES - 1, False, True)

            go = nc.scalar.activation
            def copy_hT(c):
                act.wait_ge(att_hT_done, c + 1)
                go(hT[:], bank[0][0:D, :], ACT.Identity, bias=bn_bias[0:D, 2:3]).then_inc(att_hT_ready, 1)

            def copy_qk(c):
                act.wait_ge(att_qk_done, c + 1)
                go(qT[:], bank[2][0:D, :], ACT.Identity, bias=cols64[0:D, 5:6]).then_inc(att_qk_ready, 1)
                go(kT[:], bank[3][0:D, :], ACT.Identity, bias=cols64[0:D, 6:7]).then_inc(att_qk_ready, 1)

            def copy_v(c):
                act.wait_ge(att_v_done, c + 1)
                go(flat(v_sb[:]), bank[4][0:SEQ, :], ACT.Copy).then_inc(att_v_ready, 1)

            def attention_step(c, front):
                if front:
                    copy_hT(c + 1)
                act.wait_ge(att_d_ready, c + 1)
                go(sc_e[:], sc[:], ACT.Exp, scale=D ** -0.5).then_inc(att_e_ready, 1)
                if front:
                    copy_qk(c + 1)
                act.wait_ge(att_eT_done, c + 1)
                go(flat(eT[:]), bank[6][0:SEQ, :], ACT.Copy).then_inc(att_eT_ready, 1)
                if front:
                    copy_v(c + 1)

            copy_hT(0)
            copy_qk(0)
            copy_v(0)
            with act.Fori(0, CHUNKS - 1) as c:
                attention_step(c, True)
            attention_step(CHUNKS - 1, False)

            def twice(c, layer, ready):
                act.wait_ge(hN_ready, c + (layer * CHUNKS + 1))
                go(x2[:], hN_chunk(c).unsqueeze(2).to_broadcast([P, CHUNK_BLOCKS, 2, D]),
                   ACT.Copy).then_inc(ready, 1)

            def lattice_front(c, par):
                twice(c, 0, x2_ready)
                act.wait_ge(xT_done, c + 1)
                go(lat_x[par], bank[0][:], ACT.Copy).then_inc(xT_ready, 1)
                act.wait_ge(lg_d_ready, c + 1)
                go(sc_e[:], sc[:], ACT.Exp).then_inc(lg_e_ready, 1)

            def lattice_out(c, par):
                act.wait_ge(lat_done, (c + 1) * EPAIRS)
                go(latT[0:D], lat_ps[par][0:D, :], ACT.Copy).then_inc(latT_ready, 1)

            lattice_front(0, 0)
            lattice_front(1, 1)
            with act.Fori(0, CHUNKS // 2 - 1) as i:
                lattice_out(i * 2, 0)
                lattice_front(i * 2 + 2, 0)
                lattice_out(i * 2 + 1, 1)
                lattice_front(i * 2 + 3, 1)
            lattice_out(CHUNKS - 2, 0)
            lattice_out(CHUNKS - 1, 1)

            def softmax_exp(c, j):
                act.wait_ge(att2_dr_ready, c * CHUNK_BLOCKS + (j + 1))
                go(p_sc[:, j % 2], p_sc[:, j % 2], ACT.Exp).then_inc(att2_e_ready, 1)

            def copy_pT(c, j, half, early=False):
                act.wait_ge(pT_done, (c * CHUNK_BLOCKS + j) * 2 + (half + 1))
                if half == 0 and not early:
                    act.wait_ge(att2_o_done, c * CHUNK_BLOCKS + (j - 1))
                go(pT[:, j % 2, half * CT:(half + 1) * CT], weights_bank(j, half)[:], ACT.Copy).then_inc(pT_ready, 1)

            def copy_vw(c, b2):
                act.wait_ge(vw_done, c * CB + (b2 + 1))
                go(vw[:, b2], values_bank(b2)[:], ACT.Copy).then_inc(vw_ready, 1)

            def square(c, p):
                act.wait_ge(q_done, c * 2 * PAIRS + (2 * p + 1))
                go(q_sq[:, p % 2], bank[1][:], ACT.Square).then_inc(q_sq_ready, 1)

            def block_diagonal(done, ready, src, dst, c):
                act.wait_ge(done, c + 1)
                for h in range(2):
                    at = slice(h * D, (h + 1) * D)
                    go(dst[at, :, h], src[at, :].rearrange("p (b s) -> p b s", s=SEQ),
                       ACT.Copy).then_inc(ready, 1)

            def rows_twice(c, first=False):
                act.wait_ge(hN_ready, c + (CHUNKS + 1))
                if not first:
                    act.wait_ge(gxT_done, c)
                go(x2[:], hN_chunk(c).unsqueeze(2).to_broadcast([P, CHUNK_BLOCKS, 2, D]),
                   ACT.Copy).then_inc(gx2_ready, 1)

            def chunk_step(b, prev, front, par, more=True):
                f = b + 1
                copy_vw(b, 0)
                if front:
                    square(f, 0)
                if prev:
                    copy_pT(b - 1, 3, 0)
                if front:
                    block_diagonal(vT_done, vbd_ready, bank[7], v_bd[par], f)
                if prev:
                    copy_pT(b - 1, 3, 1)
                copy_vw(b, 1)
                if front:
                    square(f, 1)
                softmax_exp(b, 0)
                if front and more:
                    rows_twice(f + 1)
                for j in (1, 2):
                    if front:
                        square(f, 3 * j - 1)
                    copy_vw(b, 2 * j)
                    copy_pT(b, j - 1, 0, not prev)
                    if front:
                        square(f, 3 * j)
                    copy_vw(b, 2 * j + 1)
                    copy_pT(b, j - 1, 1)
                    if front:
                        square(f, 3 * j + 1)
                    softmax_exp(b, j)
                copy_vw(b, 6)
                copy_vw(b, 7)
                copy_pT(b, 2, 0)
                copy_pT(b, 2, 1)
                if front:
                    block_diagonal(kT_done, kbd_ready, bank[3], k_bd[par], f)
                softmax_exp(b, 3)

            rows_twice(0, True)
            square(0, 0)
            act.wait_ge(bd_zeroed, 2)
            block_diagonal(vT_done, vbd_ready, bank[7], v_bd[0], 0)
            for p in range(1, PAIRS):
                square(0, p)
            block_diagonal(kT_done, kbd_ready, bank[3], k_bd[0], 0)
            rows_twice(1)
            chunk_step(0, False, True, 1)
            with act.Fori(0, CHUNKS // 2 - 2) as i:
                chunk_step(i * 2 + 1, True, True, 0)
                chunk_step(i * 2 + 2, True, True, 1)
            chunk_step(CHUNKS - 3, True, True, 0)
            chunk_step(CHUNKS - 2, True, True, 1, False)
            chunk_step(CHUNKS - 1, True, False, 0)
            copy_pT(CHUNKS - 1, 3, 0)
            copy_pT(CHUNKS - 1, 3, 1)

            def router_exp(c):
                act.wait_ge(r_d_ready, c + 1)
                go(sc_e[:, :, 0:EXPERTS1], sc[:, :, 0:EXPERTS1], ACT.Exp).then_inc(r_e_ready, 1)

            def gelu_step(c):
                for e in range(EXPERTS1):
                    act.wait_ge(h1_done, c * EXPERTS1 + (e + 1))
                    go(hid[:, e % 2], bank[2 + e % 2][:], ACT.Gelu,
                       bias=e1_b[:, e:e + 1]).then_inc(h1_ready, 1)
                    if e == 1:
                        router_exp(c)

            with act.Fori(0, CHUNKS) as c:
                gelu_step(c)

        @block.vector
        def _(dve):
            vec = nc.vector
            order = Chain(dve, dve_order)
            dve.wait_ge(consts_in, 16 * len(CONSTS))
            order(vec.memset(bn_tmp[:], 1.0))
            order(vec.memset(bn_bias[:], 0.0))
            order.wait()
            order(vec.tensor_scalar(bn_tmp[:, 0:2], cols[:, 4:10:5], EPS_BN, None, ALU.add))
            order.wait()
            vec.tensor_scalar(bn_tmp[0:D, 2:3], cols64[0:D, 4:5], EPS_BN, None,
                              ALU.add).then_inc(bn_var, 1)
            dve.wait_ge(bn_rsqrt, 1)
            order(vec.tensor_tensor(bn_scale[:, 0:2], bn_scale[:, 0:2], cols[:, 1:7:5], ALU.mult))
            order(vec.tensor_tensor(bn_scale[0:D, 2:3], bn_scale[0:D, 2:3], cols64[0:D, 1:2], ALU.mult))
            order(vec.tensor_tensor(bn_bias[:, 0:2], cols[:, 0:6:5], cols[:, 3:9:5], ALU.subtract))
            order(vec.tensor_tensor(bn_bias[0:D, 2:3], cols64[0:D, 0:1], cols64[0:D, 3:4], ALU.subtract))
            order.wait()
            order(vec.tensor_tensor(bn_bias[:, 0:3], bn_bias[:, 0:3], bn_scale[:, 0:3], ALU.mult))
            order.wait()
            order(vec.tensor_tensor(bn_bias[:, 0:2], bn_bias[:, 0:2], cols[:, 2:8:5], ALU.add))
            order(vec.tensor_tensor(bn_bias[0:D, 2:3], bn_bias[0:D, 2:3], cols64[0:D, 2:3], ALU.add))
            order.wait()
            order(vec.tensor_scalar(neg_b1[:], bn_bias[:, 1:2], -1.0, None, ALU.mult))
            for n, col in enumerate((bn_scale[:, 0:1], bn_bias[:, 0:1], bn_scale[:, 1:2])):
                order(vec.tensor_scalar(diag[:, n], ident[:], col, None, ALU.mult))
            order(vec.tensor_scalar(diag[:, 3], ident[:], bn_scale[:, 2:3], None, ALU.mult))
            order.wait()
            vec.tensor_scalar(diag[:, 4], ident[:], bn_bias[:, 2:3], None,
                              ALU.mult).then_inc(diag_ready, 1)
            dve.wait_ge(rows_done, 1)
            order(vec.tensor_copy(rows_b[:, 0:4].rearrange("p a b -> p (a b)"), mix_ps[:, 0:512]))
            order(vec.tensor_copy(rows_b[:, 4], z_ps[0][:, 0:P]))
            order.wait()
            per_token = "p (j c) -> p j c"
            order(vec.tensor_tensor(
                w0_tmp.rearrange(per_token, j=GROUP), w0_raw.rearrange(per_token, j=GROUP),
                rows_b[:, 0:1, :].to_broadcast([P, GROUP, CH]), ALU.mult))
            order.wait()
            order(vec.scalar_tensor_tensor(
                w0_tmp.rearrange(per_token, j=GROUP),
                rows_b[:, 1:2, :].to_broadcast([P, GROUP, CH]), cols[:, 10:11],
                w0_tmp.rearrange(per_token, j=GROUP), ALU.mult, ALU.add))
            order.wait()
            order(vec.tensor_copy(w0_hl[:], w0_tmp))
            order.wait()
            order(vec.tensor_tensor(w0_hl[32:64], w0_tmp[32:64], w0_hl[32:64].bitcast(F32),
                                    ALU.subtract))
            order.wait()
            vec.tensor_tensor(w0_hl[96:128], w0_tmp[96:128], w0_hl[96:128].bitcast(F32),
                              ALU.subtract).then_inc(weights_ready, 1)

            abar_u = abar[:].unsqueeze(1).to_broadcast([CH, UNIT, V])

            def y_split(b, par):
                dve.wait_ge(y_done, b * 2 + (par + 1))
                flat = y_hl[:, par].rearrange("p g v -> p (g v)")
                y = y_ps[0:2 * ROWS, 0:ITER // GROUP * V]
                vec.tensor_scalar(flat[0:2 * ROWS], y, cols[0:2 * ROWS, 10:11],
                                  None, ALU.add).then_inc(y_high, 1)
                dve.wait_ge(y_high, b * 2 + (par + 1))
                vec.tensor_tensor(flat[2 * ROWS:P], y, flat[0:2 * ROWS].bitcast(F32),
                                  ALU.subtract).then_inc(y_ready, 1)

            def node_sum(b, k, first):
                slot = (k // 4) % 2
                dve.wait_ge(z_done, b * UNITS + (k + 1))
                if k % 4 == 0 and not (first and k < 8):
                    dve.wait_ge(s_ready, b * 4 + (k // 4 - 1))
                vec.scalar_tensor_tensor(
                    prod[:, slot, k % 4].rearrange("p (j v) -> p j v", v=V),
                    z_ps[k % 2][:, 0:UNIT * V].rearrange("p (j v) -> p j v", v=V), neg_b1[:, 0:1],
                    abar_u, ALU.max, ALU.mult).then_inc(prod_done, 1)
                if k % 4 == 3:
                    dve.wait_ge(prod_done, b * UNITS + (k + 1))
                    vec.tensor_reduce(
                        sT[:, bass.ds(b * SEQ + 4 * (k - 3), 16)],
                        prod[:, slot].rearrange("p q (j v) -> p (q j) v", v=V),
                        AX_X, ALU.add).then_inc(s_ready, 1)

            def batch(b, first, last):
                for k in range(UNITS):
                    if k > 0:
                        node_sum(b, k - 1, first)
                    elif not first:
                        node_sum(b - 1, UNITS - 1, False)
                    if k == 3:
                        y_split(b, 1)
                    if k == 11 and not last:
                        y_split(b + 1, 0)

            y_split(0, 0)
            dve.wait_ge(abar_done, 1)
            order(vec.tensor_scalar(abar[:], z_ps[1][:, 0:V], NODES_INV, None, ALU.mult))
            order.wait()
            order(vec.tensor_reduce(a_sum[:], abar[:], AX_X, ALU.add))
            order(vec.tensor_tensor(w1_s[:], w1_raw[:], rows_b[:, 2], ALU.mult))
            order(vec.tensor_tensor(w2_s[:], w2_raw[:], rows_b[:, 3, 0:D], ALU.mult))
            order.wait()
            vec.tensor_tensor(s_corr[:], a_sum[:], bn_bias[:, 1:2], ALU.mult).then_inc(w1_ready, 1)
            dve.wait_ge(w1_ready, 1)
            batch(0, True, False)
            with dve.Fori(1, BATCHES - 1) as b:
                batch(b, False, False)
            batch(BATCHES - 1, False, True)
            node_sum(BATCHES - 1, UNITS - 1, False)

            tt, stt, ts = vec.tensor_tensor, vec.scalar_tensor_tensor, vec.tensor_scalar

            def normalize(n, src, dst, after=None):
                center(src)
                variance()
                normalized(n, dst, after)

            def center(src):
                order.wait()
                order(vec.tensor_reduce(ln_mean[:], src, AX_X, ALU.add))
                order.wait()
                order(ts(ln_mean[:], ln_mean[:], -1.0 / D, None, ALU.mult))
                order.wait()
                order(tt(xc[:], src, per_block(ln_mean[:]), ALU.add))

            def variance():
                order.wait()
                order(tt(xsq[:], xc[:], xc[:], ALU.mult))
                order.wait()
                order(vec.tensor_reduce(ln_var[:], xsq[:], AX_X, ALU.add))
                order.wait()
                ts(ln_var[:], ln_var[:], 1.0 / D, EPS_LN, ALU.mult, ALU.add).then_inc(ln_var_ready, 1)

            def normalized(n, dst, after=None):
                dve.wait_ge(ln_rstd_ready, n)
                ins = tt(dst, xc[:], per_block(ln_rstd[:]), ALU.mult)
                if after is None:
                    order(ins)
                else:
                    ins.then_inc(after, 1)

            def chunk_sums(c, first=False):
                if not first:
                    dve.wait_ge(att_h_done, c)
                ts(s_chunk[:], sT[:, bass.ds(c * CT, CT)], s_corr[:, 0:1], None, ALU.add).then_inc(sT_copied, 1)

            def attention_step(c, front):
                if front:
                    chunk_sums(c + 1)
                dve.wait_ge(att_s_done, c + 1)
                scores = bank[5][:, 0:CHUNK_BLOCKS * SEQ].rearrange("p (j s) -> p j s", s=SEQ)
                order(vec.tensor_reduce(row_max[:], scores, AX_X, ALU.max))
                order.wait()
                tt(sc[:], scores, per_block(row_max[:]), ALU.subtract).then_inc(att_d_ready, 1)
                dve.wait_ge(att_h_done, c + 1)
                tt(x_tok[:], bank[1][:, 0:CHUNK_BLOCKS * D].rearrange("p (j d) -> p j d", d=D),
                   per_block(rows_b[:, 4, 0:D]), ALU.add).then_inc(att_x_read, 1)
                dve.wait_ge(att_x_read, c + 1)
                order(tt(x_tok[:], x_tok[:], per_block(row("bv")), ALU.add))
                dve.wait_ge(att_e_ready, c + 1)
                order(vec.tensor_reduce(row_sum[:], sc_e[:], AX_X, ALU.add))
                order.wait()
                order(vec.reciprocal(row_inv[:], row_sum[:]))
                order.wait()
                dve.wait_ge(att_o_done, c + 1)
                tt(res[:], bank[7][:, 0:CHUNK_BLOCKS * D].rearrange("p (j d) -> p j d", d=D),
                   per_block(row_inv[:]), ALU.mult).then_inc(att_o_read, 1)
                dve.wait_ge(att_o_read, c + 1)
                order(tt(res[:], res[:], x_tok[:], ALU.add))
                normalize(c + 1, res[:], hN_chunk(c), hN_ready)

            dve.wait_ge(later_in, LATER_IN)
            dve.wait_ge(s_ready, BATCHES * 4)
            chunk_sums(0, True)
            with dve.Fori(0, CHUNKS - 1) as c:
                order.enter(c, N_ATT)
                attention_step(c, True)
            order.leave(CHUNKS - 1)
            attention_step(CHUNKS - 1, False)
            dve.wait_ge(hN_ready, CHUNKS)

            def split_xT(done, ready, c, bank_x, xT_hl=xT_hl):
                dve.wait_ge(done, c + 1)
                order(vec.tensor_copy(xT_hl[:], bank_x[:]))
                order.wait()
                tt(xT_hl[D:P], bank_x[D:P, :], xT_hl[D:P].bitcast(F32), ALU.subtract).then_inc(ready, 1)

            def gelu_rows(c, n):
                center(hN_chunk(c))
                variance()
                gelu_rows_out(n)

            def gelu_rows_out(n):
                normalized(n, x_tok[:])
                order.wait()
                order(tt(x_tok[:], x_tok[:], per_block(row("gamma")), ALU.mult))
                order.wait()
                order(tt(x2[:, :, 0], x_tok[:], per_block(row("beta")), ALU.add))
                tt(x2[:, :, 1], x_tok[:], per_block(row("beta")), ALU.add).then_inc(m2_ready, 1)

            def gate_max(c):
                dve.wait_ge(lg_done, c + 1)
                order(vec.tensor_copy(lg[:], bank[1][:, 0:CHUNK_BLOCKS * EXPERTS0].rearrange(
                    "p (j e) -> p j e", e=EXPERTS0)))
                order.wait()
                order(vec.tensor_reduce(top_max[:], lg[:], AX_X, ALU.max))

            def gate_top():
                for j in range(CHUNK_BLOCKS):
                    order(vec.max(top[:, j], lg[:, j]))
                order.wait()
                order(vec.memset(top[:, :, TOP0:8], BIG))

            def gate_select():
                order.wait()
                tt(sc[:], lg[:], per_block(top_max[:]), ALU.subtract).then_inc(lg_d_ready, 1)
                for j in range(CHUNK_BLOCKS):
                    order(vec.match_replace(left[:, j], top[:, j], lg[:, j], -BIG))

            def gate_mask():
                order.wait()
                order(tt(left[:], left[:], lg[:], ALU.not_equal))

            def gate_weights(c):
                order.wait()
                dve.wait_ge(lg_e_ready, c + 1)
                order(tt(left[:], left[:], sc_e[:], ALU.mult))
                order.wait()
                order(vec.tensor_reduce(row_sum[:], left[:], AX_X, ALU.add))
                order.wait()
                order(vec.reciprocal(row_inv[:], row_sum[:]))

            def gate_divide():
                order.wait()
                order(tt(w2x[:, :, 0], left[:], per_block(row_inv[:]), ALU.mult))
                tt(w2x[:, :, 1], left[:], per_block(row_inv[:]), ALU.mult).then_inc(w2_ready, 1)

            def gate_split(c, par):
                split_xT(wT_done, wT_ready, c, bank[0], lat_w_hl[par])

            def take_projection(c):
                dve.wait_ge(proj_done, c + 1)
                tt(res[:], bank[1][:, 0:CHUNK_BLOCKS * D].rearrange("p (j d) -> p j d", d=D),
                   per_block(row("out_b")), ALU.add).then_inc(proj_read, 1)
                dve.wait_ge(proj_read, c + 1)
                order(tt(res[:], res[:], hN_chunk(c), ALU.add))

            def lattice_step(c, par, back, front):
                b, f = c - 1, c + 1
                for p in range(EPAIRS):
                    n = c * EPAIRS + (p + 1)
                    dve.wait_ge(bc_done, n)
                    if back or p >= 4:
                        dve.wait_ge(lat_done, n - 4)
                    tt(lat_z[p % 4], spread_ps[p % 4][:], lat_x[par], ALU.mult).then_inc(z_ready, 1)
                    if back:
                        if p == 4:
                            take_projection(b)
                        if p == 6:
                            center(res[:])
                        if p == 7:
                            variance()
                        if p == 9:
                            normalized(b * 2 + (ATT_NORMS + 1), res[:])
                        if p == 10:
                            order.wait()
                            order(tt(res[:], res[:], per_block(row("ln_g")), ALU.mult))
                        if p == 11:
                            order.wait()
                            order(tt(res[:], res[:], per_block(row("ln_b")), ALU.add))
                        if p == 12:
                            order.wait()
                            order(tt(res[:], res[:], hN_chunk(b), ALU.add))
                        if p == 16:
                            center(res[:])
                        if p == 18:
                            variance()
                        if p == 25:
                            normalized(b * 2 + (ATT_NORMS + 2), hN_chunk(b), hN_ready)
                    if front:
                        if p == 14:
                            gate_max(f)
                        if p == 15:
                            gate_top()
                        if p == 17:
                            gate_select()
                        if p == 19:
                            gate_mask()
                        if p == 20:
                            gate_weights(f)
                        if p == 22:
                            gate_divide()
                        if p == 27:
                            gate_split(f, 1 - par)

            gate_max(0)
            gate_top()
            gate_select()
            gate_mask()
            gate_weights(0)
            gate_divide()
            gate_split(0, 0)
            dve.wait_ge(xT_ready, 1)
            lattice_step(0, 0, False, True)
            with dve.Fori(0, CHUNKS // 2 - 1) as i:
                order.enter(i, N_LAT)
                lattice_step(i * 2 + 1, 1, True, True)
                lattice_step(i * 2 + 2, 0, True, True)
            order.leave(CHUNKS // 2 - 1)
            lattice_step(CHUNKS - 1, 1, True, False)

            def tok_trig(n):
                return trig_t[:, n].unsqueeze(1).to_broadcast([P, CHUNK_BLOCKS, D])

            def feat_trig(n):
                return trig_f[:, n].unsqueeze(1).to_broadcast([P, CB, SEQ])

            def by_batch(ap):
                return ap.rearrange("p (b s) -> p b s", s=SEQ)

            def scores_max(c, j, early=False):
                dve.wait_ge(att2_s_done, c * CHUNK_BLOCKS + (j + 1))
                for half in range(2):
                    order(vec.tensor_reduce(
                        p_max[:, j % 2, half * PAIRS:(half + 1) * PAIRS],
                        bank[4 + half][:].rearrange("p (h s) -> p h s", s=SEQ), AX_X, ALU.max))
                order.wait()
                if not early:
                    dve.wait_ge(pT_done, (c * CHUNK_BLOCKS + (j - 1)) * 2)
                for half in range(2):
                    ins = tt(p_sc[:, j % 2, half * CT:(half + 1) * CT].rearrange("p (h s) -> p h s", s=SEQ),
                             bank[4 + half][:].rearrange("p (h s) -> p h s", s=SEQ),
                             p_max[:, j % 2, half * PAIRS:(half + 1) * PAIRS].unsqueeze(2).to_broadcast(
                                 [P, PAIRS, SEQ]), ALU.subtract)
                    if half == 0:
                        order(ins)
                ins.then_inc(att2_d_ready, 1)

            def softmax_sum(c, j, early=False):
                dve.wait_ge(att2_e_ready, c * CHUNK_BLOCKS + (j + 1))
                order(vec.tensor_reduce(p_sum[:, j % 2], p_sc[:, j % 2].rearrange("p (h s) -> p h s", s=SEQ),
                                        AX_X, ALU.add))
                order.wait()
                if not early:
                    dve.wait_ge(att2_p_ready, c * CHUNK_BLOCKS + (j - 1))
                vec.reciprocal(p_inv[:, j % 2], p_sum[:, j % 2]).then_inc(p_inv_ready, 1)

            def key_norm(c):
                dve.wait_ge(kn_done, c + 1)
                kk = bank[3][:].rearrange("p (j s d) -> p j s d", s=2, d=D)
                order(tt(k_t[:], kk[:, :, 0], tok_trig(0), ALU.mult))
                tt(k_s[:], kk[:, :, 1], tok_trig(1), ALU.mult).then_inc(kn_read, 1)
                order.wait()
                dve.wait_ge(kn_read, c + 1)
                order(tt(k_t[:], k_t[:], k_s[:], ALU.add))
                order.wait()
                order(tt(k_s[:], k_t[:], k_t[:], ALU.mult))
                order.wait()
                order(vec.tensor_reduce(k_var[:], k_s[:], AX_X, ALU.add))
                order.wait()
                ts(k_var[:], k_var[:], 1.0 / D, EPS_RMS, ALU.mult, ALU.add).then_inc(k_rms_in, 1)

            def key_scale(c, first=False):
                order(tt(k_t[:], k_t[:], per_block(qk_gain[:]), ALU.mult))
                order.wait()
                if not first:
                    dve.wait_ge(kT_done, c)
                dve.wait_ge(k_rms_out, c + 1)
                order(tt(w2x[:, :, 0], k_t[:], per_block(k_rms[:]), ALU.mult))
                tt(w2x[:, :, 1], k_t[:], per_block(k_rms[:]), ALU.mult).then_inc(k2_ready, 1)

            def rope(c, par, p):
                n = c * 2 * PAIRS + 2 * p
                dve.wait_ge(q_sq_ready, c * PAIRS + (p + 1))
                tt(by_batch(rope_c[:, p % 2]), by_batch(bank[1][:]), feat_trig(0),
                   ALU.mult).then_inc(q_rope_ready, 1)
                dve.wait_ge(q_done, n + 2)
                tt(by_batch(rope_s[:, p % 2]), by_batch(bank[2][:]), feat_trig(1),
                   ALU.mult).then_inc(q_rope_ready, 1)
                dve.wait_ge(q_rope_ready, n + 2)
                tt(qr[par][p], rope_c[:, p % 2], rope_s[:, p % 2],
                   ALU.add).then_inc(q_sum_ready, 1)

            def query_var(c, first=False):
                dve.wait_ge(norm_done, c + 1)
                if not first:
                    dve.wait_ge(q_rms_out, c * CHUNK_BLOCKS)
                ts(q_var[:], bank[7][:, 0:CHUNK_BLOCKS * HEADS], 1.0 / D, EPS_RMS, ALU.mult,
                   ALU.add).then_inc(q_rms_in, 1)

            def take_out(c):
                dve.wait_ge(att2_o_done, (c + 1) * CHUNK_BLOCKS)
                tt(res[:], bank[0][:, 0:CHUNK_BLOCKS * D].rearrange("p (j d) -> p j d", d=D),
                   hN_chunk(c), ALU.add).then_inc(o_read, 1)


            def chunk_step(b, prev, front, par, more=True):
                f = b + 1
                if prev:
                    softmax_sum(b - 1, 3)
                scores_max(b, 0, not prev)
                if front:
                    rope(f, par, 0)
                    rope(f, par, 1)
                    key_norm(f)
                if prev:
                    take_out(b - 1)
                for j in (1, 2):
                    softmax_sum(b, j - 1, not prev)
                    if front:
                        rope(f, par, 3 * j - 1)
                    scores_max(b, j, not prev and j == 1)
                    if front:
                        rope(f, par, 3 * j)
                        rope(f, par, 3 * j + 1)
                        if j == 2:
                            key_scale(f)
                    if prev and j == 1:
                        dve.wait_ge(o_read, b)
                        center(res[:])
                    if prev and j == 2:
                        variance()
                softmax_sum(b, 2)
                if front:
                    query_var(f)
                scores_max(b, 3)
                if front and more:
                    split_xT(gxT_done, gxT_ready, f + 1, bank[7])
                if prev:
                    normalized(b + ROT_NORMS, hN_chunk(b - 1), hN_ready)

            split_xT(gxT_done, gxT_ready, 0, bank[7])
            b = CHUNKS - 1
            take_projection(b)
            for p in range(PAIRS):
                rope(0, 0, p)
                if p == 0:
                    center(res[:])
                    variance()
                if p == 1:
                    key_norm(0)
                    normalized(b * 2 + (ATT_NORMS + 1), res[:])
                    order.wait()
                    order(tt(res[:], res[:], per_block(row("ln_g")), ALU.mult))
                    order.wait()
                    order(tt(res[:], res[:], per_block(row("ln_b")), ALU.add))
                if p == 2:
                    order.wait()
                    order(tt(res[:], res[:], hN_chunk(b), ALU.add))
                    center(res[:])
                if p == 3:
                    variance()
                if p == 5:
                    normalized(b * 2 + (ATT_NORMS + 2), hN_chunk(b), hN_ready)
            key_scale(0, True)
            query_var(0, True)
            split_xT(gxT_done, gxT_ready, 1, bank[7])
            chunk_step(0, False, True, 1)
            with dve.Fori(0, CHUNKS // 2 - 2) as i:
                order.enter(i, N_ROT)
                chunk_step(i * 2 + 1, True, True, 0)
                chunk_step(i * 2 + 2, True, True, 1)
            order.leave(CHUNKS // 2 - 2)
            chunk_step(CHUNKS - 3, True, True, 0)
            chunk_step(CHUNKS - 2, True, True, 1, False)
            chunk_step(CHUNKS - 1, True, False, None)
            gelu_rows(0, GELU_NORMS)
            softmax_sum(CHUNKS - 1, 3)
            take_out(CHUNKS - 1)
            dve.wait_ge(o_read, CHUNKS)
            center(res[:])
            variance()
            split_xT(mT_done, mT_ready, 0, bank[0], mT_hl[0])
            normalized(GELU_NORMS + 1, hN_chunk(CHUNKS - 1), hN_ready)
            dve.wait_ge(hN_ready, 3 * CHUNKS)

            def route(c):
                dve.wait_ge(r_done, c + 1)
                rl = lg[:, :, 0:EXPERTS1]
                order(tt(rl, bank[1][:, 0:CHUNK_BLOCKS * EXPERTS1].rearrange("p (j e) -> p j e", e=EXPERTS1),
                         per_block(row("br", EXPERTS1), EXPERTS1), ALU.add))
                order.wait()
                order(vec.tensor_reduce(top_max[:], rl, AX_X, ALU.max))
                for j in range(CHUNK_BLOCKS):
                    order(vec.max(top[:, j], rl[:, j]))
                order.wait()
                order(vec.memset(top[:, :, 2:8], BIG))
                order.wait()
                tt(sc[:, :, 0:EXPERTS1], rl, per_block(top_max[:], EXPERTS1), ALU.subtract).then_inc(r_d_ready, 1)
                sel = left[:, :, 0:EXPERTS1]
                for j in range(CHUNK_BLOCKS):
                    order(vec.match_replace(sel[:, j], top[:, j], rl[:, j], -BIG))
                order.wait()
                order(tt(sel, sel, rl, ALU.not_equal))

            def route_weights(c, par):
                sel = left[:, :, 0:EXPERTS1]
                order.wait()
                dve.wait_ge(r_e_ready, c + 1)
                order(tt(sel, sel, sc_e[:, :, 0:EXPERTS1], ALU.mult))
                order.wait()
                order(vec.tensor_reduce(row_sum[:], sel, AX_X, ALU.add))
                order.wait()
                order(vec.reciprocal(row_inv[:], row_sum[:]))
                order.wait()
                order(tt(wf[:, par], sel, per_block(row_inv[:], EXPERTS1), ALU.mult))

            def take_outputs(c):
                dve.wait_ge(y2_done, c + 1)
                for j in range(CHUNK_BLOCKS):
                    ins = tt(moe[j], bank[4 + j][:], row("b2", EXPERTS1 * D), ALU.add)
                    if j + 1 < CHUNK_BLOCKS:
                        order(ins)
                ins.then_inc(y2_read, 1)

            def combine(c):
                for j in range(CHUNK_BLOCKS):
                    dve.wait_ge(moe_ready, c * CHUNK_BLOCKS + (j + 1))
                    order(vec.tensor_reduce(res[:, j], moe[j].rearrange("p (e d) -> p d e", d=D),
                                            AX_X, ALU.add))
                order.wait()
                order(tt(res[:], res[:], hN_chunk(c), ALU.add))
                center(res[:])
                variance()

            def gelu_step(c, par, back, front):
                if front:
                    center(hN_chunk(c + 1))
                    variance()
                route_weights(c, par)
                if front:
                    gelu_rows_out(c * 2 + (GELU_NORMS + 1) if back else GELU_NORMS + 2)
                    split_xT(mT_done, mT_ready, c + 1, bank[0], mT_hl[1 - par])
                if back:
                    combine(c - 1)
                take_outputs(c)
                if front:
                    route(c + 1)
                if back:
                    normalized(c * 2 + (GELU_NORMS + (2 if front else 1)), hN_chunk(c - 1), hN_ready)

            route(0)
            gelu_step(0, 0, False, True)
            with dve.Fori(0, CHUNKS // 2 - 1) as i:
                order.enter(i, N_GELU)
                gelu_step(i * 2 + 1, 1, True, True)
                gelu_step(i * 2 + 2, 0, True, True)
            order.leave(CHUNKS // 2 - 1)
            gelu_step(CHUNKS - 1, 1, True, False)
            combine(CHUNKS - 1)
            normalized(2 * CHUNKS + GELU_NORMS, hN_chunk(CHUNKS - 1), hN_ready)


def _layout(inputs):
    import numpy as np
    f = {k: np.asarray(v) for k, v in inputs.items()}
    a = {}
    a["x"] = f["x"].reshape(TOKENS, V, C0).transpose(1, 0, 2).reshape(V, TOKENS * C0)
    a["ident"] = np.eye(P, dtype=np.float32)
    cols = np.zeros((P, 16), np.float32)
    for layer in range(2):
        for n, name in enumerate(("b", "g", "be", "m", "v")):
            cols[:, 5 * layer + n] = f[f"L0_tok_{name}{layer}"]
    cols[BIAS_ROW, 10] = cols[ROWS + BIAS_ROW, 10] = 1.0
    a["cols"] = cols
    cols64 = np.zeros((P, 8), np.float32)
    for n, name in enumerate(("b", "g", "be", "m", "v")):
        cols64[0:D, n] = f[f"L0_tok_{name}2"]
    cols64[0:D, 5], cols64[0:D, 6] = f["L0_attn_bq"], f["L0_attn_bk"]
    a["cols64"] = cols64
    a["A"] = f["L0_tok_A"]
    a["AT"] = np.zeros((P, V), np.float32)
    a["AT"][0:V] = f["L0_tok_A"].T
    w0 = np.zeros((P // ROWS, ROWS, GROUP, CH), np.float32)
    for j in range(GROUP):
        w0[:, C0 * j:C0 * (j + 1), j] = f["L0_tok_W0"]
    a["w0_blocks"] = w0.reshape(P, GROUP * CH)
    a["W1"], a["W2"] = f["L0_tok_W1"], f["L0_tok_W2"]
    rowv = np.concatenate([f["L0_attn_bv"], f["L0_ffn_out_b"], f["L0_ffn_ln_g"], f["L0_ffn_ln_b"],
                           f["L1_attn_q_norm_w"], f["L1_attn_k_norm_w"], f["L1_ffn_gamma"],
                           f["L1_ffn_beta"], f["L1_ffn_b2"].reshape(-1), f["L1_ffn_br"]])
    a["rows"] = rowv.reshape(ROW_WIDTH)
    a["att_w"] = np.concatenate([f["L0_attn_Wq"], f["L0_attn_Wk"], f["L0_attn_Wv"]], 1)
    a["gate_wT"] = f["L0_ffn_gate_w"].T
    a["lat_w"] = f["L0_ffn_lattice_weights"].reshape(EXPERTS0 // 2, 2 * D, D).transpose(1, 0, 2)
    a["out_wT"] = f["L0_ffn_out_w"].T
    a["ident2"] = np.concatenate([np.eye(D, dtype=np.float32)] * 2, 0)
    swap = np.arange(D).reshape(D // 2, 2)[:, ::-1].reshape(-1)
    wqT = f["L1_attn_wq"].T.reshape(D, HEADS, D)
    q_w = np.stack([wqT.reshape(D, -1), wqT[:, :, swap].reshape(D, -1)], 1)
    a["q_w"] = np.concatenate([q_w, q_w], 0)
    wkT, wvT = f["L1_attn_wkv"][0:D].T, f["L1_attn_wkv"][D:].T
    kv = np.concatenate([wkT, wkT[:, swap], wvT, wvT], 1)
    a["kv_w"] = np.concatenate([kv, kv], 0)
    a["wo_w"] = f["L1_attn_wo"].reshape(D, PAIRS, 2, D).transpose(2, 3, 1, 0).reshape(P, PAIRS, D)
    freqs = np.float32(10000.0) ** (np.float32(-2.0) * np.arange(D // 2, dtype=np.float32) / np.float32(D))
    theta = np.arange(SEQ, dtype=np.float32)[:, None] * freqs[None, :].astype(np.float32)
    cos = np.repeat(np.cos(theta), 2, axis=1).astype(np.float32)
    sin = np.repeat(np.sin(theta), 2, axis=1).astype(np.float32)
    sin[:, 0::2] *= -1
    a["trig_f"] = np.concatenate([np.stack([cos.T, sin.T], 1)] * 2, 0)
    a["trig_t"] = np.concatenate([np.stack([cos, sin], 1)] * 2, 0)
    head_of = np.zeros((P, 2), np.float32)
    head_of[0:D, 0] = head_of[D:P, 1] = 1.0
    a["head_of"] = head_of
    above = np.where(np.arange(SEQ)[None, :] > np.arange(SEQ)[:, None], MASKED, 0.0).astype(np.float32)
    a["mask"] = np.tile(above, (2, CT // SEQ))
    twice = lambda m: np.concatenate([m, m], 0)
    a["r_w"] = twice(f["L1_ffn_Wr"])
    a["e1_w"] = twice(f["L1_ffn_W1"].transpose(1, 0, 2).reshape(D, EXPERTS1 * HID1))
    a["e1_b"] = f["L1_ffn_b1"].T
    a["e2_w"] = f["L1_ffn_W2"].transpose(1, 0, 2)
    return {k: np.ascontiguousarray(v) for k, v in a.items()}

def kernel(**inputs):
    import numpy as _np
    import concourse.bacc as _bacc
    from concourse import mybir as _mybir
    from concourse.bass_utils import run_bass_kernel_spmd as _run

    nc = _bacc.Bacc("TRN2", target_bir_lowering=False, num_devices=1)
    arrays, args = {}, {}
    for name, a in _layout(inputs).items():
        arrays[f"in_{name}_dram"] = a
        args[name] = nc.dram_tensor(f"in_{name}_dram", a.shape, _mybir.dt.from_np(a.dtype),
                                    kind="ExternalInput").ap()
    args["out"] = nc.dram_tensor("out_0_dram", (P, BLOCKS, D), _mybir.dt.float32,
                                 kind="ExternalOutput").ap()
    build(nc, args)
    r = _run(nc, [arrays], core_ids=[0])
    got = _np.asarray(r.results[0]["out_0_dram"])
    return got.transpose(1, 0, 2).reshape(BATCHES, SEQ, D)
```
